# Optimizing a Trainium2 kernel written in Bass

```python
import numpy as np
import jax
import jax.numpy as jnp

def _softmax(x, axis=-1):
    return jax.nn.softmax(x, axis=axis)

def _gelu(x):
    return jax.nn.gelu(x, approximate=True)

def _silu(x):
    return jax.nn.silu(x)

def _sigmoid(x):
    return jax.nn.sigmoid(x)

def _layernorm(x, axis=-1, eps=1e-05):
    m = jnp.mean(x, axis=axis, keepdims=True)
    v = jnp.var(x, axis=axis, keepdims=True)
    return (x - m) / jnp.sqrt(v + eps)

def _scatter_add(tgt, idx, src, axis=0):
    return tgt.at[idx].add(src)

def _segment_sum(src, seg, n):
    return jax.ops.segment_sum(src, seg, n)
kernel_name = 'mk_gnn_ffn_d2_gnn_r8_3f4a28'

def setup_inputs(seed: int=0):
    np.random.seed(seed)
    _w = jnp.asarray

    def _rec_inputs():
        import jax
        import jax.numpy as jnp
        _gk = jax.random.key(seed)
        x = -0.0003713 + 1 * jax.random.normal(jax.random.fold_in(_gk, 1), (6250, 256), jnp.float32)
        _s = jax.random.randint(jax.random.fold_in(_gk, 2), (50000,), 0, 6250, jnp.int32)
        _d = jax.random.randint(jax.random.fold_in(_gk, 3), (50000,), 0, 6250, jnp.int32)
        _loop = jnp.arange(6250, dtype=jnp.int32)
        src = jnp.concatenate([_s, _d, _loop])
        dst = jnp.concatenate([_d, _s, _loop])
        _o = jnp.argsort(dst, stable=True)
        src = src[_o]
        dst = dst[_o]
        edge_weight = jax.random.uniform(jax.random.fold_in(_gk, 13), (106250,), jnp.float32, 0.0, 1)
        return (x, src, dst, edge_weight)
    x, src, dst, edge_weight = _rec_inputs()

    def _L0_gnn_setup():
        import jax, jax.numpy as jnp
        import numpy as np
        N, M, E = (6250, 1250, 62500)
        IN_CH, OUT_CH, HEADS = (256, 32, 8)
        NEG_SLOPE = 0.2
        EPS = 1e-16
        key = jax.random.key(seed)
        k1, k2, k3, k4, k5, k6 = jax.random.split(key, 6)
        x = jax.random.normal(k1, (N, IN_CH), dtype=jnp.float32)
        node_idx = jax.random.randint(k2, (E,), 0, N, dtype=jnp.int32)
        edge_idx = jax.random.randint(k3, (E,), 0, M, dtype=jnp.int32)
        hyperedge_index = jnp.stack([node_idx, edge_idx], axis=0)
        hyperedge_attr = jax.random.normal(k4, (M, IN_CH), dtype=jnp.float32)
        W = jax.random.normal(k5, (IN_CH, HEADS * OUT_CH), dtype=jnp.float32) / np.sqrt(IN_CH)
        att = jax.random.normal(k6, (1, HEADS, 2 * OUT_CH), dtype=jnp.float32) / np.sqrt(2 * OUT_CH)
        return {'x': x, 'hyperedge_index': hyperedge_index, 'hyperedge_attr': hyperedge_attr, 'W': W, 'att': att}
    _L0_gnn_all = _L0_gnn_setup()
    _L0_gnn_in = {k: v for k, v in _L0_gnn_all.items() if k in ('hyperedge_attr', 'W', 'att')}
    del _L0_gnn_all

    def _L0_ffn_setup():
        import jax, jax.numpy as jnp
        import numpy as np
        BN_EPS = 0.001

        def _bn(h, g, b, m, v):
            return g * (h - m) * jax.lax.rsqrt(v + BN_EPS) + b
        key = jax.random.key(seed)
        ks = jax.random.split(key, 8)
        B, F, Df = (256, 64, 256)
        E, H, D = (8, 256, 256)
        s1 = 1.0 / np.sqrt(Df)
        s2 = 1.0 / np.sqrt(H)
        return {'x': jax.random.normal(ks[0], (B, F, Df), jnp.float32), 'Wr': jax.random.normal(ks[1], (Df, E), jnp.float32) * s1, 'br': jnp.zeros((E,), jnp.float32), 'W1': jax.random.normal(ks[2], (E, Df, H), jnp.float32) * s1, 'b1': jnp.zeros((E, H), jnp.float32), 'g1': jnp.ones((E, H), jnp.float32), 'be1': jnp.zeros((E, H), jnp.float32), 'm1': jnp.zeros((E, H), jnp.float32), 'v1': jnp.ones((E, H), jnp.float32), 'W2': jax.random.normal(ks[3], (E, H, H), jnp.float32) * s2, 'b2': jnp.zeros((E, H), jnp.float32), 'g2': jnp.ones((E, H), jnp.float32), 'be2': jnp.zeros((E, H), jnp.float32), 'm2': jnp.zeros((E, H), jnp.float32), 'v2': jnp.ones((E, H), jnp.float32), 'Wo': jax.random.normal(ks[4], (E, H, D), jnp.float32) * s2, 'bo': jnp.zeros((E, D), jnp.float32)}
    _L0_ffn_all = _L0_ffn_setup()
    _L0_ffn_in = {k: v for k, v in _L0_ffn_all.items() if k in ('Wr', 'br', 'W1', 'b1', 'g1', 'be1', 'm1', 'v1', 'W2', 'b2', 'g2', 'be2', 'm2', 'v2', 'Wo', 'bo')}
    del _L0_ffn_all

    def _L1_gnn_setup():
        import jax, jax.numpy as jnp
        import numpy as np
        N, E, F_IN, F_OUT = (12500, 200000, 256, 256)
        key = jax.random.key(seed)
        k1, k2, k3, k4, k5, k6 = jax.random.split(key, 6)
        x = jax.random.normal(k1, (N, F_IN), dtype=jnp.float32)
        row = jax.random.randint(k2, (E,), 0, N, dtype=jnp.int32)
        col = jax.random.randint(k3, (E,), 0, N, dtype=jnp.int32)
        edge_weight = jax.random.uniform(k4, (E,), dtype=jnp.float32)
        weight = jax.random.normal(k5, (F_IN, F_OUT), dtype=jnp.float32)
        bias = jax.random.normal(k6, (F_OUT,), dtype=jnp.float32)
        return {'x': x, 'row': row, 'col': col, 'edge_weight': edge_weight, 'weight': weight, 'bias': bias}
    _L1_gnn_all = _L1_gnn_setup()
    _L1_gnn_in = {k: v for k, v in _L1_gnn_all.items() if k in ('weight', 'bias')}
    del _L1_gnn_all

    def _L1_ffn_setup():
        import jax, jax.numpy as jnp
        import numpy as np
        B, N, D = (16, 512, 256)
        NUM_EXPERTS, TOP_K, HEADS = (4, 2, 4)
        N_EDGES = 131072
        LN_EPS = 1e-05

        def _layernorm(x, g, b):
            mu = x.mean(-1, keepdims=True)
            var = ((x - mu) ** 2).mean(-1, keepdims=True)
            return (x - mu) * jax.lax.rsqrt(var + LN_EPS) * g + b

        def _forward(x, edge_index, W_gat, att_src, att_dst, b_gat, ln_gamma, ln_beta, W1, b1, W2, b2):
            Bc, Nc, Dc = x.shape
            M = Bc * Nc
            x_flat = x.reshape(M, Dc)
            h = (x_flat @ W_gat).reshape(M, HEADS, NUM_EXPERTS)
            loops = jnp.arange(M, dtype=edge_index.dtype)
            src = jnp.concatenate([edge_index[0], loops])
            dst = jnp.concatenate([edge_index[1], loops])
            a_src = (h * att_src).sum(-1)
            a_dst = (h * att_dst).sum(-1)
            e = jax.nn.leaky_relu(a_src[src] + a_dst[dst], negative_slope=0.2)
            e_max = jax.ops.segment_max(e, dst, num_segments=M)
            ee = jnp.exp(e - e_max[dst])
            denom = jax.ops.segment_sum(ee, dst, num_segments=M)
            alpha = ee / (denom[dst] + 1e-16)
            msg = h[src] * alpha[:, :, None]
            agg = jax.ops.segment_sum(msg, dst, num_segments=M).reshape(M, HEADS * NUM_EXPERTS) + b_gat
            scores = _layernorm(agg, ln_gamma, ln_beta).reshape(M, HEADS, NUM_EXPERTS).mean(1)
            scores = scores.reshape(Bc, Nc, NUM_EXPERTS)
            topk_s, topk_i = jax.lax.top_k(scores, TOP_K)
            w = jax.nn.softmax(topk_s, axis=-1)
            out = jnp.zeros_like(x)
            for ei in range(NUM_EXPERTS):
                g = jnp.where(topk_i == ei, w, 0.0).sum(-1)
                hh = jax.nn.gelu(x @ W1[ei] + b1[ei], approximate=False)
                out = out + g[..., None] * (hh @ W2[ei] + b2[ei])
            return out
        key = jax.random.key(seed)
        ks = jax.random.split(key, 8)
        s = 0.05
        return {'x': jax.random.normal(ks[0], (B, N, D), jnp.float32), 'W_gat': jax.random.normal(ks[1], (D, HEADS * NUM_EXPERTS), jnp.float32) * s, 'att_src': jax.random.normal(ks[2], (HEADS, NUM_EXPERTS), jnp.float32) * s, 'att_dst': jax.random.normal(ks[3], (HEADS, NUM_EXPERTS), jnp.float32) * s, 'b_gat': jnp.zeros((HEADS * NUM_EXPERTS,), jnp.float32), 'ln_gamma': jnp.ones((HEADS * NUM_EXPERTS,), jnp.float32), 'ln_beta': jnp.zeros((HEADS * NUM_EXPERTS,), jnp.float32), 'W1': jax.random.normal(ks[4], (NUM_EXPERTS, D, 2 * D), jnp.float32) * s, 'b1': jnp.zeros((NUM_EXPERTS, 2 * D), jnp.float32), 'W2': jax.random.normal(ks[5], (NUM_EXPERTS, 2 * D, D), jnp.float32) * s, 'b2': jnp.zeros((NUM_EXPERTS, D), jnp.float32), 'edge_index': jax.random.randint(ks[6], (2, N_EDGES), 0, B * N, jnp.int32)}
    _L1_ffn_all = _L1_ffn_setup()
    _L1_ffn_in = {k: v for k, v in _L1_ffn_all.items() if k in ('W_gat', 'att_src', 'att_dst', 'b_gat', 'ln_gamma', 'ln_beta', 'W1', 'b1', 'W2', 'b2', 'edge_index')}
    del _L1_ffn_all
    return {'x': x, 'src': src, 'dst': dst, 'edge_weight': edge_weight, 'L0_gnn_hyperedge_attr': _L0_gnn_in['hyperedge_attr'], 'L0_gnn_W': _L0_gnn_in['W'], 'L0_gnn_att': _L0_gnn_in['att'], 'L0_ffn_Wr': _L0_ffn_in['Wr'], 'L0_ffn_br': _L0_ffn_in['br'], 'L0_ffn_W1': _L0_ffn_in['W1'], 'L0_ffn_b1': _L0_ffn_in['b1'], 'L0_ffn_g1': _L0_ffn_in['g1'], 'L0_ffn_be1': _L0_ffn_in['be1'], 'L0_ffn_m1': _L0_ffn_in['m1'], 'L0_ffn_v1': _L0_ffn_in['v1'], 'L0_ffn_W2': _L0_ffn_in['W2'], 'L0_ffn_b2': _L0_ffn_in['b2'], 'L0_ffn_g2': _L0_ffn_in['g2'], 'L0_ffn_be2': _L0_ffn_in['be2'], 'L0_ffn_m2': _L0_ffn_in['m2'], 'L0_ffn_v2': _L0_ffn_in['v2'], 'L0_ffn_Wo': _L0_ffn_in['Wo'], 'L0_ffn_bo': _L0_ffn_in['bo'], 'L1_gnn_weight': _L1_gnn_in['weight'], 'L1_gnn_bias': _L1_gnn_in['bias'], 'L1_ffn_W_gat': _L1_ffn_in['W_gat'], 'L1_ffn_att_src': _L1_ffn_in['att_src'], 'L1_ffn_att_dst': _L1_ffn_in['att_dst'], 'L1_ffn_b_gat': _L1_ffn_in['b_gat'], 'L1_ffn_ln_gamma': _L1_ffn_in['ln_gamma'], 'L1_ffn_ln_beta': _L1_ffn_in['ln_beta'], 'L1_ffn_W1': _L1_ffn_in['W1'], 'L1_ffn_b1': _L1_ffn_in['b1'], 'L1_ffn_W2': _L1_ffn_in['W2'], 'L1_ffn_b2': _L1_ffn_in['b2'], 'L1_ffn_edge_index': _L1_ffn_in['edge_index']}

def reference(x, src, dst, edge_weight, L0_gnn_hyperedge_attr, L0_gnn_W, L0_gnn_att, L0_ffn_Wr, L0_ffn_br, L0_ffn_W1, L0_ffn_b1, L0_ffn_g1, L0_ffn_be1, L0_ffn_m1, L0_ffn_v1, L0_ffn_W2, L0_ffn_b2, L0_ffn_g2, L0_ffn_be2, L0_ffn_m2, L0_ffn_v2, L0_ffn_Wo, L0_ffn_bo, L1_gnn_weight, L1_gnn_bias, L1_ffn_W_gat, L1_ffn_att_src, L1_ffn_att_dst, L1_ffn_b_gat, L1_ffn_ln_gamma, L1_ffn_ln_beta, L1_ffn_W1, L1_ffn_b1, L1_ffn_W2, L1_ffn_b2, L1_ffn_edge_index):
    import jax
    import jax.numpy as jnp

    def _L0_gnn_ref(x, hyperedge_index, hyperedge_attr, W, att):
        import jax, jax.numpy as jnp
        import numpy as np
        N, M, E = (6250, 1250, 62500)
        IN_CH, OUT_CH, HEADS = (256, 32, 8)
        NEG_SLOPE = 0.2
        EPS = 1e-16
        node = hyperedge_index[0]
        edge = hyperedge_index[1]
        num_nodes = x.shape[0]
        num_edges = hyperedge_attr.shape[0]
        xh = (x @ W).reshape(num_nodes, HEADS, OUT_CH)
        eh = (hyperedge_attr @ W).reshape(num_edges, HEADS, OUT_CH)
        x_i = xh[node]
        x_j = eh[edge]
        alpha = jnp.sum(jnp.concatenate([x_i, x_j], axis=-1) * att, axis=-1)
        alpha = jax.nn.leaky_relu(alpha, NEG_SLOPE)
        amax = jax.ops.segment_max(alpha, node, num_segments=num_nodes)
        alpha = jnp.exp(alpha - amax[node])
        asum = jax.ops.segment_sum(alpha, node, num_segments=num_nodes)
        alpha = alpha / (asum[node] + EPS)
        ones = jnp.ones((node.shape[0],), dtype=x.dtype)
        D = jax.ops.segment_sum(ones, node, num_segments=num_nodes)
        Dinv = jnp.where(D > 0, 1.0 / D, 0.0)
        B = jax.ops.segment_sum(ones, edge, num_segments=num_edges)
        Binv = jnp.where(B > 0, 1.0 / B, 0.0)
        msg1 = Binv[edge][:, None, None] * alpha[:, :, None] * x_i
        out_e = jax.ops.segment_sum(msg1, edge, num_segments=num_edges)
        msg2 = Dinv[node][:, None, None] * alpha[:, :, None] * out_e[edge]
        out_n = jax.ops.segment_sum(msg2, node, num_segments=num_nodes)
        return out_n.reshape(num_nodes, HEADS * OUT_CH)

    def _L0_ffn_ref(x, Wr, br, W1, b1, g1, be1, m1, v1, W2, b2, g2, be2, m2, v2, Wo, bo):
        import jax, jax.numpy as jnp
        import numpy as np
        BN_EPS = 0.001

        def _bn(h, g, b, m, v):
            return g * (h - m) * jax.lax.rsqrt(v + BN_EPS) + b
        feat = jnp.mean(x, axis=0)
        w = jax.nn.softmax(feat @ Wr + br, axis=-1)
        h = jnp.einsum('bfd,edh->bfeh', x, W1) + b1
        h = jax.nn.relu(_bn(h, g1, be1, m1, v1))
        h = jnp.einsum('bfeh,ehk->bfek', h, W2) + b2
        h = jax.nn.relu(_bn(h, g2, be2, m2, v2))
        y = jnp.einsum('bfeh,ehd->bfed', h, Wo) + bo
        return jnp.einsum('bfed,fe->bfd', y, w)

    def _L1_gnn_ref(x, row, col, edge_weight, weight, bias):
        import jax, jax.numpy as jnp
        import numpy as np
        N, E, F_IN, F_OUT = (12500, 200000, 256, 256)
        h = x @ weight
        msgs = edge_weight[:, None] * h[col]
        out = jax.ops.segment_sum(msgs, row, num_segments=x.shape[0])
        return out + bias

    def _L1_ffn_ref(x, W_gat, att_src, att_dst, b_gat, ln_gamma, ln_beta, W1, b1, W2, b2, edge_index):
        import jax, jax.numpy as jnp
        import numpy as np
        B, N, D = (16, 512, 256)
        NUM_EXPERTS, TOP_K, HEADS = (4, 2, 4)
        N_EDGES = 131072
        LN_EPS = 1e-05

        def _layernorm(x, g, b):
            mu = x.mean(-1, keepdims=True)
            var = ((x - mu) ** 2).mean(-1, keepdims=True)
            return (x - mu) * jax.lax.rsqrt(var + LN_EPS) * g + b

        def _forward(x, edge_index, W_gat, att_src, att_dst, b_gat, ln_gamma, ln_beta, W1, b1, W2, b2):
            Bc, Nc, Dc = x.shape
            M = Bc * Nc
            x_flat = x.reshape(M, Dc)
            h = (x_flat @ W_gat).reshape(M, HEADS, NUM_EXPERTS)
            loops = jnp.arange(M, dtype=edge_index.dtype)
            src = jnp.concatenate([edge_index[0], loops])
            dst = jnp.concatenate([edge_index[1], loops])
            a_src = (h * att_src).sum(-1)
            a_dst = (h * att_dst).sum(-1)
            e = jax.nn.leaky_relu(a_src[src] + a_dst[dst], negative_slope=0.2)
            e_max = jax.ops.segment_max(e, dst, num_segments=M)
            ee = jnp.exp(e - e_max[dst])
            denom = jax.ops.segment_sum(ee, dst, num_segments=M)
            alpha = ee / (denom[dst] + 1e-16)
            msg = h[src] * alpha[:, :, None]
            agg = jax.ops.segment_sum(msg, dst, num_segments=M).reshape(M, HEADS * NUM_EXPERTS) + b_gat
            scores = _layernorm(agg, ln_gamma, ln_beta).reshape(M, HEADS, NUM_EXPERTS).mean(1)
            scores = scores.reshape(Bc, Nc, NUM_EXPERTS)
            topk_s, topk_i = jax.lax.top_k(scores, TOP_K)
            w = jax.nn.softmax(topk_s, axis=-1)
            out = jnp.zeros_like(x)
            for ei in range(NUM_EXPERTS):
                g = jnp.where(topk_i == ei, w, 0.0).sum(-1)
                hh = jax.nn.gelu(x @ W1[ei] + b1[ei], approximate=False)
                out = out + g[..., None] * (hh @ W2[ei] + b2[ei])
            return out
        return _forward(x, edge_index, W_gat, att_src, att_dst, b_gat, ln_gamma, ln_beta, W1, b1, W2, b2)
    edge_index = jnp.stack([src, dst])
    x = x + _L0_gnn_ref(_layernorm(x, axis=-1), edge_index, L0_gnn_hyperedge_attr, L0_gnn_W, L0_gnn_att)
    x = x + _L0_ffn_ref(_layernorm(x, axis=-1)[None], L0_ffn_Wr, L0_ffn_br, L0_ffn_W1, L0_ffn_b1, L0_ffn_g1, L0_ffn_be1, L0_ffn_m1, L0_ffn_v1, L0_ffn_W2, L0_ffn_b2, L0_ffn_g2, L0_ffn_be2, L0_ffn_m2, L0_ffn_v2, L0_ffn_Wo, L0_ffn_bo)[0]
    x = x + _L1_gnn_ref(_layernorm(x, axis=-1), src, dst, edge_weight, L1_gnn_weight, L1_gnn_bias)
    x = x + _L1_ffn_ref(_layernorm(x, axis=-1)[None], L1_ffn_W_gat, L1_ffn_att_src, L1_ffn_att_dst, L1_ffn_b_gat, L1_ffn_ln_gamma, L1_ffn_ln_beta, L1_ffn_W1, L1_ffn_b1, L1_ffn_W2, L1_ffn_b2, L1_ffn_edge_index)[0]
    return x

_drawn_inputs = setup_inputs


def setup_inputs(seed=0):
    import zlib

    import numpy as np

    out = dict(_drawn_inputs(seed))
    spreads = {'L0_ffn_br': (0.0, 0.1),
     'L0_ffn_b1': (0.0, 0.1),
     'L0_ffn_g1': (1.0, 0.2),
     'L0_ffn_be1': (0.0, 0.1),
     'L0_ffn_m1': (0.0, 0.1),
     'L0_ffn_v1': (1.0, 0.2),
     'L0_ffn_b2': (0.0, 0.1),
     'L0_ffn_g2': (1.0, 0.2),
     'L0_ffn_be2': (0.0, 0.1),
     'L0_ffn_m2': (0.0, 0.1),
     'L0_ffn_v2': (1.0, 0.2),
     'L0_ffn_bo': (0.0, 0.1),
     'L1_ffn_b_gat': (0.0, 0.8),
     'L1_ffn_ln_gamma': (1.0, 0.6),
     'L1_ffn_ln_beta': (0.0, 0.8),
     'L1_ffn_b1': (0.0, 0.8),
     'L1_ffn_b2': (0.0, 2.0)}
    factors = {'L0_gnn_hyperedge_attr': 8.0,
     'L0_gnn_W': 8.0,
     'L0_gnn_att': 8.0,
     'L1_ffn_W_gat': 8.0,
     'L1_ffn_att_src': 8.0,
     'L1_ffn_att_dst': 8.0,
     'L1_ffn_W1': 6.412,
     'L1_ffn_W2': 5.98}
    for name, (base, spread) in spreads.items():
        noise = np.random.default_rng([zlib.crc32(name.encode()), seed]).standard_normal(out[name].shape)
        drawn = base * np.exp(spread * noise) if base else spread * noise
        out[name] = jnp.asarray(drawn.astype(out[name].dtype))
    for name, factor in factors.items():
        out[name] = (out[name] * factor).astype(out[name].dtype)
    return out
```

```python
from contextlib import ExitStack

import concourse.bass as bass
from concourse import mybir

F32 = mybir.dt.float32
I32 = mybir.dt.int32
ALU = mybir.AluOpType
ACT = mybir.ActivationFunctionType
AX = mybir.AxisListType
DVE = mybir.EngineType.DVE
PE = mybir.EngineType.PE

P = 128
N, F = 6250, 256
E = 106250
M = 1250
EG = 131072
NJ = -(-N // P)
MJ = -(-M // P)
H0, C0 = 8, 32
EX0, HID0 = 8, 256
H1, C1 = 4, 4
EX1, HID1 = 4, 512
LN_EPS = 1e-5
BN_EPS = 1e-3
HALF = 8
BODY = 2 * HALF
BT = 7
NB = NJ // BT
NOWHERE = float(2 ** 20)


def steps_for(edges, tiles):
    most = (edges + tiles * (P - 1)) // P
    return -(-most // BODY) * BODY


S_SRC = steps_for(E, NJ)
S_DST = steps_for(E, MJ)
S_GAT = steps_for(EG, NJ)


class Link:

    def __init__(self, eng, sem):
        self.eng, self.sem, self.base, self.n, self.start = eng, sem, 0, 0, None

    def __call__(self, ins):
        ins.then_inc(self.sem, 1)
        self.n += 1
        self.eng.wait_ge(self.sem, self.base + self.n)

    def loop(self, i, per):
        if self.start is None:
            self.start, self.per = self.base + self.n, per
        else:
            assert self.n == per
        self.base, self.n = self.start + i * per, 0

    def end(self, count):
        assert self.n == self.per, (self.n, self.per)
        self.base, self.n, self.start = self.start + count * self.per, 0, None


def turns(eng, count, body):
    body(0)
    with eng.Fori(1, count) as i:
        body(i)


def reached(eng, sem, value):
    if not (isinstance(value, int) and value == 0):
        eng.wait_ge(sem, value)


def hold(k, eng, sem, value):
    if not (isinstance(value, int) and value == 0):
        eng.wait_ge(sem, value)
        eng.sem_inc(k.held, 1)


def tile_rows(dram):
    return dram.rearrange("(j p) f -> p j f", p=P)


class Core:

    def __init__(self, nc, stack):
        self.nc, self.stack, self.scopes, self.names = nc, stack, [stack], {}
        self.live = []

    def name(self, name):
        self.names[name] = self.names.get(name, 0) + 1
        return name if self.names[name] == 1 else f"{name}_{self.names[name]}"

    def sb(self, name, shape, dt=F32):
        return self.scopes[-1].enter_context(self.nc.sbuf_tensor(self.name(name), shape, dt))

    def ps(self, name, shape):
        return self.scopes[-1].enter_context(self.nc.psum_tensor(self.name(name), shape, F32))

    def sem(self, name):
        self.live.append(self.nc.alloc_semaphore(name=name))
        return self.live[-1]

    def recycle(self):
        self.nc.clear_and_free_semaphores(self.live)
        self.nc.all_engine_barrier()
        self.live = []

    def sems(self, name, n):
        return [self.sem(f"{name}{k}") for k in range(n)]

    def dram(self, name, shape, dt=F32):
        return self.nc.dram_tensor(name, shape, dt).ap()

    def scope(self):
        return Scope(self)


class Scope:

    def __init__(self, core):
        self.core = core

    def __enter__(self):
        self.own = ExitStack()
        self.own.__enter__()
        self.core.scopes.append(self.own)
        return self

    def __exit__(self, *a):
        self.core.scopes.pop()
        return self.own.__exit__(*a)


def load_nodes(k, x):
    nc = k.nc
    loaded, made, linked = k.sem("x_loaded"), k.sem("consts_made"), k.sem("setup_link")
    iota_i = k.sb("iota_i", [P, P], I32)
    part_i = k.sb("part_i", [P, P], I32)
    part_f = k.sb("part_f", [P, P])
    full = (NJ - 1) * P
    with nc.Block() as block:

        @block.gpsimd
        def _(pool):
            pool.iota(iota_i[:, :], [[1, P]], base=0, channel_multiplier=0).then_inc(made, 1)
            pool.iota(part_i[:, :], [[0, P]], base=0, channel_multiplier=1).then_inc(made, 1)

        @block.sync
        def _(sp):
            sp.dma_start(k.X[:, 0:NJ - 1, :], tile_rows(x[0:full, :])).then_inc(loaded, 16)
            sp.wait_ge(linked, 1)
            sp.dma_start(k.X[0:N - full, NJ - 1, :], x[full:N, :]).then_inc(loaded, 16)
            sp.wait_ge(loaded, 32)

        @block.vector
        def _(dve):
            link = Link(dve, linked)
            link(dve.memset(k.X[:, NJ - 1, :], 0.0))
            dve.memset(k.ones[:, :], 1.0)
            dve.wait_ge(made, 2)
            link(dve.tensor_copy(k.iota[:, :], iota_i[:, :]))
            link(dve.tensor_copy(part_f[:, :], part_i[:, :]))
            link(dve.tensor_tensor(k.ident[:, :], k.iota[:, :], part_f[:, :], ALU.is_equal))
            link(dve.tensor_tensor(k.before[:, :], k.iota[:, :], part_f[:, :], ALU.is_gt))


def rank_edges(k, name, key, rows, cols, tiles, steps, slot, step_tile):
    nc = k.nc
    loaded, counted, offset, linked = (k.sem(f"{name}_{s}") for s in ("key_loaded", "counted", "offset", "link"))
    with k.scope():
        key_i = k.sb("key_i", [rows, cols], I32)
        tile_f = k.sb("tile_f", [rows, cols])
        hit = k.sb("hit", [rows, cols])
        run = k.sb("run", [rows, cols])
        place = k.sb("place", [rows, cols])
        count = k.sb("count", [rows, tiles])
        tot_f = k.sb("tot_f", [P, tiles])
        tot_i = k.sb("tot_i", [P, tiles], I32)
        first = k.sb("first", [P, tiles])
        base = k.sb("base", [rows, tiles])
        step_i = k.sb("step_i", [1, steps], I32)
        step_f = k.sb("step_f", [1, steps])
        tile_of = k.sb("tile_of", [1, steps])
        ps_before = k.ps("ps_before", [P, 512])
        ps_total = k.ps("ps_total", [P, 512])
        made = k.sem(f"{name}_steps_made")
        with nc.Block() as block:

            @block.sync
            def _(sp):
                sp.dma_start(key_i[:, :], key.rearrange("(p c) -> p c", p=rows)).then_inc(loaded, 16)

            @block.gpsimd
            def _(pool):
                pool.iota(step_i[:, :], [[1, steps]], base=0, channel_multiplier=0).then_inc(made, 1)

            @block.vector
            def _(dve):
                link = Link(dve, linked)
                dve.wait_ge(made, 1)
                link(dve.tensor_copy(step_f[:, :], step_i[:, :]))
                link(dve.memset(tile_of[:, :], -1.0))
                link(dve.memset(place[:, :], 0.0))
                dve.wait_ge(loaded, 16)
                link(dve.tensor_scalar(key_i[:, :], key_i[:, :], 7, None, ALU.arith_shift_right))
                link(dve.tensor_copy(tile_f[:, :], key_i[:, :]))
                with dve.Fori(0, tiles) as b:
                    link.loop(b, 1)
                    link(dve.tensor_scalar(hit[:, :], tile_f[:, :], k.iota[0:rows, bass.ds(b, 1)], None,
                                           ALU.is_equal, ALU.add, accum_out=count[:, bass.ds(b, 1)]))
                link.end(tiles)
                dve.sem_inc(counted, 1)
                dve.wait_ge(offset, 2)
                link(dve.tensor_scalar(tot_f[:, :], ps_total[:, 0:tiles], float(P - 1), None, ALU.add))
                link(dve.tensor_copy(tot_i[:, :], tot_f[:, :]))
                link(dve.tensor_scalar(tot_i[:, :], tot_i[:, :], 7, None, ALU.arith_shift_right))
                link(dve.tensor_copy(tot_f[:, :], tot_i[:, :]))
                link(dve.tensor_tensor_scan(first[:, :], tot_f[:, :], tot_f[:, :], 0.0, ALU.add, ALU.max))
                link(dve.tensor_tensor(first[:, :], first[:, :], tot_f[:, :], ALU.subtract))
                link(dve.scalar_tensor_tensor(base[:, :], first[0:rows, :], float(P), ps_before[0:rows, 0:tiles],
                                              ALU.mult, ALU.add))
                with dve.Fori(0, tiles) as b:
                    link.loop(b, 5)
                    this = k.iota[0:rows, bass.ds(b, 1)]
                    link(dve.tensor_scalar(hit[:, :], tile_f[:, :], this, None, ALU.is_equal))
                    link(dve.tensor_tensor_scan(run[:, :], hit[:, :], hit[:, :], base[:, bass.ds(b, 1)],
                                                ALU.add, ALU.max))
                    link(dve.tensor_tensor(hit[:, :], hit[:, :], run[:, :], ALU.mult))
                    link(dve.tensor_tensor(place[:, :], place[:, :], hit[:, :], ALU.add))
                    link(dve.scalar_tensor_tensor(tile_of[:, :], step_f[:, :], first[0:1, bass.ds(b, 1)],
                                                  tile_of[:, :], ALU.is_ge, ALU.add))
                link.end(tiles)
                link(dve.tensor_copy(step_tile[0:1, :], tile_of[:, :]))
                link(dve.tensor_scalar(hit[:, :], place[:, :], 1.0, NOWHERE, ALU.is_lt, ALU.mult))
                link(dve.scalar_tensor_tensor(place[:, :], place[:, :], -1.0, hit[:, :], ALU.add, ALU.add))
                link(dve.tensor_copy(key_i[:, :], place[:, :]))
                link(dve.tensor_scalar(slot[:, :], key_i[:, :], P - 1, None, ALU.bitwise_and))
                link(dve.tensor_scalar(key_i[:, :], key_i[:, :], 7, None, ALU.arith_shift_right))
                link(dve.tensor_copy(hit[:, :], slot[:, :]))
                link(dve.tensor_copy(run[:, :], key_i[:, :]))
                link(dve.scalar_tensor_tensor(place[:, :], hit[:, :], float(steps), run[:, :], ALU.mult, ALU.add))
                link(dve.tensor_copy(slot[:, :], place[:, :]))

            @block.tensor
            def _(pe):
                pe.wait_ge(counted, 1)
                pe.matmul(ps_before[0:rows, 0:tiles], k.before[0:rows, 0:rows], count[:, :],
                          start=True, stop=True).then_inc(offset, 1)
                pe.matmul(ps_total[:, 0:tiles], k.ones[0:rows, 0:P], count[:, :],
                          start=True, stop=True).then_inc(offset, 1)


def scatter_records(k, name, rows, cols, chunk, slot, fields, width, fill, out):
    nc = k.nc
    bodies = cols // (2 * chunk)
    assert bodies * 2 * chunk == cols
    slots = out.shape[0]
    copies = len(fields) + 1
    filled, blank, ready = (k.sem(f"{name}_{s}") for s in ("filled", "blank", "record_ready"))
    stored = k.sems(f"{name}_stored", 2)
    with k.scope():
        wide = slots // P * width
        empty = k.sb("empty", [P, wide])
        record = [k.sb(f"record{h}", [rows, chunk, width]) for h in (0, 1)]
        where = [k.sb(f"where{h}", [rows, chunk], I32) for h in (0, 1)]
        with nc.Block() as block:

            @block.sync
            def _(sp):
                sp.wait_ge(blank, 1)
                sp.dma_start(out.rearrange("(p s) w -> p (s w)", p=P), empty[:, :]).then_inc(filled, 16)

            @block.vector
            def _(dve):
                dve.memset(empty[:, :], fill).then_inc(blank, 1)

                def fill_both(i):
                    for h in (0, 1):
                        reached(dve, stored[h], i * (chunk * 16))
                        at = bass.ds(i * (2 * chunk) + h * chunk, chunk)
                        for lo, w, src in fields:
                            if src is None:
                                dve.memset(record[h][:, :, lo:lo + w], 1.0).then_inc(ready, 1)
                            else:
                                dve.tensor_copy(record[h][:, :, lo:lo + w], src[:, at, :]).then_inc(ready, 1)
                        dve.tensor_copy(where[h][:, :], slot[:, at]).then_inc(ready, 1)

                turns(dve, bodies, fill_both)

            @block.gpsimd
            def _(pool):
                pool.wait_ge(filled, 16)
                with pool.Fori(0, bodies) as i:
                    for h in (0, 1):
                        hold(k, pool, ready, i * (2 * copies) + (h + 1) * copies)
                        for u in range(chunk):
                            pool.indirect_dma_start(
                                out=out, out_offset=bass.IndirectOffsetOnAxis(ap=where[h][:, u:u + 1], axis=0),
                                in_=record[h][:, u, :], in_offset=None, bounds_check=slots - 1,
                                oob_is_err=False).then_inc(stored[h], 16)
                for h in (0, 1):
                    pool.wait_ge(stored[h], bodies * chunk * 16)


def gather_rows(k, pool, steps, table, index, index_now, copied, freed, rows, landed):
    def body(i):
        for h in (0, 1):
            hold(k, pool, freed[h], i)
            pool.tensor_copy(index_now[h][:, :], index[:, bass.ds(i * BODY + h * HALF, HALF)]).then_inc(copied, 1)
            hold(k, pool, copied, i * 2 + (h + 1))
            for u in range(HALF):
                pool.indirect_dma_start(
                    out=rows[h][:, u, :], out_offset=None, in_=table,
                    in_offset=bass.IndirectOffsetOnAxis(ap=index_now[h][:, u:u + 1], axis=0)).then_inc(landed[h], 16)

    turns(pool, steps // BODY, body)


def load_tiles(nc, step_tile, i, tiles, engine):
    return nc.values_load_multi_w_load_instructions(
        step_tile[0:1, bass.ds(i * BODY, BODY)], engines=[engine], min_val=0, max_val=tiles - 1)[1]


def segment_max(k, name, steps, heads, width, table, index, local, step_tile, low, value, top):
    nc = k.nc
    copied, linked, ready, product = (k.sem(f"{name}_{s}") for s in ("index", "link", "diag", "product"))
    landed, kept = k.sems(f"{name}_landed", 2), k.sems(f"{name}_kept", 2)
    banks = heads * P // 512
    with k.scope():
        index_now = [k.sb(f"index_now{h}", [P, HALF], I32) for h in (0, 1)]
        rows = [k.sb(f"rows{h}", [P, HALF, width]) for h in (0, 1)]
        lifted = k.sb("lifted", [P, HALF, heads])
        hot = [k.sb(f"hot{h}", [P, HALF, P]) for h in (0, 1)]
        diag = [k.sb(f"diag{h}", [P, heads, P]) for h in (0, 1)]
        most = k.sb("most", [P, heads])
        ps = [k.ps(f"ps_max{h}", [P, heads, P]) for h in (0, 1)]
        with nc.Block() as block:

            @block.gpsimd
            def _(pool):
                gather_rows(k, pool, steps, table, index, index_now, copied, kept, rows, landed)

            @block.scalar
            def _(act):
                with act.Fori(0, steps // BODY) as i:
                    for h in (0, 1):
                        act.wait_ge(landed[h], i * (HALF * 16) + HALF * 16)
                        act.copy(value[:, bass.ds(i * BODY + h * HALF, HALF), :], rows[h][:, :, :]).then_inc(kept[h], 1)

            @block.vector
            def _(dve):
                link = Link(dve, linked)
                with dve.Fori(0, steps // BODY) as i:
                    link.loop(i, 2 * (2 + 2 * HALF))
                    tiles = load_tiles(nc, step_tile, i, top.shape[1], DVE)

                    def build(h, u):
                        dve.tensor_tensor(
                            diag[u % 2][:, :, :], k.ident[:, :].unsqueeze(1).to_broadcast([P, heads, P]),
                            lifted[:, u, :].unsqueeze(2).to_broadcast([P, heads, P]), ALU.mult).then_inc(ready, 1)

                    def take(h, u):
                        dve.wait_ge(product, (i * BODY + (h * HALF + u + 1)) * banks)
                        link(dve.tensor_reduce(most[:, :], ps[u % 2][:, :, :], AX.X, ALU.max))
                        into = top[:, bass.ds(tiles[h * HALF + u], 1), :].rearrange("p a h -> p (a h)")
                        link(dve.tensor_tensor(into, into, most[:, :], ALU.max))

                    for h in (0, 1):
                        dve.wait_ge(kept[h], i + 1)
                        at = bass.ds(i * BODY + h * HALF, HALF)
                        link(dve.tensor_tensor(lifted[:, :, :], value[:, at, 0:heads],
                                               low[:, :].unsqueeze(1).to_broadcast([P, HALF, heads]), ALU.subtract))
                        link(dve.tensor_tensor(hot[h][:, :, :], k.iota[:, :].unsqueeze(1).to_broadcast([P, HALF, P]),
                                               local[:, at].unsqueeze(2).to_broadcast([P, HALF, P]), ALU.is_equal))
                        build(h, 0)
                        for u in range(HALF):
                            if u + 1 < HALF:
                                build(h, u + 1)
                            take(h, u)
                link.end(steps // BODY)

            @block.tensor
            def _(pe):
                with pe.Fori(0, steps // BODY) as i:
                    for h in (0, 1):
                        for u in range(HALF):
                            pe.wait_ge(ready, i * BODY + (h * HALF + u + 1))
                            for c in range(banks):
                                g = heads // banks
                                pe.matmul(ps[u % 2][:, c * g:(c + 1) * g, :], hot[h][:, u, :],
                                          diag[u % 2][:, c * g:(c + 1) * g, :], start=True, stop=True).then_inc(product, 1)


def segment_softmax(k, name, steps, heads, local, step_tile, node, value, wide, message, keep, total):
    nc = k.nc
    names = ("hot", "flipped", "turned", "spread", "shifted", "exped", "message", "summed", "link", "blank", "kept")
    hot_ok, flipped, turned, spread, shifted, exped, message_ok, summed, linked, blank, kept = (
        k.sem(f"{name}_{s}") for s in names)
    with k.scope():
        hot = [k.sb(f"hot{h}", [P, HALF, P]) for h in (0, 1)]
        hot_t = [k.sb(f"hot_t{h}", [P, HALF, P]) for h in (0, 1)]
        logit = [k.sb(f"logit{h}", [P, HALF, heads]) for h in (0, 1)]
        msg = [k.sb(f"msg{h}", [P, HALF, wide]) for h in (0, 1)]
        ps_t = [k.ps(f"ps_t{h}", [P, HALF, P]) for h in (0, 1)]
        ps_n = [k.ps(f"ps_n{h}", [P, 512]) for h in (0, 1)]
        ps_s = [k.ps(f"ps_s{h}", [P, 512]) for h in (0, 1)]
        at_node = [x[:, 0:HALF * 2 * heads].rearrange("p (u c) -> p u c", u=HALF) for x in ps_n]
        sums = [x[:, 0:HALF * wide].rearrange("p (u c) -> p u c", u=HALF) for x in ps_s]
        links = 2 * (3 + message(None, None, None, None) + HALF)
        with nc.Block() as block:

            @block.vector
            def _(dve):
                link = Link(dve, linked)
                for h in (0, 1):
                    dve.memset(msg[h][:, :, :], 1.0).then_inc(blank, 1)
                with dve.Fori(0, steps // BODY) as i:
                    link.loop(i, links)
                    tiles = load_tiles(nc, step_tile, i, total.shape[1], DVE)
                    for h in (0, 1):
                        at = bass.ds(i * BODY + h * HALF, HALF)
                        dve.tensor_tensor(hot[h][:, :, :], k.iota[:, :].unsqueeze(1).to_broadcast([P, HALF, P]),
                                          local[:, at].unsqueeze(2).to_broadcast([P, HALF, P]),
                                          ALU.is_equal).then_inc(hot_ok, 1)
                    for h in (0, 1):
                        at = bass.ds(i * BODY + h * HALF, HALF)
                        dve.wait_ge(spread, (i * 2 + (h + 1)) * HALF)
                        link(dve.tensor_tensor(logit[h][:, :, :], value[:, at, 0:heads],
                                               at_node[h][:, :, heads:2 * heads], ALU.add))
                        link(dve.scalar_tensor_tensor(logit[h][:, :, :], logit[h][:, :, :], 0.2, logit[h][:, :, :],
                                                      ALU.mult, ALU.max))
                        link(dve.tensor_tensor(logit[h][:, :, :], logit[h][:, :, :], at_node[h][:, :, 0:heads],
                                               ALU.subtract))
                        dve.tensor_scalar(logit[h][:, :, :], logit[h][:, :, :], 0.0, None, ALU.min).then_inc(shifted, 1)
                    for h in (0, 1):
                        at = bass.ds(i * BODY + h * HALF, HALF)
                        dve.wait_ge(exped, i * 2 + (h + 1))
                        message(dve, link, msg[h], at)
                        dve.sem_inc(message_ok, 1)
                    for h in (0, 1):
                        for u in range(HALF):
                            dve.wait_ge(summed, i * BODY + (h + 1) * HALF)
                            into = total[:, bass.ds(tiles[h * HALF + u], 1), :].rearrange("p a w -> p (a w)")
                            link(dve.tensor_tensor(into, into, sums[h][:, u, :], ALU.add))
                link.end(steps // BODY)

            @block.tensor
            def _(pe):
                with pe.Fori(0, steps // BODY) as i:
                    tiles = load_tiles(nc, step_tile, i, total.shape[1], PE)
                    for h in (0, 1):
                        pe.wait_ge(hot_ok, i * 2 + (h + 1))
                        for u in range(HALF):
                            pe.transpose(ps_t[h][:, u, :], hot[h][:, u, :], k.ident[:, :]).then_inc(flipped, 1)
                    for h in (0, 1):
                        pe.wait_ge(turned, i * 2 + (h + 1))
                        for u in range(HALF):
                            pe.matmul(at_node[h][:, u, :], hot_t[h][:, u, :],
                                      node[:, bass.ds(tiles[h * HALF + u], 1), :].rearrange("p a c -> p (a c)"),
                                      start=True, stop=True).then_inc(spread, 1)
                    for h in (0, 1):
                        pe.wait_ge(message_ok, i * 2 + (h + 1))
                        for u in range(HALF):
                            pe.matmul(sums[h][:, u, :], hot[h][:, u, :], msg[h][:, u, :],
                                      start=True, stop=True).then_inc(summed, 1)

            @block.scalar
            def _(act):
                act.wait_ge(blank, 2)
                with act.Fori(0, steps // BODY) as i:
                    for h in (0, 1):
                        act.wait_ge(flipped, (i * 2 + (h + 1)) * HALF)
                        act.copy(hot_t[h][:, :, :], ps_t[h][:, :, :]).then_inc(turned, 1)
                    for h in (0, 1):
                        act.wait_ge(shifted, i * 2 + (h + 1))
                        act.activation(msg[h][:, :, 0:heads], logit[h][:, :, :], ACT.Exp).then_inc(exped, 1)
                        if keep:
                            act.wait_ge(exped, i * 2 + (h + 1))
                            act.copy(value[:, bass.ds(i * BODY + h * HALF, HALF), 0:heads],
                                     msg[h][:, :, 0:heads]).then_inc(kept, 1)


def segment_sum(k, name, steps, table, index, local, step_tile, total, width=F, edge_weight=None, probs=None,
                count=None):
    nc = k.nc
    copied, linked, hot_ok, message_ok = (k.sem(f"{name}_{s}") for s in ("index", "link", "hot", "message"))
    landed, used = k.sems(f"{name}_landed", 2), k.sems(f"{name}_used", 2)
    summed = k.sem(f"{name}_summed")
    with k.scope():
        index_now = [k.sb(f"index_now{h}", [P, HALF], I32) for h in (0, 1)]
        rows = [k.sb(f"rows{h}", [P, HALF, F]) for h in (0, 1)]
        hot = [k.sb(f"hot{h}", [P, HALF, P]) for h in (0, 1)]
        msg = rows if probs is None else [k.sb(f"msg{h}", [P, HALF, width]) for h in (0, 1)]
        ps = [k.ps(f"ps_sum{b}", [P, 512]) for b in range(4)]
        with nc.Block() as block:

            @block.gpsimd
            def _(pool):
                gather_rows(k, pool, steps, table, index, index_now, copied, used, rows, landed)

            @block.vector
            def _(dve):
                link = Link(dve, linked)

                def body(i):
                    link.loop(i, 2 * ((1 if edge_weight is not None else 0) + HALF))
                    tiles = load_tiles(nc, step_tile, i, total.shape[1], DVE)
                    for h in (0, 1):
                        at = bass.ds(i * BODY + h * HALF, HALF)
                        same = dve.tensor_tensor(
                            hot[h][:, :, :], k.iota[:, :].unsqueeze(1).to_broadcast([P, HALF, P]),
                            local[:, at].unsqueeze(2).to_broadcast([P, HALF, P]), ALU.is_equal)
                        if edge_weight is None:
                            same.then_inc(hot_ok, 1)
                        else:
                            link(same)
                            dve.tensor_tensor(hot[h][:, :, :], hot[h][:, :, :],
                                              edge_weight[:, at].unsqueeze(2).to_broadcast([P, HALF, P]),
                                              ALU.mult).then_inc(hot_ok, 1)
                        if probs is not None:
                            dve.wait_ge(landed[h], i * (HALF * 16) + HALF * 16)
                            for u in range(HALF):
                                now = probs[:, bass.ds(i * BODY + (h * HALF + u), 1), :]
                                ins = dve.tensor_tensor(
                                    msg[h][:, u, 0:F].rearrange("p (a c) -> p a c", a=H0),
                                    rows[h][:, u, :].rearrange("p (a c) -> p a c", a=H0),
                                    now.rearrange("p a h -> p (a h)").unsqueeze(2).to_broadcast([P, H0, C0]), ALU.mult)
                                ins.then_inc(message_ok, 1)
                            if count is not None:
                                dve.tensor_copy(msg[h][:, :, F:F + 1], count[:, at].unsqueeze(2)).then_inc(message_ok, 1)
                    for h in (0, 1):
                        for u in range(HALF):
                            n = h * HALF + u
                            dve.wait_ge(summed, i * BODY + (n + 1))
                            into = total[:, bass.ds(tiles[n], 1), :].rearrange("p a w -> p (a w)")
                            reached(dve, linked, link.base + link.n)
                            dve.tensor_tensor(into, into, ps[n % 4][:, 0:width], ALU.add).then_inc(linked, 1)
                            link.n += 1

                turns(dve, steps // BODY, body)
                link.end(steps // BODY)

            @block.tensor
            def _(pe):
                first = 0 if edge_weight is None else 1
                per_body = 2 * (first + HALF)
                msgs = HALF + (1 if count is not None else 0)

                def body(i):
                    for h in (0, 1):
                        pe.wait_ge(hot_ok, i * 2 + (h + 1))
                        if probs is None:
                            pe.wait_ge(landed[h], i * (HALF * 16) + HALF * 16)
                        else:
                            pe.wait_ge(message_ok, (i * 2 + (h + 1)) * msgs)
                        for u in range(HALF):
                            n = h * HALF + u
                            if n >= 4:
                                pe.wait_ge(linked, i * per_body + 2 * first + (n - 4 + 1))
                            else:
                                reached(pe, linked, i * per_body)
                            pe.matmul(ps[n % 4][:, 0:width], hot[h][:, u, :], msg[h][:, u, 0:width],
                                      start=True, stop=True).then_inc(summed, 1)

                turns(pe, steps // BODY, body)

            @block.scalar
            def _(act):
                with act.Fori(0, steps // BODY) as i:
                    for h in (0, 1):
                        act.wait_ge(summed, (i * 2 + (h + 1)) * HALF)
                        act.sem_inc(used[h], 1)


def norm_scales(k, name, scale, shift):
    nc = k.nc
    stats_ok, rooted, linked = (k.sem(f"{name}_{s}") for s in ("variance", "root", "link"))
    with k.scope():
        stats = k.sb("stats", [P, NJ, 6])
        mean_var = k.sb("mean_var", [P, NJ, 2])
        with nc.Block() as block:

            @block.vector
            def _(dve):
                link = Link(dve, linked)
                for j in range(NJ):
                    ins = dve.bn_stats(stats[:, j, :], k.X[:, j, :])
                link(ins)
                for j in range(NJ):
                    ins = dve.bn_aggr(mean_var[:, j, :], stats[:, j, :])
                link(ins)
                dve.tensor_scalar(scale[:, :], mean_var[:, :, 1], LN_EPS, None, ALU.add).then_inc(stats_ok, 1)
                dve.wait_ge(rooted, 1)
                link(dve.reciprocal(scale[:, :], scale[:, :]))
                link(dve.scalar_tensor_tensor(shift[:, :], mean_var[:, :, 0], -1.0, scale[:, :], ALU.mult, ALU.mult))

            @block.scalar
            def _(act):
                act.wait_ge(stats_ok, 1)
                act.activation(scale[:, :], scale[:, :], ACT.Sqrt).then_inc(rooted, 1)


class Normed:

    def __init__(self, k, name, src, bt, scale, shift, ps):
        self.k, self.src, self.bt, self.scale, self.shift, self.ps = k, src, bt, scale, shift, ps
        self.flat = k.sb("flat", [P, bt, F])
        self.xt = k.sb("xt", [P, 2, bt * P])
        self.normed, self.flipped, self.copied = (k.sem(f"{name}_{s}") for s in ("normed", "flipped", "xt_copied"))

    def vector(self, dve, b):
        for u in range(self.bt):
            at = bass.ds(b * self.bt + u, 1)
            dve.tensor_scalar(self.flat[:, u, :], self.src[:, at, :].rearrange("p a f -> p (a f)"),
                              self.scale[:, at], self.shift[:, at], ALU.mult, ALU.add).then_inc(self.normed, 1)

    def tensor(self, pe, b):
        for u in range(self.bt):
            pe.wait_ge(self.normed, b * self.bt + (u + 1))
            for c in (0, 1):
                at = (u % 2) * F + c * P
                pe.transpose(self.ps[u // 2][:, at:at + P], self.flat[:, u, c * P:(c + 1) * P],
                             self.k.ident[:, :]).then_inc(self.flipped, 1)
        pe.wait_ge(self.copied, b * self.bt + self.bt)

    def scalar(self, act, b, free=None):
        for u in range(self.bt):
            act.wait_ge(self.flipped, b * (2 * self.bt) + 2 * min(u | 1, self.bt - 1) + 2)
            if u == 0 and free is not None:
                free()
            act.copy(self.xt[:, :, u * P:(u + 1) * P],
                     self.ps[u // 2][:, (u % 2) * F:(u % 2) * F + F].rearrange("p (c n) -> p c n", c=2)
                     ).then_inc(self.copied, 1)


def project(k, name, src, blocks, bt, scale, shift, weight, cols, table=None, keep=None, att=None, side=None):
    nc = k.nc
    loaded, product, out_ok, saved, linked = (
        k.sem(f"{name}_{s}") for s in ("w_loaded", "product", "out", "saved", "link"))
    with k.scope():
        w = k.sb("w", [P, 2, cols])
        rows = k.sb("rows", [P, bt, cols])
        scaled = k.sb("scaled", [P, F])
        ps_x = [k.ps(f"ps_x{u}", [P, 512]) for u in range(4)]
        ps_w = [k.ps(f"ps_w{u}", [P, 512]) for u in range(4)]
        norm = Normed(k, name, src, bt, scale, shift, ps_x)
        with nc.Block() as block:

            @block.sync
            def _(sp):
                sp.dma_start(w[:, :, :], weight.rearrange("(a p) c -> p a c", p=P)).then_inc(loaded, 16)
                if table is not None:
                    out = table.rearrange("(b j p) f -> b p j f", p=P, j=bt)
                    with sp.Fori(0, blocks) as b:
                        hold(k, sp, out_ok, b * bt + bt)
                        sp.dma_start(out[bass.ds(b, 1), :, :, :].rearrange("a p j f -> p (a j) f"),
                                     rows[:, :, :]).then_inc(saved, 16)
                    sp.wait_ge(saved, blocks * 16)

            @block.vector
            def _(dve):
                link = Link(dve, linked)

                def body(b):
                    reached(dve, norm.flipped, b * (2 * bt))
                    norm.vector(dve, b)
                    if att is not None:
                        link.loop(b, 2 * bt)
                        for u in range(bt):
                            dve.wait_ge(out_ok, b * bt + (u + 1))
                            link(dve.tensor_tensor(scaled[:, :], rows[:, u, :],
                                                   att[:, :, :].rearrange("p h c -> p (h c)"), ALU.mult))
                            link(dve.tensor_reduce(side[:, bass.ds(b * bt + u, 1), :].rearrange("p a h -> p (a h)"),
                                                   scaled[:, :].rearrange("p (h c) -> p h c", h=H0), AX.X, ALU.add))

                turns(dve, blocks, body)

            @block.tensor
            def _(pe):
                pe.wait_ge(loaded, 16)

                def body(b):
                    norm.tensor(pe, b)
                    reached(pe, out_ok, b * bt)
                    for u in range(bt):
                        for c in (0, 1):
                            at = (u % 2) * F
                            ins = pe.matmul(ps_w[u // 2][:, at:at + cols], norm.xt[:, c, u * P:(u + 1) * P],
                                            w[:, c, :], start=c == 0, stop=c == 1)
                        ins.then_inc(product, 1)

                turns(pe, blocks, body)

            @block.scalar
            def _(act):

                def body(b):
                    norm.scalar(act, b)
                    if table is not None:
                        reached(act, saved, b * 16)
                    if att is not None:
                        reached(act, linked, b * (2 * bt))
                    for u in range(bt):
                        act.wait_ge(product, b * bt + (min(u | 1, bt - 1) + 1))
                        into = rows[:, u, :] if keep is None else (
                            keep[:, bass.ds(b * bt + u, 1), :].rearrange("p a c -> p (a c)"))
                        act.copy(into, ps_w[u // 2][:, (u % 2) * F:(u % 2) * F + cols]).then_inc(out_ok, 1)

                turns(act, blocks, body)


def mixture(k, name, scale, shift, gate, experts, hidden, func, layers, w_out, b_out):
    nc = k.nc
    ct = hidden // P
    groups = 2 * ct * len(layers)
    wide = BT * P // 2
    names = ("w_loaded", "group", "evacuated", "y", "y_taken", "link")
    loaded, group_ok, evacuated, y_ok, y_taken, linked = (k.sem(f"{name}_{s}") for s in names)
    with k.scope():
        ws = [k.sb(f"w{n}", [P, experts, 2, hidden]) for n in range(len(layers))]
        wo = k.sb("wo", [P, experts, ct, F])
        bo = k.sb("bo", [P, experts, F])
        hid = [k.sb(f"hid{n}", [P, ct, BT * P]) for n in range(len(layers))]
        part = k.sb("part", [P, F])
        ps_h = [k.ps(f"ps_h{u}", [P, 512]) for u in range(4)]
        ps_y = [k.ps(f"ps_y{u}", [P, 512]) for u in range(4)]
        norm = Normed(k, name, k.X, BT, scale, shift, ps_h)
        with nc.Block() as block:

            @block.sync
            def _(sp):
                for w, (dram, _, _) in zip(ws, layers):
                    for e in range(experts):
                        sp.dma_start(w[:, e, :, :], dram[e, :, :].rearrange("(a p) h -> p a h", p=P)).then_inc(loaded, 16)
                for e in range(experts):
                    sp.dma_start(wo[:, e, :, :], w_out[e, :, :].rearrange("(a p) f -> p a f", p=P)).then_inc(loaded, 16)
                sp.dma_start(bo[:, :, :], b_out.partition_broadcast(P)).then_inc(loaded, 16)

            loads = (len(layers) * experts + experts + 1) * 16

            @block.tensor
            def _(pe):
                pe.wait_ge(loaded, loads)
                with pe.Fori(0, NB) as b:
                    pe.wait_ge(evacuated, b * (experts * groups) + 4)
                    norm.tensor(pe, b)
                    for e in range(experts):
                        for n, w in enumerate(ws):
                            src, kt = (norm.xt, 2) if n == 0 else (hid[n - 1], ct)
                            for half in (0, 1):
                                for c in range(ct):
                                    g = e * groups + n * 2 * ct + half * ct + c
                                    if n and c == 0:
                                        pe.wait_ge(evacuated, b * (experts * groups) + (g - 2 * ct + ct + 4))
                                    pe.wait_ge(evacuated, b * (experts * groups) + (g + 1))
                                    for a in range(kt):
                                        ins = pe.matmul(ps_h[g % 4][:, 0:wide], w[:, e, a, c * P:(c + 1) * P],
                                                        src[:, a, half * wide:(half + 1) * wide],
                                                        start=a == 0, stop=a == kt - 1)
                                    ins.then_inc(group_ok, 1)
                        pe.wait_ge(evacuated, b * (experts * groups) + ((e + 1) * groups + 4))
                        for u in range(BT):
                            m = e * BT + u
                            pe.wait_ge(y_taken, b * (experts * BT) + (m + 1))
                            for a in range(ct):
                                ins = pe.matmul(ps_y[m % 4][:, 0:F], hid[-1][:, a, u * P:(u + 1) * P],
                                                wo[:, e, a, :], start=a == 0, stop=a == ct - 1)
                            ins.then_inc(y_ok, 1)

            @block.scalar
            def _(act):
                act.sem_inc(evacuated, 4)
                with act.Fori(0, NB) as b:
                    norm.scalar(act, b)
                    for e in range(experts):
                        for n, (_, s, t) in enumerate(layers):
                            for half in (0, 1):
                                for c in range(ct):
                                    g = e * groups + n * 2 * ct + half * ct + c
                                    act.wait_ge(group_ok, b * (experts * groups) + (g + 1))
                                    act.activation(
                                        hid[n][:, c, half * wide:(half + 1) * wide], ps_h[g % 4][:, 0:wide], func,
                                        bias=t[:, e, c:c + 1],
                                        scale=1.0 if s is None else s[:, e, c:c + 1]).then_inc(evacuated, 1)

            @block.vector
            def _(dve):
                link = Link(dve, linked)
                dve.sem_inc(y_taken, 4)
                dve.wait_ge(loaded, loads)
                with dve.Fori(0, NB) as b:
                    norm.vector(dve, b)
                    link.loop(b, experts * BT)
                    for e in range(experts):
                        for u in range(BT):
                            m = e * BT + u
                            at = bass.ds(b * BT + u, 1)
                            x = k.X[:, at, :].rearrange("p a f -> p (a f)")
                            dve.wait_ge(y_ok, b * (experts * BT) + (m + 1))
                            dve.tensor_tensor(part[:, :], ps_y[m % 4][:, 0:F], bo[:, e, :], ALU.add).then_inc(y_taken, 1)
                            dve.wait_ge(y_taken, b * (experts * BT) + (m + 1 + 4))
                            link(dve.scalar_tensor_tensor(
                                x, part[:, :], gate[:, at, e:e + 1].rearrange("p a e -> p (a e)"), x,
                                ALU.mult, ALU.add))
                link.end(NB)


def vector_only(k, name, body):
    linked = k.sem(f"{name}_link")
    with k.nc.Block() as block:

        @block.vector
        def _(dve):
            body(dve, Link(dve, linked))


def load_all(k, name, pairs, store=False):
    done = k.sem(f"{name}_done")
    with k.nc.Block() as block:

        @block.sync
        def _(sp):
            for to, src in pairs:
                sp.dma_start(to, src).then_inc(done, 16)
            sp.wait_ge(done, 16 * len(pairs))


def least(k, name, src, low, heads):
    most, spread, linked = k.sem(f"{name}_most"), k.sem(f"{name}_spread"), k.sem(f"{name}_link")
    with k.scope():
        own = k.sb("own", [P, heads])
        each = k.sb("each", [P, heads])
        with k.nc.Block() as block:

            @block.vector
            def _(dve):
                link = Link(dve, linked)
                link(dve.tensor_reduce(own[:, :], src.rearrange("p j h -> p h j"), AX.X, ALU.min))
                dve.tensor_scalar(own[:, :], own[:, :], -1.0, None, ALU.mult).then_inc(most, 1)
                dve.wait_ge(spread, 1)
                link(dve.tensor_scalar(low[:, :], each[:, :], -1.0, None, ALU.mult))

            @block.gpsimd
            def _(pool):
                pool.wait_ge(most, 1)
                pool.partition_all_reduce(each[:, :], own[:, :], P, bass.bass_isa.ReduceOp.max).then_inc(spread, 1)


def flat2(ap):
    return ap.rearrange("p a b -> p (a b)")


def graph_network(nc, x, src, dst, edge_weight, attr, w_gnn, att, wr, br, w1, b1, g1, be1, m1, v1, w2, b2, g2, be2,
                  m2, v2, wo, bo, weight, bias, w_gat, att_src, att_dst, b_gat, ln_gamma, ln_beta, u1, c1, u2, c2,
                  edge_index, out, stop=None):
    stack = ExitStack()
    with stack:
        k = Core(nc, stack)
        k.held = stack.enter_context(nc.semaphore("held"))
        k.X = k.sb("X", [P, NJ, F])
        k.iota = k.sb("iota", [P, P])
        k.ident = k.sb("ident", [P, P])
        k.ones = k.sb("ones", [P, P])
        k.before = k.sb("before", [P, P])
        scale = k.sb("scale", [P, NJ])
        shift = k.sb("shift", [P, NJ])
        tile_src = k.sb("tile_src", [1, S_SRC], I32)
        tile_dst = k.sb("tile_dst", [1, S_DST], I32)
        tile_gat = k.sb("tile_gat", [1, S_GAT], I32)

        REC_SRC, REC_DST, REC_GAT = 5, H0 + 3, 2
        by_src = k.dram("by_src", (P * S_SRC, REC_SRC))
        by_dst = k.dram("by_dst", (P * S_DST, REC_DST))
        by_gat = k.dram("by_gat", (P * S_GAT, REC_GAT))
        hyper_a = k.dram("hyper_a", (MJ * P, H0))
        node_h = k.dram("node_h", (NJ * P, F))
        hyper_out = k.dram("hyper_out", (MJ * P, F))
        gat_table = k.dram("gat_table", (NJ * P, H1 * C1 + H1))

        load_nodes(k, x)

        EP, EC = 125, E // 125
        with k.scope():
            slot_src = k.sb("slot_src", [EP, EC], I32)
            slot_dst = k.sb("slot_dst", [EP, EC], I32)
            rank_edges(k, "rank_src", src, EP, EC, NJ, S_SRC, slot_src, tile_src)
            rank_edges(k, "rank_dst", dst, EP, EC, MJ, S_DST, slot_dst, tile_dst)
            low_bits = k.sb("low_bits", [EP, EC], I32)
            fields = k.sb("fields", [EP, EC, REC_SRC])
            weights = k.sb("weights", [EP, EC])
            src_i = k.sb("src_i", [EP, EC], I32)
            dst_i = k.sb("dst_i", [EP, EC], I32)
            load_all(k, "edge_loads", [(t[:, :], d.rearrange("(p c) -> p c", p=EP))
                                       for t, d in ((src_i, src), (dst_i, dst), (weights, edge_weight))])

            def edge_fields(dve, link):
                link(dve.tensor_scalar(low_bits[:, :], src_i[:, :], P - 1, None, ALU.bitwise_and))
                for n, t in enumerate((low_bits, src_i, dst_i, weights, slot_dst)):
                    link(dve.tensor_copy(fields[:, :, n], t[:, :]))

            vector_only(k, "edge_fields", edge_fields)
            scatter_records(k, "by_src", EP, EC, 17, slot_src, [(0, REC_SRC, fields)], REC_SRC, -1.0, by_src)

        k.recycle()

        GC = EG // P
        with k.scope():
            slot_gat = k.sb("slot_gat", [P, GC], I32)
            rank_edges(k, "rank_gat", edge_index[1, :], P, GC, NJ, S_GAT, slot_gat, tile_gat)
            g_src = k.sb("g_src", [P, GC], I32)
            g_dst = k.sb("g_dst", [P, GC], I32)
            g_fields = k.sb("g_fields", [P, GC, REC_GAT])
            load_all(k, "gat_loads", [(g_src[:, :], edge_index[0, :].rearrange("(p c) -> p c", p=P)),
                                      (g_dst[:, :], edge_index[1, :].rearrange("(p c) -> p c", p=P))])

            def gat_fields(dve, link):
                link(dve.tensor_scalar(g_dst[:, :], g_dst[:, :], P - 1, None, ALU.bitwise_and))
                link(dve.tensor_copy(g_fields[:, :, 0], g_dst[:, :]))
                link(dve.tensor_copy(g_fields[:, :, 1], g_src[:, :]))

            vector_only(k, "gat_fields", gat_fields)
            scatter_records(k, "by_gat", P, GC, 16, slot_gat, [(0, REC_GAT, g_fields)], REC_GAT, -1.0, by_gat)

        with k.scope():
            local = k.sb("local", [P, S_SRC])
            to_dst = k.sb("to_dst", [P, S_SRC], I32)
            ew = k.sb("ew", [P, S_SRC])
            degree_part = k.sb("degree_part", [P, NJ, H0])
            with k.scope():
                prob = k.sb("prob", [P, S_SRC, H0])
                to_hyper = k.sb("to_hyper", [P, S_SRC], I32)
                with k.scope():
                    src_f = k.sb("src_f", [P, S_SRC])
                    hyper_local = k.sb("hyper_local", [P, S_SRC])
                    hyper_slot = k.sb("hyper_slot", [P, S_SRC], I32)
                    with k.scope():
                        rec = k.sb("rec", [P, S_SRC, REC_SRC])
                        low_i = k.sb("low_i", [P, S_SRC], I32)
                        dst_f = k.sb("dst_f", [P, S_SRC])
                        load_all(k, "by_src_load", [(rec[:, :, :], by_src.rearrange("(p s) w -> p s w", p=P))])

                        def unpack(dve, link):
                            link(dve.tensor_copy(local[:, :], rec[:, :, 0]))
                            link(dve.tensor_scalar(src_f[:, :], rec[:, :, 1], 0.0, None, ALU.max))
                            link(dve.tensor_scalar(dst_f[:, :], rec[:, :, 2], 0.0, None, ALU.max))
                            link(dve.tensor_copy(to_dst[:, :], dst_f[:, :]))
                            link(dve.tensor_scalar(low_i[:, :], to_dst[:, :], P - 1, None, ALU.bitwise_and))
                            link(dve.tensor_copy(hyper_local[:, :], low_i[:, :]))
                            link(dve.tensor_scalar(dst_f[:, :], dst_f[:, :], float(M - 1), None, ALU.min))
                            link(dve.tensor_copy(to_hyper[:, :], dst_f[:, :]))
                            link(dve.tensor_copy(ew[:, :], rec[:, :, 3]))
                            link(dve.tensor_scalar(dst_f[:, :], rec[:, :, 4], 0.0, NOWHERE, ALU.is_lt, ALU.mult))
                            link(dve.scalar_tensor_tensor(dst_f[:, :], rec[:, :, 4], 0.0, dst_f[:, :], ALU.max, ALU.add))
                            link(dve.tensor_copy(hyper_slot[:, :], dst_f[:, :]))

                        vector_only(k, "unpack", unpack)

                    with k.scope():
                        node_a = k.sb("node_a", [P, NJ, H0])
                        top = k.sb("top", [P, NJ, H0])
                        low = k.sb("low", [P, H0])
                        node = k.sb("node", [P, NJ, 2 * H0])
                        total = k.sb("total", [P, NJ, H0 + 1])
                        inv = k.sb("inv", [P, NJ, H0])
                        norm_scales(k, "norm0", scale, shift)
                        with k.scope():
                            atts = k.sb("atts", [P, H0, 2 * C0])
                            half_att = [k.sb(f"att{n}", [P, H0, C0]) for n in (0, 1)]
                            hyper = k.sb("hyper", [P, MJ, F])
                            hyper_side = k.sb("hyper_side", [P, MJ, H0])
                            plain = k.sb("plain", [P, 2, MJ])
                            full = (MJ - 1) * P

                            def clear(dve, link):
                                link(dve.memset(hyper[:, :, :], 0.0))
                                link(dve.memset(plain[:, 0, :], 1.0))
                                link(dve.memset(plain[:, 1, :], 0.0))

                            vector_only(k, "hyper_clear", clear)
                            load_all(k, "hyper_loads", [
                                (atts[:, :, :], att[0, :, :].partition_broadcast(P)),
                                (hyper[:, 0:MJ - 1, :], tile_rows(attr[0:full, :])),
                                (hyper[0:M - full, MJ - 1, :], attr[full:M, :])])

                            def split_att(dve, link):
                                for n in (0, 1):
                                    link(dve.tensor_copy(half_att[n][:, :, :], atts[:, :, n * C0:(n + 1) * C0]))

                            vector_only(k, "split_att", split_att)
                            project(k, "node0", k.X, NB, BT, scale, shift, w_gnn, F, table=node_h, att=half_att[0],
                                    side=node_a)
                            hyper_h = k.dram("hyper_h", (MJ * P, F))
                            project(k, "hyper0", hyper, 2, MJ // 2, plain[:, 0, :], plain[:, 1, :], w_gnn, F,
                                    table=hyper_h, att=half_att[1], side=hyper_side)
                            least(k, "least0", hyper_side[:, :, :], low, H0)
                            load_all(k, "hyper_a", [(tile_rows(hyper_a), hyper_side[:, :, :])])

                        vector_only(k, "top0_clear", lambda dve, link: (
                            link(dve.memset(top[:, :, :], 0.0)), link(dve.memset(total[:, :, :], 0.0))))
                        segment_max(k, "max0", S_SRC, H0, H0, hyper_a, to_hyper, local, tile_src, low, prob, top)

                        def node_side0(dve, link):
                            link(dve.tensor_tensor(top[:, :, :], top[:, :, :],
                                                   low[:, :].unsqueeze(1).to_broadcast([P, NJ, H0]), ALU.add))
                            link(dve.tensor_tensor(top[:, :, :], top[:, :, :], node_a[:, :, :], ALU.add))
                            link(dve.scalar_tensor_tensor(node[:, :, 0:H0], top[:, :, :], 0.2, top[:, :, :],
                                                          ALU.mult, ALU.max))
                            link(dve.tensor_copy(node[:, :, H0:2 * H0], node_a[:, :, :]))

                        vector_only(k, "node_side0", node_side0)
                        segment_softmax(k, "soft0", S_SRC, H0, local, tile_src, node, prob, H0 + 1,
                                        lambda dve, link, msg, at: 0, True, total)

                        def inverses0(dve, link):
                            link(dve.tensor_scalar(inv[:, :, :], total[:, :, 0:H0], 1e-16, None, ALU.add))
                            link(dve.reciprocal(inv[:, :, :], inv[:, :, :]))
                            link(dve.tensor_scalar(total[:, :, H0], total[:, :, H0], 1.0, None, ALU.max))
                            link(dve.reciprocal(total[:, :, H0], total[:, :, H0]))
                            link(dve.tensor_tensor(degree_part[:, :, :], inv[:, :, :],
                                                   total[:, :, H0:H0 + 1].to_broadcast([P, NJ, H0]), ALU.mult))

                        vector_only(k, "inverses0", inverses0)
                        scale_rows(k, "scale_h", node_h, inv)

                    scatter_records(k, "by_dst", P, S_SRC, 20, hyper_slot,
                                    [(0, H0, prob), (H0, 1, src_f[:, :].unsqueeze(2)),
                                     (H0 + 1, 1, hyper_local[:, :].unsqueeze(2)), (H0 + 2, 1, None)],
                                    REC_DST, 0.0, by_dst)
                with k.scope():
                    rec_d = k.sb("rec_d", [P, S_DST, REC_DST])
                    from_src = k.sb("from_src", [P, S_DST], I32)
                    local_d = k.sb("local_d", [P, S_DST])
                    sums = k.sb("sums", [P, MJ, F + 1])
                    load_all(k, "by_dst_load", [(rec_d[:, :, :], by_dst.rearrange("(p s) w -> p s w", p=P))])

                    def unpack_d(dve, link):
                        link(dve.tensor_copy(from_src[:, :], rec_d[:, :, H0]))
                        link(dve.tensor_copy(local_d[:, :], rec_d[:, :, H0 + 1]))
                        link(dve.memset(sums[:, :, :], 0.0))

                    vector_only(k, "unpack_d", unpack_d)
                    segment_sum(k, "hyper_sum", S_DST, node_h, from_src, local_d, tile_dst, sums, width=F + 1,
                                probs=rec_d[:, :, 0:H0], count=rec_d[:, :, H0 + 2])

                    def mean_d(dve, link):
                        link(dve.tensor_scalar(sums[:, :, F], sums[:, :, F], 1.0, None, ALU.max))
                        link(dve.reciprocal(sums[:, :, F], sums[:, :, F]))
                        link(dve.tensor_tensor(sums[:, :, 0:F], sums[:, :, 0:F],
                                               sums[:, :, F:F + 1].to_broadcast([P, MJ, F]), ALU.mult))

                    vector_only(k, "mean_d", mean_d)
                    load_all(k, "hyper_out", [(tile_rows(hyper_out), sums[:, :, 0:F])])

                with k.scope():
                    acc = k.sb("acc", [P, NJ, F])
                    vector_only(k, "acc0_clear", lambda dve, link: link(dve.memset(acc[:, :, :], 0.0)))
                    segment_sum(k, "node_sum", S_SRC, hyper_out, to_hyper, local, tile_src, acc, probs=prob[:, :, :])

                    def add0(dve, link):
                        for j in range(NJ):
                            x_heads = acc[:, j, :].rearrange("p (h c) -> p h c", h=H0)
                            ins = dve.tensor_tensor(x_heads, x_heads,
                                                    degree_part[:, j, :].unsqueeze(2).to_broadcast([P, H0, C0]), ALU.mult)
                        link(ins)
                        link(dve.tensor_tensor(flat2(k.X[:, :, :]), flat2(k.X[:, :, :]), flat2(acc[:, :, :]), ALU.add))

                    vector_only(k, "add0", add0)

            if stop == "gnn0":
                return store_nodes(k, out)

            k.recycle()
            norm_scales(k, "norm1", scale, shift)
            with k.scope():
                gate = k.sb("gate", [P, NJ, EX0])
                project(k, "logits0", k.X, NB, BT, scale, shift, wr, EX0, keep=gate)
                softmax_gate(k, gate, br)
                bn = [batch_norm(k, f"bn{n}", *a) for n, a in enumerate(((b1, g1, be1, m1, v1), (b2, g2, be2, m2, v2)))]
                mixture(k, "ffn0", scale, shift, gate, EX0, HID0, ACT.Relu, [(w1, *bn[0]), (w2, *bn[1])], wo, bo)
            if stop == "ffn0":
                return store_nodes(k, out)

            norm_scales(k, "norm2", scale, shift)
            project(k, "node1", k.X, NB, BT, scale, shift, weight, F, table=node_h)
            with k.scope():
                acc = k.sb("acc1", [P, NJ, F])
                bias_b = k.sb("bias_b", [P, F])
                vector_only(k, "acc1_clear", lambda dve, link: link(dve.memset(acc[:, :, :], 0.0)))
                load_all(k, "bias_load", [(bias_b[:, :], bias.partition_broadcast(P))])
                segment_sum(k, "edge_sum", S_SRC, node_h, to_dst, local, tile_src, acc, edge_weight=ew)

                def add1(dve, link):
                    link(dve.tensor_tensor(flat2(k.X[:, :, :]), flat2(k.X[:, :, :]), flat2(acc[:, :, :]), ALU.add))
                    link(dve.tensor_tensor(k.X[:, :, :], k.X[:, :, :],
                                           bias_b[:, :].unsqueeze(1).to_broadcast([P, NJ, F]), ALU.add))

                vector_only(k, "add1", add1)
        if stop == "gnn1":
            return store_nodes(k, out)

        k.recycle()
        norm_scales(k, "norm3", scale, shift)
        gate1 = k.sb("gate1", [P, NJ, EX1])
        HC = H1 * C1
        with k.scope():
            g_local = k.sb("g_local", [P, S_GAT])
            g_from = k.sb("g_from", [P, S_GAT], I32)
            with k.scope():
                rec_g = k.sb("rec_g", [P, S_GAT, REC_GAT])
                from_f = k.sb("from_f", [P, S_GAT])
                load_all(k, "by_gat_load", [(rec_g[:, :, :], by_gat.rearrange("(p s) w -> p s w", p=P))])

                def unpack_g(dve, link):
                    link(dve.tensor_copy(g_local[:, :], rec_g[:, :, 0]))
                    link(dve.tensor_scalar(from_f[:, :], rec_g[:, :, 1], 0.0, float(N - 1), ALU.max, ALU.min))
                    link(dve.tensor_copy(g_from[:, :], from_f[:, :]))

                vector_only(k, "unpack_g", unpack_g)
            h_node = k.sb("h_node", [P, NJ, HC])
            project(k, "gat_h", k.X, NB, BT, scale, shift, w_gat, HC, keep=h_node)
            attention_gates(k, h_node, gate1, gat_table, g_local, g_from, tile_gat, att_src, att_dst, b_gat,
                            ln_gamma, ln_beta)
        if stop == "gates":
            return store_nodes(k, out, gate1)

        with k.scope():
            c1_t = k.sb("c1_t", [P, EX1, HID1 // P])
            by_channel(k, "c1_load", [c1], flat2(c1_t[:, :, :]))
            mixture(k, "ffn1", scale, shift, gate1, EX1, HID1, ACT.Gelu, [(u1, None, c1_t)], u2, c2)
        store_nodes(k, out)


def store_nodes(k, out, gates=None):
    full = (NJ - 1) * P
    load_all(k, "store", [(tile_rows(out[0:full, :]), k.X[:, 0:NJ - 1, :]),
                          (out[full:N, :], k.X[0:N - full, NJ - 1, :])])
    if gates is not None:
        load_all(k, "store_g", [(tile_rows(out[0:full, 0:EX1]), gates[:, 0:NJ - 1, :])])


def scale_rows(k, name, table, by):
    nc = k.nc
    loaded, scaled, stored = (k.sem(f"{name}_{s}") for s in ("loaded", "scaled", "stored"))
    with k.scope():
        rows = k.sb("rows", [P, BT, F])
        blocks = table.rearrange("(b j p) f -> b p j f", p=P, j=BT)
        with nc.Block() as block:

            @block.sync
            def _(sp):
                with sp.Fori(0, NB) as b:
                    now = blocks[bass.ds(b, 1), :, :, :].rearrange("a p j f -> p (a j) f")
                    sp.dma_start(rows[:, :, :], now).then_inc(loaded, 16)
                    hold(k, sp, scaled, b * BT + BT)
                    sp.dma_start(now, rows[:, :, :]).then_inc(stored, 16)
                    hold(k, sp, stored, b * 16 + 16)

            @block.vector
            def _(dve):
                with dve.Fori(0, NB) as b:
                    dve.wait_ge(loaded, b * 16 + 16)
                    for u in range(BT):
                        heads = rows[:, u, :].rearrange("p (h c) -> p h c", h=H0)
                        weight = by[:, bass.ds(b * BT + u, 1), :].rearrange("p a h -> p (a h)")
                        dve.tensor_tensor(heads, heads, weight.unsqueeze(2).to_broadcast([P, H0, C0]),
                                          ALU.mult).then_inc(scaled, 1)


def softmax_gate(k, gate, br):
    shifted, exped, linked = k.sem("gate_shifted"), k.sem("gate_exp"), k.sem("gate_link")
    with k.scope():
        br_b = k.sb("br_b", [P, EX0])
        most = k.sb("most", [P, NJ])
        load_all(k, "br_load", [(br_b[:, :], br.partition_broadcast(P))])
        with k.nc.Block() as block:

            @block.vector
            def _(dve):
                link = Link(dve, linked)
                link(dve.tensor_tensor(gate[:, :, :], gate[:, :, :], br_b[:, :].unsqueeze(1).to_broadcast([P, NJ, EX0]),
                                       ALU.add))
                link(dve.tensor_reduce(most[:, :], gate[:, :, :], AX.X, ALU.max))
                dve.tensor_tensor(gate[:, :, :], gate[:, :, :], most[:, :].unsqueeze(2).to_broadcast([P, NJ, EX0]),
                                  ALU.subtract).then_inc(shifted, 1)
                dve.wait_ge(exped, 1)
                link(dve.tensor_reduce(most[:, :], gate[:, :, :], AX.X, ALU.add))
                link(dve.reciprocal(most[:, :], most[:, :]))
                link(dve.tensor_tensor(gate[:, :, :], gate[:, :, :], most[:, :].unsqueeze(2).to_broadcast([P, NJ, EX0]),
                                       ALU.mult))

            @block.scalar
            def _(act):
                act.wait_ge(shifted, 1)
                act.activation(gate[:, :, :], gate[:, :, :], ACT.Exp).then_inc(exped, 1)


def by_channel(k, name, arrays, out):
    nc = k.nc
    loaded, flipped, copied = (k.sem(f"{name}_{s}") for s in ("loaded", "flipped", "copied"))
    experts, channels = arrays[0].shape
    each = experts * channels // P
    rows = each * len(arrays)
    with k.scope():
        lines = k.sb("lines", [rows, P])
        ps = k.ps("ps_lines", [P, 512])
        with nc.Block() as block:

            @block.sync
            def _(sp):
                for n, a in enumerate(arrays):
                    sp.dma_start(lines[n * each:(n + 1) * each, :], a.rearrange("e (c p) -> (e c) p", p=P)).then_inc(loaded, 16)

            @block.tensor
            def _(pe):
                pe.wait_ge(loaded, 16 * len(arrays))
                pe.transpose(ps[:, 0:rows], lines[:, :], k.ident[0:rows, 0:rows]).then_inc(flipped, 1)

            @block.scalar
            def _(act):
                act.wait_ge(flipped, 1)
                act.copy(out, ps[:, 0:rows]).then_inc(copied, 1)


def batch_norm(k, name, b, g, be, m, v):
    ct = HID0 // P
    every = k.sb(f"{name}_params", [P, 5, EX0, ct])
    t = {n: every[:, i, :, :] for i, n in enumerate(("b", "g", "be", "m", "v"))}
    ready, rooted, linked = k.sem(f"{name}_ready"), k.sem(f"{name}_root"), k.sem(f"{name}_link")
    by_channel(k, f"{name}_load", [b, g, be, m, v], every[:, :, :, :].rearrange("p n e c -> p (n e c)"))
    with k.nc.Block() as block:

        @block.vector
        def _(dve):
            link = Link(dve, linked)
            dve.tensor_scalar(t["v"][:, :, :], t["v"][:, :, :], BN_EPS, None, ALU.add).then_inc(ready, 1)
            dve.wait_ge(rooted, 1)
            link(dve.reciprocal(t["v"][:, :, :], t["v"][:, :, :]))
            link(dve.tensor_tensor(t["g"][:, :, :], t["g"][:, :, :], t["v"][:, :, :], ALU.mult))
            link(dve.tensor_tensor(t["b"][:, :, :], t["b"][:, :, :], t["m"][:, :, :], ALU.subtract))
            link(dve.tensor_tensor(t["b"][:, :, :], t["b"][:, :, :], t["g"][:, :, :], ALU.mult))
            link(dve.tensor_tensor(t["b"][:, :, :], t["b"][:, :, :], t["be"][:, :, :], ALU.add))

        @block.scalar
        def _(act):
            act.wait_ge(ready, 1)
            act.activation(t["v"][:, :, :], t["v"][:, :, :], ACT.Sqrt).then_inc(rooted, 1)

    return t["g"], t["b"]


def attention_gates(k, h_node, gate, gat_table, g_local, g_from, tile_gat, att_src, att_dst, b_gat, ln_gamma, ln_beta):
    nc = k.nc
    HC = H1 * C1
    ROW = H1 + HC
    with k.scope():
        value = k.sb("value", [P, S_GAT, ROW])
        row = k.sb("row", [P, NJ, ROW])
        prod = k.sb("prod", [P, NJ, HC])
        a_dst = k.sb("a_dst", [P, NJ, H1])
        top = k.sb("top", [P, NJ, H1])
        own = k.sb("own", [P, NJ, H1])
        low = k.sb("low", [P, H1])
        node = k.sb("node", [P, NJ, 2 * H1])
        total = k.sb("total", [P, NJ, ROW])
        small = {n: k.sb(n, [P, HC]) for n in ("s_src", "s_dst", "s_bias", "s_gamma", "s_beta")}
        load_all(k, "gat_params", [
            (small["s_src"][:, :], att_src.rearrange("h c -> (h c)").partition_broadcast(P)),
            (small["s_dst"][:, :], att_dst.rearrange("h c -> (h c)").partition_broadcast(P)),
            (small["s_bias"][:, :], b_gat.partition_broadcast(P)),
            (small["s_gamma"][:, :], ln_gamma.partition_broadcast(P)),
            (small["s_beta"][:, :], ln_beta.partition_broadcast(P))])

        def wide(t):
            return t[:, :].unsqueeze(1).to_broadcast([P, NJ, HC])

        def heads(t):
            return t.rearrange("p j (h c) -> p (j h) c", h=H1)

        def per_head(t):
            return t.rearrange("p j h -> p (j h)").unsqueeze(2).to_broadcast([P, NJ * H1, C1])

        def sides(dve, link):
            link(dve.tensor_tensor(prod[:, :, :], h_node[:, :, :], wide(small["s_dst"]), ALU.mult))
            link(dve.tensor_reduce(flat2(a_dst[:, :, :]), heads(prod[:, :, :]), AX.X, ALU.add))
            link(dve.tensor_tensor(prod[:, :, :], h_node[:, :, :], wide(small["s_src"]), ALU.mult))
            link(dve.tensor_reduce(flat2(own[:, :, :]), heads(prod[:, :, :]), AX.X, ALU.add))
            link(dve.tensor_copy(row[:, :, 0:H1], own[:, :, :]))
            link(dve.tensor_copy(row[:, :, H1:ROW], h_node[:, :, :]))

        vector_only(k, "gat_sides", sides)
        load_all(k, "gat_rows", [(tile_rows(gat_table), row[:, :, :])])
        least(k, "least1", own[:, :, :], low, H1)

        def first_top(dve, link):
            link(dve.tensor_tensor(top[:, :, :], own[:, :, :], low[:, :].unsqueeze(1).to_broadcast([P, NJ, H1]),
                                   ALU.subtract))

        vector_only(k, "gat_first_top", first_top)
        segment_max(k, "max1", S_GAT, H1, ROW, gat_table, g_from, g_local, tile_gat, low, value, top)

        shifted, exped, linked = k.sem("own_shifted"), k.sem("own_exp"), k.sem("own_link")
        with nc.Block() as block:

            @block.vector
            def _(dve):
                link = Link(dve, linked)
                link(dve.tensor_tensor(top[:, :, :], top[:, :, :], low[:, :].unsqueeze(1).to_broadcast([P, NJ, H1]),
                                       ALU.add))
                link(dve.tensor_tensor(top[:, :, :], top[:, :, :], a_dst[:, :, :], ALU.add))
                link(dve.scalar_tensor_tensor(node[:, :, 0:H1], top[:, :, :], 0.2, top[:, :, :], ALU.mult, ALU.max))
                link(dve.tensor_copy(node[:, :, H1:2 * H1], a_dst[:, :, :]))
                link(dve.tensor_tensor(own[:, :, :], own[:, :, :], a_dst[:, :, :], ALU.add))
                link(dve.scalar_tensor_tensor(own[:, :, :], own[:, :, :], 0.2, own[:, :, :], ALU.mult, ALU.max))
                link(dve.tensor_tensor(own[:, :, :], own[:, :, :], node[:, :, 0:H1], ALU.subtract))
                dve.tensor_scalar(own[:, :, :], own[:, :, :], 0.0, None, ALU.min).then_inc(shifted, 1)
                dve.wait_ge(exped, 1)
                link(dve.tensor_copy(total[:, :, 0:H1], own[:, :, :]))
                link(dve.tensor_tensor(heads(prod[:, :, :]), heads(h_node[:, :, :]), per_head(own[:, :, :]), ALU.mult))
                link(dve.tensor_copy(total[:, :, H1:ROW], prod[:, :, :]))

            @block.scalar
            def _(act):
                act.wait_ge(shifted, 1)
                act.activation(own[:, :, :], own[:, :, :], ACT.Exp).then_inc(exped, 1)

        def message(dve, link, msg, at):
            if dve is None:
                return HALF
            for u in range(HALF):
                link(dve.tensor_tensor(
                    msg[:, u, H1:ROW].rearrange("p (h c) -> p h c", h=H1),
                    value[:, bass.ds(at.start + u, 1), H1:ROW].rearrange("p a (h c) -> p (a h) c", h=H1),
                    msg[:, u, 0:H1].unsqueeze(2).to_broadcast([P, H1, C1]), ALU.mult))
            return HALF

        segment_softmax(k, "soft1", S_GAT, H1, g_local, tile_gat, node, value, ROW, message, False, total)

        mean = k.sb("mean", [P, NJ])
        var = k.sb("var", [P, NJ])
        agg = k.sb("agg", [P, NJ, HC])
        scores = k.sb("scores", [P, NJ, EX1])
        picked = [k.sb(f"picked{n}", [P, NJ, EX1]) for n in (0, 1)]
        best = [k.sb(f"best{n}", [P, NJ]) for n in (0, 1)]
        taken = k.sb("taken", [P, NJ])
        free = k.sb("free", [P, NJ])
        ready, rooted, shifted2, exped2, linked2 = (k.sem(f"gates_{s}") for s in
                                                    ("var", "root", "shifted", "exp", "link"))
        with nc.Block() as block:

            @block.vector
            def _(dve):
                link = Link(dve, linked2)

                def each(t):
                    return t[:, :].unsqueeze(2).to_broadcast([P, NJ, HC])

                link(dve.tensor_scalar(own[:, :, :], total[:, :, 0:H1], 1e-16, None, ALU.add))
                link(dve.reciprocal(own[:, :, :], own[:, :, :]))
                link(dve.tensor_copy(agg[:, :, :], total[:, :, H1:ROW]))
                link(dve.tensor_tensor(heads(agg[:, :, :]), heads(agg[:, :, :]), per_head(own[:, :, :]), ALU.mult))
                link(dve.tensor_tensor(agg[:, :, :], agg[:, :, :], wide(small["s_bias"]), ALU.add))
                link(dve.tensor_reduce(mean[:, :], agg[:, :, :], AX.X, ALU.add))
                link(dve.tensor_scalar(mean[:, :], mean[:, :], 1.0 / HC, None, ALU.mult))
                link(dve.tensor_tensor(agg[:, :, :], agg[:, :, :], each(mean), ALU.subtract))
                link(dve.tensor_tensor(prod[:, :, :], agg[:, :, :], agg[:, :, :], ALU.mult))
                link(dve.tensor_reduce(var[:, :], prod[:, :, :], AX.X, ALU.add))
                dve.tensor_scalar(var[:, :], var[:, :], 1.0 / HC, LN_EPS, ALU.mult, ALU.add).then_inc(ready, 1)
                dve.wait_ge(rooted, 1)
                link(dve.reciprocal(var[:, :], var[:, :]))
                link(dve.tensor_tensor(agg[:, :, :], agg[:, :, :], each(var), ALU.mult))
                link(dve.tensor_tensor(agg[:, :, :], agg[:, :, :], wide(small["s_gamma"]), ALU.mult))
                link(dve.tensor_tensor(agg[:, :, :], agg[:, :, :], wide(small["s_beta"]), ALU.add))
                link(dve.tensor_reduce(scores[:, :, :], agg[:, :, :].rearrange("p j (h c) -> p j c h", h=H1),
                                       AX.X, ALU.add))
                link(dve.tensor_scalar(scores[:, :, :], scores[:, :, :], 1.0 / H1, None, ALU.mult))
                for n in (0, 1):
                    link(dve.tensor_reduce(best[n][:, :], scores[:, :, :], AX.X, ALU.max))
                    link(dve.memset(taken[:, :], 0.0))
                    for e in range(EX1):
                        link(dve.tensor_tensor(picked[n][:, :, e], scores[:, :, e], best[n][:, :], ALU.is_equal))
                        link(dve.tensor_scalar(free[:, :], taken[:, :], -1.0, 1.0, ALU.mult, ALU.add))
                        link(dve.tensor_tensor(picked[n][:, :, e], picked[n][:, :, e], free[:, :], ALU.mult))
                        link(dve.tensor_tensor(taken[:, :], taken[:, :], picked[n][:, :, e], ALU.add))
                    if n == 0:
                        link(dve.scalar_tensor_tensor(scores[:, :, :], picked[0][:, :, :], -3e38, scores[:, :, :],
                                                      ALU.mult, ALU.add))
                dve.tensor_tensor(best[1][:, :], best[1][:, :], best[0][:, :], ALU.subtract).then_inc(shifted2, 1)
                dve.wait_ge(exped2, 1)
                link(dve.tensor_scalar(best[0][:, :], best[1][:, :], 1.0, None, ALU.add))
                link(dve.reciprocal(best[0][:, :], best[0][:, :]))
                link(dve.tensor_tensor(best[1][:, :], best[1][:, :], best[0][:, :], ALU.mult))
                for n in (0, 1):
                    link(dve.tensor_tensor(picked[n][:, :, :], picked[n][:, :, :],
                                           best[n][:, :].unsqueeze(2).to_broadcast([P, NJ, EX1]), ALU.mult))
                link(dve.tensor_tensor(gate[:, :, :], picked[0][:, :, :], picked[1][:, :, :], ALU.add))

            @block.scalar
            def _(act):
                act.wait_ge(ready, 1)
                act.activation(var[:, :], var[:, :], ACT.Sqrt).then_inc(rooted, 1)
                act.wait_ge(shifted2, 1)
                act.activation(best[1][:, :], best[1][:, :], ACT.Exp).then_inc(exped2, 1)


_INS = ["x", "src", "dst", "edge_weight", "L0_gnn_hyperedge_attr", "L0_gnn_W", "L0_gnn_att", "L0_ffn_Wr", "L0_ffn_br",
        "L0_ffn_W1", "L0_ffn_b1", "L0_ffn_g1", "L0_ffn_be1", "L0_ffn_m1", "L0_ffn_v1", "L0_ffn_W2", "L0_ffn_b2",
        "L0_ffn_g2", "L0_ffn_be2", "L0_ffn_m2", "L0_ffn_v2", "L0_ffn_Wo", "L0_ffn_bo", "L1_gnn_weight", "L1_gnn_bias",
        "L1_ffn_W_gat", "L1_ffn_att_src", "L1_ffn_att_dst", "L1_ffn_b_gat", "L1_ffn_ln_gamma", "L1_ffn_ln_beta",
        "L1_ffn_W1", "L1_ffn_b1", "L1_ffn_W2", "L1_ffn_b2", "L1_ffn_edge_index"]


def kernel(**inputs):
    import concourse.bacc as bacc
    import numpy as np
    from concourse.bass_utils import run_bass_kernel_spmd

    nc = bacc.Bacc("TRN2", target_bir_lowering=False, num_devices=1)
    arrays, args = {}, []
    for name in _INS:
        a = np.ascontiguousarray(inputs[name])
        arrays[f"in_{name}"] = a
        args.append(nc.dram_tensor(f"in_{name}", a.shape, mybir.dt.from_np(a.dtype), kind="ExternalInput").ap())
    args.append(nc.dram_tensor("out_0", (N, F), F32, kind="ExternalOutput").ap())
    graph_network(nc, *args)
    r = run_bass_kernel_spmd(nc, [arrays], core_ids=[0])
    return r.results[0]["out_0"]
```

```python
from contextlib import ExitStack

import concourse.bass as bass
from concourse import mybir

F32 = mybir.dt.float32
I32 = mybir.dt.int32
BF16 = mybir.dt.bfloat16
ALU = mybir.AluOpType
ACT = mybir.ActivationFunctionType
AX = mybir.AxisListType
DVE = mybir.EngineType.DVE
PE = mybir.EngineType.PE

P = 128
N, F = 6250, 256
E = 106250
M = 1250
EG = 131072
NJ = -(-N // P)
MJ = -(-M // P)
H0, C0 = 8, 32
EX0, HID0 = 8, 256
H1, C1 = 4, 4
EX1, HID1 = 4, 512
LN_EPS = 1e-5
BN_EPS = 1e-3
HALF = 8
BODY = 2 * HALF
BT = 7
NB = NJ // BT
NOWHERE = float(2 ** 20)


def steps_for(edges, tiles):
    most = (edges + tiles * (P - 1)) // P
    return -(-most // BODY) * BODY


S_SRC = steps_for(E, NJ)
S_DST = steps_for(E, MJ)
S_GAT = steps_for(EG, NJ)


class Link:

    def __init__(self, eng, sem):
        self.eng, self.sem, self.base, self.n = eng, sem, 0, 0

    def __call__(self, ins):
        ins.then_inc(self.sem, 1)
        self.n += 1
        self.eng.wait_ge(self.sem, self.base + self.n)

    def loop(self, i, per, first=0):
        self.start, self.per = self.base + self.n, per
        self.base, self.n = i * per + (self.start - first * per), 0

    def end(self, count):
        assert self.n == self.per, (self.n, self.per)
        self.base, self.n = self.start + count * self.per, 0


def turns(eng, count, body, link=None, per=0, tail=False):
    body(0, False)
    stop = count - 1 if tail else count
    with eng.Fori(1, stop) as i:
        if link is not None:
            link.loop(i, per, 1)
        body(i, False)
    if link is not None:
        link.end(stop - 1)
    if tail:
        body(count - 1, True)


def is_first(i):
    return isinstance(i, int) and i == 0


def reached(eng, sem, value):
    if not (isinstance(value, int) and value == 0):
        eng.wait_ge(sem, value)


def hold(k, eng, sem, value):
    if not (isinstance(value, int) and value == 0):
        eng.wait_ge(sem, value)
        eng.sem_inc(k.held, 1)


def tile_rows(dram):
    return dram.rearrange("(j p) f -> p j f", p=P)


class Core:

    def __init__(self, nc, stack):
        self.nc, self.stack, self.scopes, self.names = nc, stack, [stack], {}
        self.live = []

    def name(self, name):
        self.names[name] = self.names.get(name, 0) + 1
        return name if self.names[name] == 1 else f"{name}_{self.names[name]}"

    def sb(self, name, shape, dt=F32):
        return self.scopes[-1].enter_context(self.nc.sbuf_tensor(self.name(name), shape, dt))

    def ps(self, name, shape, dt=F32):
        return self.scopes[-1].enter_context(self.nc.psum_tensor(self.name(name), shape, dt))

    def sem(self, name):
        self.live.append(self.nc.alloc_semaphore(name=name))
        return self.live[-1]

    def recycle(self):
        self.nc.clear_and_free_semaphores(self.live)
        self.nc.all_engine_barrier()
        self.live = []

    def sems(self, name, n):
        return [self.sem(f"{name}{k}") for k in range(n)]

    def dram(self, name, shape, dt=F32):
        return self.nc.dram_tensor(name, shape, dt).ap()

    def scope(self):
        return Scope(self)


class Scope:

    def __init__(self, core):
        self.core = core

    def __enter__(self):
        self.own = ExitStack()
        self.own.__enter__()
        self.core.scopes.append(self.own)
        return self

    def __exit__(self, *a):
        self.core.scopes.pop()
        return self.own.__exit__(*a)


def load_nodes(k, x):
    nc = k.nc
    loaded, made, linked = k.sem("x_loaded"), k.sem("consts_made"), k.sem("setup_link")
    iota_i = k.sb("iota_i", [P, P], I32)
    part_i = k.sb("part_i", [P, P], I32)
    part_f = k.sb("part_f", [P, P])
    full = (NJ - 1) * P
    with nc.Block() as block:

        @block.gpsimd
        def _(pool):
            pool.iota(iota_i[:, :], [[1, P]], base=0, channel_multiplier=0).then_inc(made, 1)
            pool.iota(part_i[:, :], [[0, P]], base=0, channel_multiplier=1).then_inc(made, 1)

        @block.sync
        def _(sp):
            sp.dma_start(k.X[:, 0:NJ - 1, :], tile_rows(x[0:full, :])).then_inc(loaded, 16)
            sp.wait_ge(linked, 1)
            sp.dma_start(k.X[0:N - full, NJ - 1, :], x[full:N, :]).then_inc(loaded, 16)
            sp.wait_ge(loaded, 32)

        @block.vector
        def _(dve):
            link = Link(dve, linked)
            link(dve.memset(k.X[:, NJ - 1, :], 0.0))
            dve.memset(k.ones[:, :], 1.0)
            dve.wait_ge(made, 2)
            link(dve.tensor_copy(k.iota[:, :], iota_i[:, :]))
            link(dve.tensor_copy(part_f[:, :], part_i[:, :]))
            link(dve.tensor_tensor(k.ident[:, :], k.iota[:, :], part_f[:, :], ALU.is_equal))
            link(dve.tensor_tensor(k.before[:, :], k.iota[:, :], part_f[:, :], ALU.is_gt))
            link(dve.tensor_copy(k.ident16[:, :], k.ident[:, :]))
            link(dve.tensor_scalar(k.far[:, :, :], k.ident[:, :].unsqueeze(1).to_broadcast([P, 4, P]), -2.0 ** 100,
                                   None, ALU.mult))
            link(dve.tensor_scalar(part_i[:, :], part_i[:, :], 31, None, ALU.bitwise_and))
            link(dve.tensor_copy(part_f[:, :], part_i[:, :]))
            link(dve.tensor_tensor(k.pick[:, :], k.iota[0:96, 0:32], part_f[0:96, 0:32], ALU.is_equal))


class Ranks:

    def __init__(self, k, name, key, rows, cols, tiles, steps, slot, step_tile):
        self.k, self.key, self.rows, self.cols, self.tiles, self.steps = k, key, rows, cols, tiles, steps
        self.slot, self.step_tile = slot, step_tile
        self.loaded, self.counted, self.offset, self.linked, self.made = (
            k.sem(f"{name}_{s}") for s in ("key_loaded", "counted", "offset", "link", "steps_made"))
        self.key_i = k.sb("key_i", [rows, cols], I32)
        self.tile_f = k.sb("tile_f", [rows, cols])
        self.hit = k.sb("hit", [rows, cols])
        self.run = k.sb("run", [rows, cols])
        self.place = k.sb("place", [rows, cols])
        self.count = k.sb("count", [rows, tiles])
        self.tot_f = k.sb("tot_f", [P, tiles])
        self.tot_i = k.sb("tot_i", [P, tiles], I32)
        self.first = k.sb("first", [P, tiles])
        self.base = k.sb("base", [rows, tiles])
        self.step_i = k.sb("step_i", [1, steps], I32)
        self.step_f = k.sb("step_f", [1, steps])
        self.tile_of = k.sb("tile_of", [1, steps])
        self.ps_before = k.ps("ps_before", [P, 512])
        self.ps_total = k.ps("ps_total", [P, 512])

    def sync(self, sp):
        sp.dma_start(self.key_i[:, :], self.key.rearrange("(p c) -> p c", p=self.rows)).then_inc(self.loaded, 16)

    def gpsimd(self, pool):
        pool.iota(self.step_i[:, :], [[1, self.steps]], base=0, channel_multiplier=0).then_inc(self.made, 1)

    def vector(self, dve):
        k, rows, tiles = self.k, self.rows, self.tiles
        key_i, tile_f, hit, run, place, slot = self.key_i, self.tile_f, self.hit, self.run, self.place, self.slot
        tot_f, tot_i, first, tile_of = self.tot_f, self.tot_i, self.first, self.tile_of
        link = Link(dve, self.linked)
        dve.wait_ge(self.made, 1)
        link(dve.tensor_copy(self.step_f[:, :], self.step_i[:, :]))
        link(dve.memset(tile_of[:, :], -1.0))
        link(dve.memset(place[:, :], 0.0))
        dve.wait_ge(self.loaded, 16)
        link(dve.tensor_scalar(key_i[:, :], key_i[:, :], 7, None, ALU.arith_shift_right))
        link(dve.tensor_copy(tile_f[:, :], key_i[:, :]))
        with dve.Fori(0, tiles) as b:
            link.loop(b, 1)
            link(dve.tensor_scalar(hit[:, :], tile_f[:, :], k.iota[0:rows, bass.ds(b, 1)], None,
                                   ALU.is_equal, ALU.add, accum_out=self.count[:, bass.ds(b, 1)]))
        link.end(tiles)
        dve.sem_inc(self.counted, 1)
        dve.wait_ge(self.offset, 2)
        link(dve.tensor_scalar(tot_f[:, :], self.ps_total[:, 0:tiles], float(P - 1), None, ALU.add))
        link(dve.tensor_copy(tot_i[:, :], tot_f[:, :]))
        link(dve.tensor_scalar(tot_i[:, :], tot_i[:, :], 7, None, ALU.arith_shift_right))
        link(dve.tensor_copy(tot_f[:, :], tot_i[:, :]))
        link(dve.tensor_tensor_scan(first[:, :], tot_f[:, :], tot_f[:, :], 0.0, ALU.add, ALU.max))
        link(dve.tensor_tensor(first[:, :], first[:, :], tot_f[:, :], ALU.subtract))
        link(dve.scalar_tensor_tensor(self.base[:, :], first[0:rows, :], float(P), self.ps_before[0:rows, 0:tiles],
                                      ALU.mult, ALU.add))
        with dve.Fori(0, tiles) as b:
            link.loop(b, 5)
            this = k.iota[0:rows, bass.ds(b, 1)]
            link(dve.tensor_scalar(hit[:, :], tile_f[:, :], this, None, ALU.is_equal))
            link(dve.tensor_tensor_scan(run[:, :], hit[:, :], hit[:, :], self.base[:, bass.ds(b, 1)],
                                        ALU.add, ALU.max))
            link(dve.tensor_tensor(hit[:, :], hit[:, :], run[:, :], ALU.mult))
            link(dve.tensor_tensor(place[:, :], place[:, :], hit[:, :], ALU.add))
            link(dve.scalar_tensor_tensor(tile_of[:, :], self.step_f[:, :], first[0:1, bass.ds(b, 1)],
                                          tile_of[:, :], ALU.is_ge, ALU.add))
        link.end(tiles)
        link(dve.tensor_copy(self.step_tile[0:1, :], tile_of[:, :]))
        link(dve.tensor_scalar(hit[:, :], place[:, :], 1.0, NOWHERE, ALU.is_lt, ALU.mult))
        link(dve.scalar_tensor_tensor(place[:, :], place[:, :], -1.0, hit[:, :], ALU.add, ALU.add))
        link(dve.tensor_copy(key_i[:, :], place[:, :]))
        link(dve.tensor_scalar(slot[:, :], key_i[:, :], P - 1, None, ALU.bitwise_and))
        link(dve.tensor_scalar(key_i[:, :], key_i[:, :], 7, None, ALU.arith_shift_right))
        link(dve.tensor_copy(hit[:, :], slot[:, :]))
        link(dve.tensor_copy(run[:, :], key_i[:, :]))
        link(dve.scalar_tensor_tensor(place[:, :], hit[:, :], float(self.steps), run[:, :], ALU.mult, ALU.add))
        link(dve.tensor_copy(slot[:, :], place[:, :]))

    def tensor(self, pe):
        k, rows, tiles = self.k, self.rows, self.tiles
        pe.wait_ge(self.counted, 1)
        pe.matmul(self.ps_before[0:rows, 0:tiles], k.before[0:rows, 0:rows], self.count[:, :],
                  start=True, stop=True).then_inc(self.offset, 1)
        pe.matmul(self.ps_total[:, 0:tiles], k.ones[0:rows, 0:P], self.count[:, :],
                  start=True, stop=True).then_inc(self.offset, 1)


def rank_edges(k, *args):
    with k.scope():
        ranks = Ranks(k, *args)
        with k.nc.Block() as block:

            @block.sync
            def _(sp):
                ranks.sync(sp)

            @block.gpsimd
            def _(pool):
                ranks.gpsimd(pool)

            @block.vector
            def _(dve):
                ranks.vector(dve)

            @block.tensor
            def _(pe):
                ranks.tensor(pe)


def fill_rows(k, name, fills):
    filled, blank = k.sem(f"{name}_filled"), k.sem(f"{name}_blank")
    with k.scope():
        empty = [k.sb("empty", [P, out.shape[0] // P * out.shape[1]]) for out, _ in fills]
        with k.nc.Block() as block:

            @block.vector
            def _(dve):
                for t, (_, value) in zip(empty, fills):
                    dve.memset(t[:, :], value).then_inc(blank, 1)

            @block.sync
            def _(sp):
                for n, (t, (out, _)) in enumerate(zip(empty, fills)):
                    sp.wait_ge(blank, n + 1)
                    sp.dma_start(out.rearrange("(p s) w -> p (s w)", p=P), t[:, :]).then_inc(filled, 16)
                sp.wait_ge(filled, 16 * len(fills))


class Scatter:

    def __init__(self, k, name, rows, chunk, width, out):
        self.k, self.rows, self.chunk, self.width, self.out = k, rows, chunk, width, out
        self.copied = k.sem(f"{name}_copied")
        self.stored = k.sems(f"{name}_stored", 2)
        self.record = [k.sb("record", [rows, chunk, width]) for _ in (0, 1)]
        self.where = [k.sb("where", [rows, chunk], I32) for _ in (0, 1)]

    def turn(self, pool, i, h, fields, slot, before=None):
        chunk = self.chunk
        at = bass.ds(i * (2 * chunk) + h * chunk, chunk)
        n = len(fields) + 1
        hold(self.k, pool, self.stored[h], i * (chunk * 16))
        if before is not None:
            before()
        for lo, w, src in fields:
            pool.tensor_copy(self.record[h][:, :, lo:lo + w], src[:, at, :]).then_inc(self.copied, 1)
        pool.tensor_copy(self.where[h][:, :], slot[:, at]).then_inc(self.copied, 1)
        hold(self.k, pool, self.copied, i * (2 * n) + (h + 1) * n)
        for u in range(chunk):
            pool.indirect_dma_start(
                out=self.out, out_offset=bass.IndirectOffsetOnAxis(ap=self.where[h][:, u:u + 1], axis=0),
                in_=self.record[h][:, u, :], in_offset=None, bounds_check=self.out.shape[0] - 1,
                oob_is_err=False).then_inc(self.stored[h], 16)

    def finish(self, pool, bodies):
        for h in (0, 1):
            pool.wait_ge(self.stored[h], bodies * self.chunk * 16)

    def all(self, pool, fields, slot, bodies):
        def body(i, last):
            for h in (0, 1):
                self.turn(pool, i, h, fields, slot)

        turns(pool, bodies, body)
        self.finish(pool, bodies)


class Gather:

    def __init__(self, k, name, steps, table, index, width):
        self.k, self.steps, self.table, self.index = k, steps, table, index
        self.copied = k.sem(f"{name}_index_copied")
        self.landed, self.used = k.sems(f"{name}_landed", 2), k.sems(f"{name}_used", 2)
        self.index_now = [k.sb("index_now", [P, HALF], I32) for _ in (0, 1)]
        self.rows = [k.sb("rows", [P, HALF, width]) for _ in (0, 1)]

    def gpsimd(self, pool):
        def body(i, last):
            for h in (0, 1):
                reached(pool, self.used[h], i)
                hold(self.k, pool, self.copied, i * 2 + (h + 1))
                for u in range(HALF):
                    pool.indirect_dma_start(
                        out=self.rows[h][:, u, :], out_offset=None, in_=self.table,
                        in_offset=bass.IndirectOffsetOnAxis(ap=self.index_now[h][:, u:u + 1], axis=0)
                    ).then_inc(self.landed[h], 16)

        turns(pool, self.steps // BODY, body)

    def copy_index(self, act, i, h):
        reached(act, self.landed[h], i * (HALF * 16))
        act.copy(self.index_now[h][:, :], self.index[:, bass.ds(i * BODY + h * HALF, HALF)]).then_inc(self.copied, 1)


def load_tiles(nc, step_tile, i, tiles, engine):
    return nc.values_load_multi_w_load_instructions(
        step_tile[0:1, bass.ds(i * BODY, BODY)], engines=[engine], min_val=0, max_val=tiles - 1)[1]


def segment_max(k, name, steps, heads, width, table, index, local, step_tile, value, top):
    nc = k.nc
    groups = HALF * heads // 32
    each = HALF // groups
    banks = heads * P // 512
    names = ("kept", "parts", "flipped", "turned", "other", "product", "reduced", "maxed", "link")
    kept, parts_ok, flipped, turned, other_ok, product, reduced, maxed, linked = (
        k.sem(f"{name}_{s}") for s in names)
    with k.scope():
        g = Gather(k, name, steps, table, index, width)
        rest = k.sb("rest", [P, HALF, heads])
        parts = [k.sb("parts", [P, groups, 3, 32], BF16) for _ in (0, 1)]
        parts_t = [k.sb("parts_t", [96, groups, P], BF16) for _ in (0, 1)]
        other = [k.sb("other", [P, HALF, P], BF16) for _ in (0, 1)]
        most = k.sb("most", [P, HALF, heads])
        ps = [k.ps("ps_max", [P, heads, P]) for _ in (0, 1)]
        ps_t = [k.ps("ps_parts", [96, groups, P], BF16) for _ in (0, 1)]

        with nc.Block() as block:

            @block.gpsimd
            def _(pool):
                g.gpsimd(pool)

            @block.scalar
            def _(act):
                def body(i, last):
                    for h in (0, 1):
                        if is_first(i):
                            g.copy_index(act, i, h)
                    for h in (0, 1):
                        act.wait_ge(g.landed[h], i * (HALF * 16) + HALF * 16)
                        act.copy(value[:, bass.ds(i * BODY + h * HALF, HALF), :], g.rows[h][:, :, :]).then_inc(kept, 1)
                        act.wait_ge(kept, i * 2 + (h + 1))
                        if not last:
                            g.copy_index(act, i + 1, h)
                        act.sem_inc(g.used[h], 1)
                        act.wait_ge(flipped, (i * 2 + (h + 1)) * groups)
                        act.copy(parts_t[h][:, :, :], ps_t[h][:, :, :]).then_inc(turned, 1)

                turns(act, steps // BODY, body, tail=True)

            @block.vector
            def _(dve):
                link = Link(dve, linked)

                def split(i, h):
                    at = bass.ds(i * BODY + h * HALF, HALF)
                    dve.wait_ge(kept, i * 2 + (h + 1))

                    def part(n):
                        return parts[h][:, :, n, :].rearrange("p g (u c) -> p g u c", c=heads)

                    def by_group(x):
                        return x.rearrange("p (g u) c -> p g u c", g=groups)

                    left = by_group(rest[:, :, :])
                    now = by_group(value[:, at, 0:heads])
                    link(dve.tensor_copy(part(0), now))
                    link(dve.tensor_tensor(left, now, part(0), ALU.subtract))
                    link(dve.tensor_copy(part(1), left))
                    dve.tensor_tensor(part(2), left, part(1), ALU.subtract).then_inc(parts_ok, 1)
                    dve.tensor_tensor(other[h][:, :, :], k.iota[:, :].unsqueeze(1).to_broadcast([P, HALF, P]),
                                      local[:, at].unsqueeze(2).to_broadcast([P, HALF, P]),
                                      ALU.not_equal).then_inc(other_ok, 1)

                def body(i, last):
                    tiles = load_tiles(nc, step_tile, i, top.shape[1], DVE)
                    if is_first(i):
                        split(i, 0)
                    for h in (0, 1):
                        for u in range(HALF):
                            dve.wait_ge(product, (i * BODY + (h * HALF + u + 1)) * banks)
                            dve.tensor_reduce(most[:, u, :], ps[u % 2][:, :, :], AX.X, ALU.max).then_inc(reduced, 1)
                        if h == 0:
                            split(i, 1)
                        elif not last:
                            split(i + 1, 0)
                        dve.wait_ge(reduced, i * BODY + (h + 1) * HALF)
                        for u in range(HALF):
                            into = top[:, bass.ds(tiles[h * HALF + u], 1), :].rearrange("p a h -> p (a h)")
                            reached(dve, maxed, i * BODY + (h * HALF + u))
                            dve.tensor_tensor(into, into, most[:, u, :], ALU.max).then_inc(maxed, 1)

                turns(dve, steps // BODY, body, link, 2 * 3, tail=True)

            @block.tensor
            def _(pe):
                def body(i, last):
                    for h in (0, 1):
                        pe.wait_ge(parts_ok, i * 2 + (h + 1))
                        for c in range(groups):
                            pe.transpose(ps_t[h][:, c, :], parts[h][:, c, :, :].rearrange("p n c -> p (n c)"),
                                         k.ident16[:, :]).then_inc(flipped, 1)
                        pe.wait_ge(other_ok, i * 2 + (h + 1))
                        pe.wait_ge(turned, i * 2 + (h + 1))
                        for u in range(HALF):
                            n = h * HALF + u
                            if is_first(i) and n < 2:
                                pass
                            else:
                                pe.wait_ge(reduced, i * BODY + (n - 1))
                            for c in range(banks):
                                at = slice(c * 4, c * 4 + 4)
                                pe.matmul(ps[u % 2][:, at, :], other[h][:, u, :], k.far[:, :, :], start=True, stop=False)
                                for d in range(4):
                                    head = c * 4 + d
                                    row = (u % each) * heads + head
                                    ins = pe.matmul(ps[u % 2][:, head, :], k.pick[:, row:row + 1].to_broadcast([96, P]),
                                                    parts_t[h][:, u // each, :], start=False, stop=d == 3)
                                ins.then_inc(product, 1)

                turns(pe, steps // BODY, body)


def segment_softmax(k, name, steps, heads, local, step_tile, node, value, wide, message, total, scatter=None):
    nc = k.nc
    names = ("hot", "flipped", "turned", "spread", "shifted", "exped", "message", "summed", "added", "link", "blank",
             "kept")
    hot_ok, flipped, turned, spread, shifted, exped, message_ok, summed, added, linked, blank, kept = (
        k.sem(f"{name}_{s}") for s in names)
    with k.scope():
        hot = [k.sb(f"hot{h}", [P, HALF, P]) for h in (0, 1)]
        hot_t = [k.sb(f"hot_t{h}", [P, HALF, P]) for h in (0, 1)]
        logit = k.sb("logit", [P, HALF, heads])
        msg = [k.sb(f"msg{h}", [P, HALF, wide]) for h in (0, 1)]
        ps_t = [k.ps(f"ps_t{h}", [P, HALF, P]) for h in (0, 1)]
        ps_n = [k.ps(f"ps_n{h}", [P, 512]) for h in (0, 1)]
        ps_s = [k.ps(f"ps_s{h}", [P, 512]) for h in (0, 1)]
        at_node = [x[:, 0:HALF * 2 * heads].rearrange("p (u c) -> p u c", u=HALF) for x in ps_n]
        sums = [x[:, 0:HALF * wide].rearrange("p (u c) -> p u c", u=HALF) for x in ps_s]

        with nc.Block() as block:

            @block.vector
            def _(dve):
                link = Link(dve, linked)
                for h in (0, 1):
                    dve.memset(msg[h][:, :, :], 1.0).then_inc(blank, 1)

                def make_hot(i, h):
                    at = bass.ds(i * BODY + h * HALF, HALF)
                    dve.tensor_tensor(hot[h][:, :, :], k.iota[:, :].unsqueeze(1).to_broadcast([P, HALF, P]),
                                      local[:, at].unsqueeze(2).to_broadcast([P, HALF, P]),
                                      ALU.is_equal).then_inc(hot_ok, 1)

                def add(i, h, tiles):
                    dve.wait_ge(summed, i * BODY + (h + 1) * HALF)
                    for u in range(HALF):
                        into = total[:, bass.ds(tiles[u], 1), :].rearrange("p a w -> p (a w)")
                        reached(dve, added, i * BODY + (h * HALF + u))
                        dve.tensor_tensor(into, into, sums[h][:, u, :], ALU.add).then_inc(added, 1)

                def half_tiles(i, h):
                    return nc.values_load_multi_w_load_instructions(
                        step_tile[0:1, bass.ds(i * BODY + h * HALF, HALF)], engines=[DVE], min_val=0,
                        max_val=total.shape[1] - 1)[1]

                def body(i, last):
                    if is_first(i):
                        make_hot(i, 0)
                    for h in (0, 1):
                        if h == 1:
                            add(i, 0, half_tiles(i, 0))
                        elif not is_first(i):
                            add(i - 1, 1, half_tiles(i - 1, 1))
                        if h == 0:
                            make_hot(i, 1)
                        elif not last:
                            make_hot(i + 1, 0)
                        at = bass.ds(i * BODY + h * HALF, HALF)
                        dve.wait_ge(spread, (i * 2 + (h + 1)) * HALF)
                        link(dve.tensor_tensor(logit[:, :, :], value[:, at, 0:heads],
                                               at_node[h][:, :, heads:2 * heads], ALU.add))
                        link(dve.scalar_tensor_tensor(logit[:, :, :], logit[:, :, :], 0.2, logit[:, :, :],
                                                      ALU.mult, ALU.max))
                        link(dve.tensor_tensor(logit[:, :, :], logit[:, :, :], at_node[h][:, :, 0:heads],
                                               ALU.subtract))
                        dve.tensor_scalar(logit[:, :, :], logit[:, :, :], 0.0, None, ALU.min).then_inc(shifted, 1)
                        dve.wait_ge(exped, i * 2 + (h + 1))
                        if message is not None:
                            message(dve, msg[h], at).then_inc(message_ok, 1)
                    if last:
                        add(i, 1, half_tiles(i, 1))

                turns(dve, steps // BODY, body, link, 2 * 3, tail=True)

            @block.tensor
            def _(pe):
                def to_slots(i, h, tiles):
                    pe.wait_ge(hot_ok, i * 2 + (h + 1))
                    for u in range(HALF):
                        pe.transpose(ps_t[h][:, u, :], hot[h][:, u, :], k.ident[:, :]).then_inc(flipped, 1)
                    pe.wait_ge(turned, i * 2 + (h + 1))
                    for u in range(HALF):
                        pe.matmul(at_node[h][:, u, :], hot_t[h][:, u, :],
                                  node[:, bass.ds(tiles[u], 1), :].rearrange("p a c -> p (a c)"),
                                  start=True, stop=True).then_inc(spread, 1)

                def half_tiles(i, h):
                    return nc.values_load_multi_w_load_instructions(
                        step_tile[0:1, bass.ds(i * BODY + h * HALF, HALF)], engines=[PE], min_val=0,
                        max_val=total.shape[1] - 1)[1]

                def body(i, last):
                    if is_first(i):
                        to_slots(i, 0, half_tiles(i, 0))
                    for h in (0, 1):
                        if h == 0:
                            to_slots(i, 1, half_tiles(i, 1))
                        elif not last:
                            to_slots(i + 1, 0, half_tiles(i + 1, 0))
                        pe.wait_ge(exped if message is None else message_ok, i * 2 + (h + 1))
                        for u in range(HALF):
                            pe.matmul(sums[h][:, u, :], hot[h][:, u, :], msg[h][:, u, :],
                                      start=True, stop=True).then_inc(summed, 1)

                turns(pe, steps // BODY, body, tail=True)

            @block.scalar
            def _(act):
                act.wait_ge(blank, 2)

                def turn_hot(i, h):
                    act.wait_ge(flipped, (i * 2 + (h + 1)) * HALF)
                    act.copy(hot_t[h][:, :, :], ps_t[h][:, :, :]).then_inc(turned, 1)

                def body(i, last):
                    if is_first(i):
                        turn_hot(i, 0)
                    for h in (0, 1):
                        if is_first(i) and h == 0:
                            turn_hot(i, 1)
                        act.wait_ge(shifted, i * 2 + (h + 1))
                        act.activation(msg[h][:, :, 0:heads], logit[:, :, :], ACT.Exp).then_inc(exped, 1)
                        if scatter is not None:
                            act.wait_ge(exped, i * 2 + (h + 1))
                            act.copy(value[:, bass.ds(i * BODY + h * HALF, HALF), 0:heads],
                                     msg[h][:, :, 0:heads]).then_inc(kept, 1)
                        if h == 0 and not is_first(i):
                            turn_hot(i, 1)
                        elif h == 1 and not last:
                            turn_hot(i + 1, 0)

                turns(act, steps // BODY, body, tail=True)

            if scatter is not None:

                @block.gpsimd
                def _(pool):
                    scatter(pool, kept)


def segment_sum(k, name, steps, table, index, local, step_tile, total, width=F, edge_weight=None, probs=None,
                count=None):
    nc = k.nc
    linked, hot_ok, message_ok, summed, added = (
        k.sem(f"{name}_{s}") for s in ("link", "hot", "message", "summed", "added"))
    with k.scope():
        g = Gather(k, name, steps, table, index, F)
        hot = [k.sb(f"hot{h}", [P, HALF, P]) for h in (0, 1)]
        msg = g.rows if probs is None else [k.sb(f"msg{h}", [P, HALF, width]) for h in (0, 1)]
        ps = [k.ps("ps_sum", [P, 512]) for _ in range(HALF)]
        msgs = 2 if count is not None else 1
        with nc.Block() as block:

            @block.gpsimd
            def _(pool):
                g.gpsimd(pool)

            @block.vector
            def _(dve):
                link = Link(dve, linked)

                def make(i, h):
                    at = bass.ds(i * BODY + h * HALF, HALF)
                    same = dve.tensor_tensor(
                        hot[h][:, :, :], k.iota[:, :].unsqueeze(1).to_broadcast([P, HALF, P]),
                        local[:, at].unsqueeze(2).to_broadcast([P, HALF, P]), ALU.is_equal)
                    if edge_weight is None:
                        same.then_inc(hot_ok, 1)
                    else:
                        link(same)
                        dve.tensor_tensor(hot[h][:, :, :], hot[h][:, :, :],
                                          edge_weight[:, at].unsqueeze(2).to_broadcast([P, HALF, P]),
                                          ALU.mult).then_inc(hot_ok, 1)
                    if probs is not None:
                        dve.wait_ge(g.landed[h], i * (HALF * 16) + HALF * 16)
                        dve.tensor_tensor(
                            msg[h][:, :, 0:F].rearrange("p u (a c) -> p u a c", a=H0),
                            g.rows[h][:, :, :].rearrange("p u (a c) -> p u a c", a=H0),
                            probs[:, at, :].unsqueeze(3).to_broadcast([P, HALF, H0, C0]),
                            ALU.mult).then_inc(message_ok, 1)
                        if count is not None:
                            dve.tensor_copy(msg[h][:, :, F:F + 1], count[:, at].unsqueeze(2)).then_inc(message_ok, 1)

                def add(i, h):
                    tiles = nc.values_load_multi_w_load_instructions(
                        step_tile[0:1, bass.ds(i * BODY + h * HALF, HALF)], engines=[DVE], min_val=0,
                        max_val=total.shape[1] - 1)[1]
                    for u in range(HALF):
                        dve.wait_ge(summed, i * BODY + (h * HALF + u + 1))
                        reached(dve, added, i * BODY + (h * HALF + u))
                        into = total[:, bass.ds(tiles[u], 1), :].rearrange("p a w -> p (a w)")
                        dve.tensor_tensor(into, into, ps[u][:, 0:width], ALU.add).then_inc(added, 1)

                def body(i, last):
                    make(i, 0)
                    if not is_first(i):
                        add(i - 1, 1)
                    make(i, 1)
                    add(i, 0)
                    if last:
                        add(i, 1)

                turns(dve, steps // BODY, body, link, 0 if edge_weight is None else 2, tail=True)

            @block.tensor
            def _(pe):
                def body(i, last):
                    for h in (0, 1):
                        pe.wait_ge(hot_ok, i * 2 + (h + 1))
                        if probs is None:
                            pe.wait_ge(g.landed[h], i * (HALF * 16) + HALF * 16)
                        else:
                            pe.wait_ge(message_ok, (i * 2 + (h + 1)) * msgs)
                        for u in range(HALF):
                            if not (is_first(i) and h == 0):
                                pe.wait_ge(added, i * BODY + (h * HALF + u + 1 - HALF))
                            pe.matmul(ps[u][:, 0:width], hot[h][:, u, :], msg[h][:, u, 0:width],
                                      start=True, stop=True).then_inc(summed, 1)

                turns(pe, steps // BODY, body)

            @block.scalar
            def _(act):
                def body(i, last):
                    for h in (0, 1):
                        if is_first(i):
                            g.copy_index(act, i, h)
                    for h in (0, 1):
                        if not last:
                            g.copy_index(act, i + 1, h)
                        if probs is None:
                            act.wait_ge(summed, (i * 2 + (h + 1)) * HALF)
                        else:
                            act.wait_ge(message_ok, (i * 2 + (h + 1)) * msgs)
                        act.sem_inc(g.used[h], 1)

                turns(act, steps // BODY, body, tail=True)


def norm_scales(k, name, scale, shift):
    nc = k.nc
    stats_ok, rooted, linked = (k.sem(f"{name}_{s}") for s in ("variance", "root", "link"))
    with k.scope():
        stats = k.sb("stats", [P, NJ, 6])
        mean_var = k.sb("mean_var", [P, NJ, 2])
        with nc.Block() as block:

            @block.vector
            def _(dve):
                link = Link(dve, linked)
                for j in range(NJ):
                    ins = dve.bn_stats(stats[:, j, :], k.X[:, j, :])
                link(ins)
                for j in range(NJ):
                    ins = dve.bn_aggr(mean_var[:, j, :], stats[:, j, :])
                link(ins)
                dve.tensor_scalar(scale[:, :], mean_var[:, :, 1], LN_EPS, None, ALU.add).then_inc(stats_ok, 1)
                dve.wait_ge(rooted, 1)
                link(dve.reciprocal(scale[:, :], scale[:, :]))
                link(dve.scalar_tensor_tensor(shift[:, :], mean_var[:, :, 0], -1.0, scale[:, :], ALU.mult, ALU.mult))

            @block.scalar
            def _(act):
                act.wait_ge(stats_ok, 1)
                act.activation(scale[:, :], scale[:, :], ACT.Sqrt).then_inc(rooted, 1)


class Normed:

    def __init__(self, k, name, src, bt, scale, shift, ps):
        self.k, self.src, self.bt, self.scale, self.shift, self.ps = k, src, bt, scale, shift, ps
        self.flat = k.sb("flat", [P, bt, F])
        self.xt = k.sb("xt", [P, 2, bt * P])
        self.normed, self.flipped, self.copied = (k.sem(f"{name}_{s}") for s in ("normed", "flipped", "xt_copied"))

    def vector(self, dve, b):
        for u in range(self.bt):
            at = bass.ds(b * self.bt + u, 1)
            dve.tensor_scalar(self.flat[:, u, :], self.src[:, at, :].rearrange("p a f -> p (a f)"),
                              self.scale[:, at], self.shift[:, at], ALU.mult, ALU.add).then_inc(self.normed, 1)

    def tensor(self, pe, b):
        for u in range(self.bt):
            pe.wait_ge(self.normed, b * self.bt + (u + 1))
            for c in (0, 1):
                at = (u % 2) * F + c * P
                pe.transpose(self.ps[u // 2][:, at:at + P], self.flat[:, u, c * P:(c + 1) * P],
                             self.k.ident[:, :]).then_inc(self.flipped, 1)
        pe.wait_ge(self.copied, b * self.bt + self.bt)

    def scalar(self, act, b, free=None):
        for u in range(self.bt):
            act.wait_ge(self.flipped, b * (2 * self.bt) + 2 * min(u | 1, self.bt - 1) + 2)
            if u == 0 and free is not None:
                free()
            act.copy(self.xt[:, :, u * P:(u + 1) * P],
                     self.ps[u // 2][:, (u % 2) * F:(u % 2) * F + F].rearrange("p (c n) -> p c n", c=2)
                     ).then_inc(self.copied, 1)


def project(k, name, src, blocks, bt, scale, shift, weight, cols, table=None, keep=None, att=None, side=None):
    nc = k.nc
    loaded, product, out_ok, saved, linked = (
        k.sem(f"{name}_{s}") for s in ("w_loaded", "product", "out", "saved", "link"))
    with k.scope():
        w = k.sb("w", [P, 2, cols])
        rows = k.sb("rows", [P, bt, cols])
        scaled = k.sb("scaled", [P, F])
        ps_x = [k.ps(f"ps_x{u}", [P, 512]) for u in range(4)]
        ps_w = [k.ps(f"ps_w{u}", [P, 512]) for u in range(4)]
        norm = Normed(k, name, src, bt, scale, shift, ps_x)
        with nc.Block() as block:

            @block.sync
            def _(sp):
                sp.dma_start(w[:, :, :], weight.rearrange("(a p) c -> p a c", p=P)).then_inc(loaded, 16)
                if table is not None:
                    out = table.rearrange("(b j p) f -> b p j f", p=P, j=bt)
                    with sp.Fori(0, blocks) as b:
                        hold(k, sp, out_ok, b * bt + bt)
                        sp.dma_start(out[bass.ds(b, 1), :, :, :].rearrange("a p j f -> p (a j) f"),
                                     rows[:, :, :]).then_inc(saved, 16)
                    sp.wait_ge(saved, blocks * 16)

            @block.vector
            def _(dve):
                link = Link(dve, linked)

                def body(b, last):
                    reached(dve, norm.flipped, b * (2 * bt))
                    norm.vector(dve, b)
                    if att is not None:
                        for u in range(bt):
                            dve.wait_ge(out_ok, b * bt + (u + 1))
                            link(dve.tensor_tensor(scaled[:, :], rows[:, u, :],
                                                   att[:, :, :].rearrange("p h c -> p (h c)"), ALU.mult))
                            link(dve.tensor_reduce(side[:, bass.ds(b * bt + u, 1), :].rearrange("p a h -> p (a h)"),
                                                   scaled[:, :].rearrange("p (h c) -> p h c", h=H0), AX.X, ALU.add))

                turns(dve, blocks, body, link, 0 if att is None else 2 * bt)

            @block.tensor
            def _(pe):
                pe.wait_ge(loaded, 16)

                def body(b, last):
                    norm.tensor(pe, b)
                    reached(pe, out_ok, b * bt)
                    for u in range(bt):
                        for c in (0, 1):
                            at = (u % 2) * F
                            ins = pe.matmul(ps_w[u // 2][:, at:at + cols], norm.xt[:, c, u * P:(u + 1) * P],
                                            w[:, c, :], start=c == 0, stop=c == 1)
                        ins.then_inc(product, 1)

                turns(pe, blocks, body)

            @block.scalar
            def _(act):

                def body(b, last):
                    norm.scalar(act, b)
                    if table is not None:
                        reached(act, saved, b * 16)
                    if att is not None:
                        reached(act, linked, b * (2 * bt))
                    for u in range(bt):
                        act.wait_ge(product, b * bt + (min(u | 1, bt - 1) + 1))
                        into = rows[:, u, :] if keep is None else (
                            keep[:, bass.ds(b * bt + u, 1), :].rearrange("p a c -> p (a c)"))
                        act.copy(into, ps_w[u // 2][:, (u % 2) * F:(u % 2) * F + cols]).then_inc(out_ok, 1)

                turns(act, blocks, body)


def mixture(k, name, scale, shift, gate, experts, hidden, func, layers, w_out, b_out, beside=None):
    nc = k.nc
    ct = hidden // P
    groups = 2 * ct * len(layers)
    wide = BT * P // 2
    names = ("w_loaded", "group", "evacuated", "y", "y_taken", "link")
    loaded, group_ok, evacuated, y_ok, y_taken, linked = (k.sem(f"{name}_{s}") for s in names)
    with k.scope():
        ws = [k.sb(f"w{n}", [P, experts, 2, hidden]) for n in range(len(layers))]
        wo = k.sb("wo", [P, experts, ct, F])
        bo = k.sb("bo", [P, experts, F])
        hid = [k.sb(f"hid{n}", [P, ct, BT * P]) for n in range(len(layers))]
        part = k.sb("part", [P, F])
        ps_h = [k.ps(f"ps_h{u}", [P, 512]) for u in range(4)]
        ps_y = [k.ps(f"ps_y{u}", [P, 512]) for u in range(4)]
        norm = Normed(k, name, k.X, BT, scale, shift, ps_h)
        with nc.Block() as block:

            @block.sync
            def _(sp):
                for w, (dram, _, _) in zip(ws, layers):
                    for e in range(experts):
                        sp.dma_start(w[:, e, :, :], dram[e, :, :].rearrange("(a p) h -> p a h", p=P)).then_inc(loaded, 16)
                for e in range(experts):
                    sp.dma_start(wo[:, e, :, :], w_out[e, :, :].rearrange("(a p) f -> p a f", p=P)).then_inc(loaded, 16)
                sp.dma_start(bo[:, :, :], b_out.partition_broadcast(P)).then_inc(loaded, 16)

            loads = (len(layers) * experts + experts + 1) * 16

            @block.tensor
            def _(pe):
                pe.wait_ge(loaded, loads)
                with pe.Fori(0, NB) as b:
                    pe.wait_ge(evacuated, b * (experts * groups) + 4)
                    norm.tensor(pe, b)
                    for e in range(experts):
                        for n, w in enumerate(ws):
                            src, kt = (norm.xt, 2) if n == 0 else (hid[n - 1], ct)
                            for half in (0, 1):
                                for c in range(ct):
                                    g = e * groups + n * 2 * ct + half * ct + c
                                    if n and c == 0:
                                        pe.wait_ge(evacuated, b * (experts * groups) + (g - 2 * ct + ct + 4))
                                    pe.wait_ge(evacuated, b * (experts * groups) + (g + 1))
                                    for a in range(kt):
                                        ins = pe.matmul(ps_h[g % 4][:, 0:wide], w[:, e, a, c * P:(c + 1) * P],
                                                        src[:, a, half * wide:(half + 1) * wide],
                                                        start=a == 0, stop=a == kt - 1)
                                    ins.then_inc(group_ok, 1)
                        pe.wait_ge(evacuated, b * (experts * groups) + ((e + 1) * groups + 4))
                        for u in range(BT):
                            m = e * BT + u
                            pe.wait_ge(y_taken, b * (experts * BT) + (m + 1))
                            for a in range(ct):
                                ins = pe.matmul(ps_y[m % 4][:, 0:F], hid[-1][:, a, u * P:(u + 1) * P],
                                                wo[:, e, a, :], start=a == 0, stop=a == ct - 1)
                            ins.then_inc(y_ok, 1)

            @block.scalar
            def _(act):
                act.sem_inc(evacuated, 4)
                with act.Fori(0, NB) as b:
                    norm.scalar(act, b)
                    for e in range(experts):
                        for n, (_, s, t) in enumerate(layers):
                            for half in (0, 1):
                                for c in range(ct):
                                    g = e * groups + n * 2 * ct + half * ct + c
                                    act.wait_ge(group_ok, b * (experts * groups) + (g + 1))
                                    act.activation(
                                        hid[n][:, c, half * wide:(half + 1) * wide], ps_h[g % 4][:, 0:wide], func,
                                        bias=t[:, e, c:c + 1],
                                        scale=1.0 if s is None else s[:, e, c:c + 1]).then_inc(evacuated, 1)

            @block.vector
            def _(dve):
                link = Link(dve, linked)
                dve.sem_inc(y_taken, 4)
                dve.wait_ge(loaded, loads)
                with dve.Fori(0, NB) as b:
                    norm.vector(dve, b)
                    link.loop(b, experts * BT)
                    for e in range(experts):
                        for u in range(BT):
                            m = e * BT + u
                            at = bass.ds(b * BT + u, 1)
                            x = k.X[:, at, :].rearrange("p a f -> p (a f)")
                            dve.wait_ge(y_ok, b * (experts * BT) + (m + 1))
                            dve.tensor_tensor(part[:, :], ps_y[m % 4][:, 0:F], bo[:, e, :], ALU.add).then_inc(y_taken, 1)
                            dve.wait_ge(y_taken, b * (experts * BT) + (m + 1 + 4))
                            link(dve.scalar_tensor_tensor(
                                x, part[:, :], gate[:, at, e:e + 1].rearrange("p a e -> p (a e)"), x,
                                ALU.mult, ALU.add))
                link.end(NB)

            if beside is not None:

                @block.gpsimd
                def _(pool):
                    beside(pool)


def vector_only(k, name, body):
    linked = k.sem(f"{name}_link")
    with k.nc.Block() as block:

        @block.vector
        def _(dve):
            body(dve, Link(dve, linked))


def load_all(k, name, pairs, store=False):
    done = k.sem(f"{name}_done")
    with k.nc.Block() as block:

        @block.sync
        def _(sp):
            for to, src in pairs:
                sp.dma_start(to, src).then_inc(done, 16)
            sp.wait_ge(done, 16 * len(pairs))


def flat2(ap):
    return ap.rearrange("p a b -> p (a b)")


def graph_network(nc, x, src, dst, edge_weight, attr, w_gnn, att, wr, br, w1, b1, g1, be1, m1, v1, w2, b2, g2, be2,
                  m2, v2, wo, bo, weight, bias, w_gat, att_src, att_dst, b_gat, ln_gamma, ln_beta, u1, c1, u2, c2,
                  edge_index, out, stop=None):
    stack = ExitStack()
    with stack:
        k = Core(nc, stack)
        k.held = stack.enter_context(nc.semaphore("held"))
        k.X = k.sb("X", [P, NJ, F])
        k.iota = k.sb("iota", [P, P])
        k.ident = k.sb("ident", [P, P])
        k.ones = k.sb("ones", [P, P])
        k.before = k.sb("before", [P, P])
        k.ident16 = k.sb("ident16", [P, P], BF16)
        k.far = k.sb("far", [P, 4, P], BF16)
        k.pick = k.sb("pick", [96, 32], BF16)
        scale = k.sb("scale", [P, NJ])
        shift = k.sb("shift", [P, NJ])
        tile_src = k.sb("tile_src", [1, S_SRC], I32)
        tile_dst = k.sb("tile_dst", [1, S_DST], I32)
        tile_gat = k.sb("tile_gat", [1, S_GAT], I32)

        REC_SRC, REC_DST, REC_GAT = 5, H0 + 3, 2
        by_src = k.dram("by_src", (P * S_SRC, REC_SRC))
        by_dst = k.dram("by_dst", (P * S_DST, REC_DST))
        by_gat = k.dram("by_gat", (P * S_GAT, REC_GAT))
        hyper_a = k.dram("hyper_a", (MJ * P, H0))
        node_h = k.dram("node_h", (NJ * P, F))
        hyper_out = k.dram("hyper_out", (MJ * P, F))
        gat_table = k.dram("gat_table", (NJ * P, H1 * C1 + H1))

        load_nodes(k, x)

        GC = EG // P
        plan_slot = k.dram("plan_slot", (P, GC), I32)
        plan_fields = k.dram("plan_fields", (P, GC, REC_GAT))
        fill_rows(k, "blank", [(by_src, -1.0), (by_gat, -1.0), (by_dst, 0.0)])

        EP, EC = 125, E // 125
        with k.scope():
            slot_src = k.sb("slot_src", [EP, EC], I32)
            slot_dst = k.sb("slot_dst", [EP, EC], I32)
            slot_gat = k.sb("slot_gat", [P, GC], I32)
            rank_edges(k, "rank_src", src, EP, EC, NJ, S_SRC, slot_src, tile_src)
            rank_edges(k, "rank_dst", dst, EP, EC, MJ, S_DST, slot_dst, tile_dst)
            low_bits = k.sb("low_bits", [EP, EC], I32)
            fields = k.sb("fields", [EP, EC, REC_SRC])
            weights = k.sb("weights", [EP, EC])
            src_i = k.sb("src_i", [EP, EC], I32)
            dst_i = k.sb("dst_i", [EP, EC], I32)
            load_all(k, "edge_loads", [(t[:, :], d.rearrange("(p c) -> p c", p=EP))
                                       for t, d in ((src_i, src), (dst_i, dst), (weights, edge_weight))])

            def edge_fields(dve, link):
                link(dve.tensor_scalar(low_bits[:, :], src_i[:, :], P - 1, None, ALU.bitwise_and))
                for n, t in enumerate((low_bits, src_i, dst_i, weights, slot_dst)):
                    ins = dve.tensor_copy(fields[:, :, n], t[:, :])
                link(ins)

            vector_only(k, "edge_fields", edge_fields)
            to_src = Scatter(k, "to_src", EP, 25, REC_SRC, by_src)
            ranks = Ranks(k, "rank_gat", edge_index[1, :], P, GC, NJ, S_GAT, slot_gat, tile_gat)
            with nc.Block() as block:

                @block.sync
                def _(sp):
                    ranks.sync(sp)

                @block.gpsimd
                def _(pool):
                    ranks.gpsimd(pool)
                    to_src.all(pool, [(0, REC_SRC, fields)], slot_src, EC // 50)

                @block.vector
                def _(dve):
                    ranks.vector(dve)

                @block.tensor
                def _(pe):
                    ranks.tensor(pe)

            g_src = k.sb("g_src", [P, GC], I32)
            g_dst = k.sb("g_dst", [P, GC], I32)
            g_fields = k.sb("g_fields", [P, GC, REC_GAT])
            load_all(k, "gat_loads", [(g_src[:, :], edge_index[0, :].rearrange("(p c) -> p c", p=P)),
                                      (g_dst[:, :], edge_index[1, :].rearrange("(p c) -> p c", p=P))])

            def gat_fields(dve, link):
                link(dve.tensor_scalar(g_dst[:, :], g_dst[:, :], P - 1, None, ALU.bitwise_and))
                dve.tensor_copy(g_fields[:, :, 0], g_dst[:, :])
                link(dve.tensor_copy(g_fields[:, :, 1], g_src[:, :]))

            vector_only(k, "gat_fields", gat_fields)
            load_all(k, "plan_store", [(plan_slot, slot_gat[:, :]), (plan_fields, g_fields[:, :, :])])
        k.recycle()

        with k.scope():
            local = k.sb("local", [P, S_SRC])
            to_dst = k.sb("to_dst", [P, S_SRC], I32)
            ew = k.sb("ew", [P, S_SRC])
            degree_part = k.sb("degree_part", [P, NJ, H0])
            with k.scope():
                prob = k.sb("prob", [P, S_SRC, H0])
                to_hyper = k.sb("to_hyper", [P, S_SRC], I32)
                with k.scope():
                    src_f = k.sb("src_f", [P, S_SRC])
                    hyper_local = k.sb("hyper_local", [P, S_SRC])
                    hyper_slot = k.sb("hyper_slot", [P, S_SRC], I32)
                    present = k.sb("present", [P, S_SRC])
                    with k.scope():
                        rec = k.sb("rec", [P, S_SRC, REC_SRC])
                        low_i = k.sb("low_i", [P, S_SRC], I32)
                        dst_f = k.sb("dst_f", [P, S_SRC])
                        load_all(k, "by_src_load", [(rec[:, :, :], by_src.rearrange("(p s) w -> p s w", p=P))])

                        def unpack(dve, link):
                            link(dve.tensor_copy(local[:, :], rec[:, :, 0]))
                            link(dve.tensor_scalar(src_f[:, :], rec[:, :, 1], 0.0, None, ALU.max))
                            link(dve.tensor_scalar(dst_f[:, :], rec[:, :, 2], 0.0, None, ALU.max))
                            link(dve.tensor_copy(to_dst[:, :], dst_f[:, :]))
                            link(dve.tensor_scalar(low_i[:, :], to_dst[:, :], P - 1, None, ALU.bitwise_and))
                            link(dve.tensor_copy(hyper_local[:, :], low_i[:, :]))
                            link(dve.tensor_scalar(dst_f[:, :], dst_f[:, :], float(M - 1), None, ALU.min))
                            link(dve.tensor_copy(to_hyper[:, :], dst_f[:, :]))
                            link(dve.tensor_copy(ew[:, :], rec[:, :, 3]))
                            link(dve.tensor_scalar(dst_f[:, :], rec[:, :, 4], 0.0, NOWHERE, ALU.is_lt, ALU.mult))
                            link(dve.scalar_tensor_tensor(dst_f[:, :], rec[:, :, 4], 0.0, dst_f[:, :], ALU.max, ALU.add))
                            link(dve.tensor_copy(hyper_slot[:, :], dst_f[:, :]))
                            link(dve.memset(present[:, :], 1.0))

                        vector_only(k, "unpack", unpack)

                    with k.scope():
                        node_a = k.sb("node_a", [P, NJ, H0])
                        top = k.sb("top", [P, NJ, H0])
                        node = k.sb("node", [P, NJ, 2 * H0])
                        total = k.sb("total", [P, NJ, H0 + 1])
                        inv = k.sb("inv", [P, NJ, H0])
                        norm_scales(k, "norm0", scale, shift)
                        with k.scope():
                            atts = k.sb("atts", [P, H0, 2 * C0])
                            half_att = [k.sb(f"att{n}", [P, H0, C0]) for n in (0, 1)]
                            hyper = k.sb("hyper", [P, MJ, F])
                            hyper_side = k.sb("hyper_side", [P, MJ, H0])
                            plain = k.sb("plain", [P, 2, MJ])
                            full = (MJ - 1) * P

                            def clear(dve, link):
                                link(dve.memset(hyper[:, :, :], 0.0))
                                link(dve.memset(plain[:, 0, :], 1.0))
                                link(dve.memset(plain[:, 1, :], 0.0))

                            vector_only(k, "hyper_clear", clear)
                            load_all(k, "hyper_loads", [
                                (atts[:, :, :], att[0, :, :].partition_broadcast(P)),
                                (hyper[:, 0:MJ - 1, :], tile_rows(attr[0:full, :])),
                                (hyper[0:M - full, MJ - 1, :], attr[full:M, :])])

                            def split_att(dve, link):
                                for n in (0, 1):
                                    link(dve.tensor_copy(half_att[n][:, :, :], atts[:, :, n * C0:(n + 1) * C0]))

                            vector_only(k, "split_att", split_att)
                            project(k, "node0", k.X, NB, BT, scale, shift, w_gnn, F, table=node_h, att=half_att[0],
                                    side=node_a)
                            hyper_h = k.dram("hyper_h", (MJ * P, F))
                            project(k, "hyper0", hyper, 2, MJ // 2, plain[:, 0, :], plain[:, 1, :], w_gnn, F,
                                    table=hyper_h, att=half_att[1], side=hyper_side)
                            load_all(k, "hyper_a", [(tile_rows(hyper_a), hyper_side[:, :, :])])

                        vector_only(k, "top0_clear", lambda dve, link: (
                            link(dve.memset(top[:, :, :], -3e38)), link(dve.memset(total[:, :, :], 0.0))))
                        segment_max(k, "max0", S_SRC, H0, H0, hyper_a, to_hyper, local, tile_src, prob, top)

                        def node_side0(dve, link):
                            link(dve.tensor_tensor(top[:, :, :], top[:, :, :], node_a[:, :, :], ALU.add))
                            link(dve.scalar_tensor_tensor(node[:, :, 0:H0], top[:, :, :], 0.2, top[:, :, :],
                                                          ALU.mult, ALU.max))
                            link(dve.tensor_copy(node[:, :, H0:2 * H0], node_a[:, :, :]))

                        vector_only(k, "node_side0", node_side0)
                        with k.scope():
                            to_dst_order = Scatter(k, "to_dst_order", P, HALF, REC_DST, by_dst)

                            def scatter(pool, kept):
                                def body(i, last):
                                    for h in (0, 1):
                                        to_dst_order.turn(
                                            pool, i, h,
                                            [(0, H0, prob), (H0, 1, src_f[:, :].unsqueeze(2)),
                                             (H0 + 1, 1, hyper_local[:, :].unsqueeze(2)),
                                             (H0 + 2, 1, present[:, :].unsqueeze(2))], hyper_slot,
                                            before=lambda: pool.wait_ge(kept, i * 2 + (h + 1)))

                                turns(pool, S_SRC // BODY, body)
                                to_dst_order.finish(pool, S_SRC // BODY)

                            segment_softmax(k, "soft0", S_SRC, H0, local, tile_src, node, prob, H0 + 1, None, total,
                                            scatter)

                        def inverses0(dve, link):
                            link(dve.tensor_scalar(inv[:, :, :], total[:, :, 0:H0], 1e-16, None, ALU.add))
                            link(dve.reciprocal(inv[:, :, :], inv[:, :, :]))
                            link(dve.tensor_scalar(total[:, :, H0], total[:, :, H0], 1.0, None, ALU.max))
                            link(dve.reciprocal(total[:, :, H0], total[:, :, H0]))
                            link(dve.tensor_tensor(degree_part[:, :, :], inv[:, :, :],
                                                   total[:, :, H0:H0 + 1].to_broadcast([P, NJ, H0]), ALU.mult))

                        vector_only(k, "inverses0", inverses0)
                        scale_rows(k, "scale_h", node_h, inv)

                with k.scope():
                    rec_d = k.sb("rec_d", [P, S_DST, REC_DST])
                    from_src = k.sb("from_src", [P, S_DST], I32)
                    local_d = k.sb("local_d", [P, S_DST])
                    sums = k.sb("sums", [P, MJ, F + 1])
                    load_all(k, "by_dst_load", [(rec_d[:, :, :], by_dst.rearrange("(p s) w -> p s w", p=P))])

                    def unpack_d(dve, link):
                        link(dve.tensor_copy(from_src[:, :], rec_d[:, :, H0]))
                        link(dve.tensor_copy(local_d[:, :], rec_d[:, :, H0 + 1]))
                        link(dve.memset(sums[:, :, :], 0.0))

                    vector_only(k, "unpack_d", unpack_d)
                    segment_sum(k, "hyper_sum", S_DST, node_h, from_src, local_d, tile_dst, sums, width=F + 1,
                                probs=rec_d[:, :, 0:H0], count=rec_d[:, :, H0 + 2])

                    def mean_d(dve, link):
                        link(dve.tensor_scalar(sums[:, :, F], sums[:, :, F], 1.0, None, ALU.max))
                        link(dve.reciprocal(sums[:, :, F], sums[:, :, F]))
                        link(dve.tensor_tensor(sums[:, :, 0:F], sums[:, :, 0:F],
                                               sums[:, :, F:F + 1].to_broadcast([P, MJ, F]), ALU.mult))

                    vector_only(k, "mean_d", mean_d)
                    load_all(k, "hyper_out", [(tile_rows(hyper_out), sums[:, :, 0:F])])

                with k.scope():
                    acc = k.sb("acc", [P, NJ, F])
                    vector_only(k, "acc0_clear", lambda dve, link: link(dve.memset(acc[:, :, :], 0.0)))
                    segment_sum(k, "node_sum", S_SRC, hyper_out, to_hyper, local, tile_src, acc, probs=prob[:, :, :])

                    def add0(dve, link):
                        for j in range(NJ):
                            x_heads = acc[:, j, :].rearrange("p (h c) -> p h c", h=H0)
                            ins = dve.tensor_tensor(x_heads, x_heads,
                                                    degree_part[:, j, :].unsqueeze(2).to_broadcast([P, H0, C0]), ALU.mult)
                        link(ins)
                        link(dve.tensor_tensor(flat2(k.X[:, :, :]), flat2(k.X[:, :, :]), flat2(acc[:, :, :]), ALU.add))

                    vector_only(k, "add0", add0)

            if stop == "gnn0":
                return store_nodes(k, out)

            k.recycle()
            norm_scales(k, "norm1", scale, shift)
            with k.scope():
                gate = k.sb("gate", [P, NJ, EX0])
                project(k, "logits0", k.X, NB, BT, scale, shift, wr, EX0, keep=gate)
                softmax_gate(k, gate, br)
                bn = [batch_norm(k, f"bn{n}", *a) for n, a in enumerate(((b1, g1, be1, m1, v1), (b2, g2, be2, m2, v2)))]
                slot_gat = k.sb("slot_gat", [P, GC], I32)
                g_fields = k.sb("g_fields", [P, GC, REC_GAT])
                load_all(k, "plan_load", [(slot_gat[:, :], plan_slot), (g_fields[:, :, :], plan_fields)])
                to_gat = Scatter(k, "to_gat", P, 16, REC_GAT, by_gat)
                mixture(k, "ffn0", scale, shift, gate, EX0, HID0, ACT.Relu, [(w1, *bn[0]), (w2, *bn[1])], wo, bo,
                        beside=lambda pool: to_gat.all(pool, [(0, REC_GAT, g_fields)], slot_gat, GC // 32))
            if stop == "ffn0":
                return store_nodes(k, out)

            norm_scales(k, "norm2", scale, shift)
            project(k, "node1", k.X, NB, BT, scale, shift, weight, F, table=node_h)
            with k.scope():
                acc = k.sb("acc1", [P, NJ, F])
                bias_b = k.sb("bias_b", [P, F])
                vector_only(k, "acc1_clear", lambda dve, link: link(dve.memset(acc[:, :, :], 0.0)))
                load_all(k, "bias_load", [(bias_b[:, :], bias.partition_broadcast(P))])
                segment_sum(k, "edge_sum", S_SRC, node_h, to_dst, local, tile_src, acc, edge_weight=ew)

                def add1(dve, link):
                    link(dve.tensor_tensor(flat2(k.X[:, :, :]), flat2(k.X[:, :, :]), flat2(acc[:, :, :]), ALU.add))
                    link(dve.tensor_tensor(k.X[:, :, :], k.X[:, :, :],
                                           bias_b[:, :].unsqueeze(1).to_broadcast([P, NJ, F]), ALU.add))

                vector_only(k, "add1", add1)
        if stop == "gnn1":
            return store_nodes(k, out)

        k.recycle()
        norm_scales(k, "norm3", scale, shift)
        gate1 = k.sb("gate1", [P, NJ, EX1])
        HC = H1 * C1
        with k.scope():
            g_local = k.sb("g_local", [P, S_GAT])
            g_from = k.sb("g_from", [P, S_GAT], I32)
            with k.scope():
                rec_g = k.sb("rec_g", [P, S_GAT, REC_GAT])
                from_f = k.sb("from_f", [P, S_GAT])
                load_all(k, "by_gat_load", [(rec_g[:, :, :], by_gat.rearrange("(p s) w -> p s w", p=P))])

                def unpack_g(dve, link):
                    link(dve.tensor_copy(g_local[:, :], rec_g[:, :, 0]))
                    link(dve.tensor_scalar(from_f[:, :], rec_g[:, :, 1], 0.0, float(N - 1), ALU.max, ALU.min))
                    link(dve.tensor_copy(g_from[:, :], from_f[:, :]))

                vector_only(k, "unpack_g", unpack_g)
            h_node = k.sb("h_node", [P, NJ, HC])
            project(k, "gat_h", k.X, NB, BT, scale, shift, w_gat, HC, keep=h_node)
            attention_gates(k, h_node, gate1, gat_table, g_local, g_from, tile_gat, att_src, att_dst, b_gat,
                            ln_gamma, ln_beta)
        if stop == "gates":
            return store_nodes(k, out, gate1)

        with k.scope():
            c1_t = k.sb("c1_t", [P, EX1, HID1 // P])
            by_channel(k, "c1_load", [c1], flat2(c1_t[:, :, :]))
            mixture(k, "ffn1", scale, shift, gate1, EX1, HID1, ACT.Gelu, [(u1, None, c1_t)], u2, c2)
        store_nodes(k, out)


def store_nodes(k, out, gates=None):
    full = (NJ - 1) * P
    load_all(k, "store", [(tile_rows(out[0:full, :]), k.X[:, 0:NJ - 1, :]),
                          (out[full:N, :], k.X[0:N - full, NJ - 1, :])])
    if gates is not None:
        load_all(k, "store_g", [(tile_rows(out[0:full, 0:EX1]), gates[:, 0:NJ - 1, :])])


def scale_rows(k, name, table, by):
    nc = k.nc
    loaded, scaled, stored = (k.sem(f"{name}_{s}") for s in ("loaded", "scaled", "stored"))
    with k.scope():
        rows = k.sb("rows", [P, BT, F])
        blocks = table.rearrange("(b j p) f -> b p j f", p=P, j=BT)
        with nc.Block() as block:

            @block.sync
            def _(sp):
                with sp.Fori(0, NB) as b:
                    now = blocks[bass.ds(b, 1), :, :, :].rearrange("a p j f -> p (a j) f")
                    sp.dma_start(rows[:, :, :], now).then_inc(loaded, 16)
                    hold(k, sp, scaled, b * BT + BT)
                    sp.dma_start(now, rows[:, :, :]).then_inc(stored, 16)
                    hold(k, sp, stored, b * 16 + 16)

            @block.vector
            def _(dve):
                with dve.Fori(0, NB) as b:
                    dve.wait_ge(loaded, b * 16 + 16)
                    for u in range(BT):
                        heads = rows[:, u, :].rearrange("p (h c) -> p h c", h=H0)
                        weight = by[:, bass.ds(b * BT + u, 1), :].rearrange("p a h -> p (a h)")
                        dve.tensor_tensor(heads, heads, weight.unsqueeze(2).to_broadcast([P, H0, C0]),
                                          ALU.mult).then_inc(scaled, 1)


def softmax_gate(k, gate, br):
    shifted, exped, linked = k.sem("gate_shifted"), k.sem("gate_exp"), k.sem("gate_link")
    with k.scope():
        br_b = k.sb("br_b", [P, EX0])
        most = k.sb("most", [P, NJ])
        load_all(k, "br_load", [(br_b[:, :], br.partition_broadcast(P))])
        with k.nc.Block() as block:

            @block.vector
            def _(dve):
                link = Link(dve, linked)
                link(dve.tensor_tensor(gate[:, :, :], gate[:, :, :], br_b[:, :].unsqueeze(1).to_broadcast([P, NJ, EX0]),
                                       ALU.add))
                link(dve.tensor_reduce(most[:, :], gate[:, :, :], AX.X, ALU.max))
                dve.tensor_tensor(gate[:, :, :], gate[:, :, :], most[:, :].unsqueeze(2).to_broadcast([P, NJ, EX0]),
                                  ALU.subtract).then_inc(shifted, 1)
                dve.wait_ge(exped, 1)
                link(dve.tensor_reduce(most[:, :], gate[:, :, :], AX.X, ALU.add))
                link(dve.reciprocal(most[:, :], most[:, :]))
                link(dve.tensor_tensor(gate[:, :, :], gate[:, :, :], most[:, :].unsqueeze(2).to_broadcast([P, NJ, EX0]),
                                       ALU.mult))

            @block.scalar
            def _(act):
                act.wait_ge(shifted, 1)
                act.activation(gate[:, :, :], gate[:, :, :], ACT.Exp).then_inc(exped, 1)


def by_channel(k, name, arrays, out):
    nc = k.nc
    loaded, flipped, copied = (k.sem(f"{name}_{s}") for s in ("loaded", "flipped", "copied"))
    experts, channels = arrays[0].shape
    each = experts * channels // P
    rows = each * len(arrays)
    with k.scope():
        lines = k.sb("lines", [rows, P])
        ps = k.ps("ps_lines", [P, 512])
        with nc.Block() as block:

            @block.sync
            def _(sp):
                for n, a in enumerate(arrays):
                    sp.dma_start(lines[n * each:(n + 1) * each, :], a.rearrange("e (c p) -> (e c) p", p=P)).then_inc(loaded, 16)

            @block.tensor
            def _(pe):
                pe.wait_ge(loaded, 16 * len(arrays))
                pe.transpose(ps[:, 0:rows], lines[:, :], k.ident[0:rows, 0:rows]).then_inc(flipped, 1)

            @block.scalar
            def _(act):
                act.wait_ge(flipped, 1)
                act.copy(out, ps[:, 0:rows]).then_inc(copied, 1)


def batch_norm(k, name, b, g, be, m, v):
    ct = HID0 // P
    every = k.sb(f"{name}_params", [P, 5, EX0, ct])
    t = {n: every[:, i, :, :] for i, n in enumerate(("b", "g", "be", "m", "v"))}
    ready, rooted, linked = k.sem(f"{name}_ready"), k.sem(f"{name}_root"), k.sem(f"{name}_link")
    by_channel(k, f"{name}_load", [b, g, be, m, v], every[:, :, :, :].rearrange("p n e c -> p (n e c)"))
    with k.nc.Block() as block:

        @block.vector
        def _(dve):
            link = Link(dve, linked)
            dve.tensor_scalar(t["v"][:, :, :], t["v"][:, :, :], BN_EPS, None, ALU.add).then_inc(ready, 1)
            dve.wait_ge(rooted, 1)
            link(dve.reciprocal(t["v"][:, :, :], t["v"][:, :, :]))
            link(dve.tensor_tensor(t["g"][:, :, :], t["g"][:, :, :], t["v"][:, :, :], ALU.mult))
            link(dve.tensor_tensor(t["b"][:, :, :], t["b"][:, :, :], t["m"][:, :, :], ALU.subtract))
            link(dve.tensor_tensor(t["b"][:, :, :], t["b"][:, :, :], t["g"][:, :, :], ALU.mult))
            link(dve.tensor_tensor(t["b"][:, :, :], t["b"][:, :, :], t["be"][:, :, :], ALU.add))

        @block.scalar
        def _(act):
            act.wait_ge(ready, 1)
            act.activation(t["v"][:, :, :], t["v"][:, :, :], ACT.Sqrt).then_inc(rooted, 1)

    return t["g"], t["b"]


def attention_gates(k, h_node, gate, gat_table, g_local, g_from, tile_gat, att_src, att_dst, b_gat, ln_gamma, ln_beta):
    nc = k.nc
    HC = H1 * C1
    ROW = H1 + HC
    with k.scope():
        value = k.sb("value", [P, S_GAT, ROW])
        row = k.sb("row", [P, NJ, ROW])
        prod = k.sb("prod", [P, NJ, HC])
        a_dst = k.sb("a_dst", [P, NJ, H1])
        top = k.sb("top", [P, NJ, H1])
        own = k.sb("own", [P, NJ, H1])
        node = k.sb("node", [P, NJ, 2 * H1])
        total = k.sb("total", [P, NJ, ROW])
        small = {n: k.sb(n, [P, HC]) for n in ("s_src", "s_dst", "s_bias", "s_gamma", "s_beta")}
        load_all(k, "gat_params", [
            (small["s_src"][:, :], att_src.rearrange("h c -> (h c)").partition_broadcast(P)),
            (small["s_dst"][:, :], att_dst.rearrange("h c -> (h c)").partition_broadcast(P)),
            (small["s_bias"][:, :], b_gat.partition_broadcast(P)),
            (small["s_gamma"][:, :], ln_gamma.partition_broadcast(P)),
            (small["s_beta"][:, :], ln_beta.partition_broadcast(P))])

        def wide(t):
            return t[:, :].unsqueeze(1).to_broadcast([P, NJ, HC])

        def heads(t):
            return t.rearrange("p j (h c) -> p (j h) c", h=H1)

        def per_head(t):
            return t.rearrange("p j h -> p (j h)").unsqueeze(2).to_broadcast([P, NJ * H1, C1])

        def sides(dve, link):
            link(dve.tensor_tensor(prod[:, :, :], h_node[:, :, :], wide(small["s_dst"]), ALU.mult))
            link(dve.tensor_reduce(flat2(a_dst[:, :, :]), heads(prod[:, :, :]), AX.X, ALU.add))
            link(dve.tensor_tensor(prod[:, :, :], h_node[:, :, :], wide(small["s_src"]), ALU.mult))
            link(dve.tensor_reduce(flat2(own[:, :, :]), heads(prod[:, :, :]), AX.X, ALU.add))
            link(dve.tensor_copy(row[:, :, 0:H1], own[:, :, :]))
            link(dve.tensor_copy(row[:, :, H1:ROW], h_node[:, :, :]))

        vector_only(k, "gat_sides", sides)
        load_all(k, "gat_rows", [(tile_rows(gat_table), row[:, :, :])])
        vector_only(k, "gat_first_top", lambda dve, link: link(dve.tensor_copy(top[:, :, :], own[:, :, :])))
        segment_max(k, "max1", S_GAT, H1, ROW, gat_table, g_from, g_local, tile_gat, value, top)

        shifted, exped, linked = k.sem("own_shifted"), k.sem("own_exp"), k.sem("own_link")
        with nc.Block() as block:

            @block.vector
            def _(dve):
                link = Link(dve, linked)
                link(dve.tensor_tensor(top[:, :, :], top[:, :, :], a_dst[:, :, :], ALU.add))
                link(dve.scalar_tensor_tensor(node[:, :, 0:H1], top[:, :, :], 0.2, top[:, :, :], ALU.mult, ALU.max))
                link(dve.tensor_copy(node[:, :, H1:2 * H1], a_dst[:, :, :]))
                link(dve.tensor_tensor(own[:, :, :], own[:, :, :], a_dst[:, :, :], ALU.add))
                link(dve.scalar_tensor_tensor(own[:, :, :], own[:, :, :], 0.2, own[:, :, :], ALU.mult, ALU.max))
                link(dve.tensor_tensor(own[:, :, :], own[:, :, :], node[:, :, 0:H1], ALU.subtract))
                dve.tensor_scalar(own[:, :, :], own[:, :, :], 0.0, None, ALU.min).then_inc(shifted, 1)
                dve.wait_ge(exped, 1)
                link(dve.tensor_copy(total[:, :, 0:H1], own[:, :, :]))
                link(dve.tensor_tensor(heads(prod[:, :, :]), heads(h_node[:, :, :]), per_head(own[:, :, :]), ALU.mult))
                link(dve.tensor_copy(total[:, :, H1:ROW], prod[:, :, :]))

            @block.scalar
            def _(act):
                act.wait_ge(shifted, 1)
                act.activation(own[:, :, :], own[:, :, :], ACT.Exp).then_inc(exped, 1)

        def message(dve, msg, at):
            return dve.tensor_tensor(
                msg[:, :, H1:ROW].rearrange("p u (h c) -> p u h c", h=H1),
                value[:, at, H1:ROW].rearrange("p u (h c) -> p u h c", h=H1),
                msg[:, :, 0:H1].unsqueeze(3).to_broadcast([P, HALF, H1, C1]), ALU.mult)

        segment_softmax(k, "soft1", S_GAT, H1, g_local, tile_gat, node, value, ROW, message, total)

        mean = k.sb("mean", [P, NJ])
        var = k.sb("var", [P, NJ])
        agg = k.sb("agg", [P, NJ, HC])
        scores = k.sb("scores", [P, NJ, EX1])
        picked = [k.sb(f"picked{n}", [P, NJ, EX1]) for n in (0, 1)]
        best = [k.sb(f"best{n}", [P, NJ]) for n in (0, 1)]
        taken = k.sb("taken", [P, NJ])
        free = k.sb("free", [P, NJ])
        ready, rooted, shifted2, exped2, linked2 = (k.sem(f"gates_{s}") for s in
                                                    ("var", "root", "shifted", "exp", "link"))
        with nc.Block() as block:

            @block.vector
            def _(dve):
                link = Link(dve, linked2)

                def each(t):
                    return t[:, :].unsqueeze(2).to_broadcast([P, NJ, HC])

                link(dve.tensor_scalar(own[:, :, :], total[:, :, 0:H1], 1e-16, None, ALU.add))
                link(dve.reciprocal(own[:, :, :], own[:, :, :]))
                link(dve.tensor_copy(agg[:, :, :], total[:, :, H1:ROW]))
                link(dve.tensor_tensor(heads(agg[:, :, :]), heads(agg[:, :, :]), per_head(own[:, :, :]), ALU.mult))
                link(dve.tensor_tensor(agg[:, :, :], agg[:, :, :], wide(small["s_bias"]), ALU.add))
                link(dve.tensor_reduce(mean[:, :], agg[:, :, :], AX.X, ALU.add))
                link(dve.tensor_scalar(mean[:, :], mean[:, :], 1.0 / HC, None, ALU.mult))
                link(dve.tensor_tensor(agg[:, :, :], agg[:, :, :], each(mean), ALU.subtract))
                link(dve.tensor_tensor(prod[:, :, :], agg[:, :, :], agg[:, :, :], ALU.mult))
                link(dve.tensor_reduce(var[:, :], prod[:, :, :], AX.X, ALU.add))
                dve.tensor_scalar(var[:, :], var[:, :], 1.0 / HC, LN_EPS, ALU.mult, ALU.add).then_inc(ready, 1)
                dve.wait_ge(rooted, 1)
                link(dve.reciprocal(var[:, :], var[:, :]))
                link(dve.tensor_tensor(agg[:, :, :], agg[:, :, :], each(var), ALU.mult))
                link(dve.tensor_tensor(agg[:, :, :], agg[:, :, :], wide(small["s_gamma"]), ALU.mult))
                link(dve.tensor_tensor(agg[:, :, :], agg[:, :, :], wide(small["s_beta"]), ALU.add))
                link(dve.tensor_reduce(scores[:, :, :], agg[:, :, :].rearrange("p j (h c) -> p j c h", h=H1),
                                       AX.X, ALU.add))
                link(dve.tensor_scalar(scores[:, :, :], scores[:, :, :], 1.0 / H1, None, ALU.mult))
                for n in (0, 1):
                    link(dve.tensor_reduce(best[n][:, :], scores[:, :, :], AX.X, ALU.max))
                    link(dve.memset(taken[:, :], 0.0))
                    for e in range(EX1):
                        link(dve.tensor_tensor(picked[n][:, :, e], scores[:, :, e], best[n][:, :], ALU.is_equal))
                        link(dve.tensor_scalar(free[:, :], taken[:, :], -1.0, 1.0, ALU.mult, ALU.add))
                        link(dve.tensor_tensor(picked[n][:, :, e], picked[n][:, :, e], free[:, :], ALU.mult))
                        link(dve.tensor_tensor(taken[:, :], taken[:, :], picked[n][:, :, e], ALU.add))
                    if n == 0:
                        link(dve.scalar_tensor_tensor(scores[:, :, :], picked[0][:, :, :], -3e38, scores[:, :, :],
                                                      ALU.mult, ALU.add))
                dve.tensor_tensor(best[1][:, :], best[1][:, :], best[0][:, :], ALU.subtract).then_inc(shifted2, 1)
                dve.wait_ge(exped2, 1)
                link(dve.tensor_scalar(best[0][:, :], best[1][:, :], 1.0, None, ALU.add))
                link(dve.reciprocal(best[0][:, :], best[0][:, :]))
                link(dve.tensor_tensor(best[1][:, :], best[1][:, :], best[0][:, :], ALU.mult))
                for n in (0, 1):
                    link(dve.tensor_tensor(picked[n][:, :, :], picked[n][:, :, :],
                                           best[n][:, :].unsqueeze(2).to_broadcast([P, NJ, EX1]), ALU.mult))
                link(dve.tensor_tensor(gate[:, :, :], picked[0][:, :, :], picked[1][:, :, :], ALU.add))

            @block.scalar
            def _(act):
                act.wait_ge(ready, 1)
                act.activation(var[:, :], var[:, :], ACT.Sqrt).then_inc(rooted, 1)
                act.wait_ge(shifted2, 1)
                act.activation(best[1][:, :], best[1][:, :], ACT.Exp).then_inc(exped2, 1)


_INS = ["x", "src", "dst", "edge_weight", "L0_gnn_hyperedge_attr", "L0_gnn_W", "L0_gnn_att", "L0_ffn_Wr", "L0_ffn_br",
        "L0_ffn_W1", "L0_ffn_b1", "L0_ffn_g1", "L0_ffn_be1", "L0_ffn_m1", "L0_ffn_v1", "L0_ffn_W2", "L0_ffn_b2",
        "L0_ffn_g2", "L0_ffn_be2", "L0_ffn_m2", "L0_ffn_v2", "L0_ffn_Wo", "L0_ffn_bo", "L1_gnn_weight", "L1_gnn_bias",
        "L1_ffn_W_gat", "L1_ffn_att_src", "L1_ffn_att_dst", "L1_ffn_b_gat", "L1_ffn_ln_gamma", "L1_ffn_ln_beta",
        "L1_ffn_W1", "L1_ffn_b1", "L1_ffn_W2", "L1_ffn_b2", "L1_ffn_edge_index"]


def kernel(**inputs):
    import concourse.bacc as bacc
    import numpy as np
    from concourse.bass_utils import run_bass_kernel_spmd

    nc = bacc.Bacc("TRN2", target_bir_lowering=False, num_devices=1)
    arrays, args = {}, []
    for name in _INS:
        a = np.ascontiguousarray(inputs[name])
        arrays[f"in_{name}"] = a
        args.append(nc.dram_tensor(f"in_{name}", a.shape, mybir.dt.from_np(a.dtype), kind="ExternalInput").ap())
    args.append(nc.dram_tensor("out_0", (N, F), F32, kind="ExternalOutput").ap())
    graph_network(nc, *args)
    r = run_bass_kernel_spmd(nc, [arrays], core_ids=[0])
    return r.results[0]["out_0"]
```

```python
from contextlib import ExitStack

import concourse.bass as bass
from concourse import mybir

F32 = mybir.dt.float32
I32 = mybir.dt.int32
I16 = mybir.dt.int16
BF16 = mybir.dt.bfloat16
ALU = mybir.AluOpType
ACT = mybir.ActivationFunctionType
AX = mybir.AxisListType
DVE = mybir.EngineType.DVE
PE = mybir.EngineType.PE

P = 128
N, F = 6250, 256
E = 106250
M = 1250
EG = 131072
NJ = -(-N // P)
MJ = -(-M // P)
H0, C0 = 8, 32
EX0, HID0 = 8, 256
H1, C1 = 4, 4
EX1, HID1 = 4, 512
LN_EPS = 1e-5
BN_EPS = 1e-3
HALF = 8
BODY = 2 * HALF
BT = 7
NB = NJ // BT
NOWHERE = float(2 ** 20)


def steps_for(edges, tiles):
    most = (edges + tiles * (P - 1)) // P
    return -(-most // BODY) * BODY


S_SRC = steps_for(E, NJ)
S_DST = steps_for(E, MJ)
S_GAT = steps_for(EG, NJ)


class Link:

    def __init__(self, eng, sem):
        self.eng, self.sem, self.base, self.n = eng, sem, 0, 0

    def __call__(self, ins, meanwhile=None):
        ins.then_inc(self.sem, 1)
        self.n += 1
        if meanwhile is not None:
            meanwhile()
        self.eng.wait_ge(self.sem, self.base + self.n)

    def loop(self, i, per, first=0):
        self.start, self.per = self.base + self.n, per
        self.base, self.n = i * per + (self.start - first * per), 0

    def end(self, count):
        assert self.n == self.per, (self.n, self.per)
        self.base, self.n = self.start + count * self.per, 0


def turns(eng, count, body, link=None, per=0, tail=False):
    body(0, False)
    stop = count - 1 if tail else count
    with eng.Fori(1, stop) as i:
        if link is not None:
            link.loop(i, per, 1)
        body(i, False)
    if link is not None:
        link.end(stop - 1)
    if tail:
        body(count - 1, True)


def is_first(i):
    return isinstance(i, int) and i == 0


def reached(eng, sem, value):
    if not (isinstance(value, int) and value == 0):
        eng.wait_ge(sem, value)


def hold(k, eng, sem, value):
    if not (isinstance(value, int) and value == 0):
        eng.wait_ge(sem, value)
        eng.sem_inc(k.held, 1)


def tile_rows(dram):
    return dram.rearrange("(j p) f -> p j f", p=P)


class Core:

    def __init__(self, nc, stack):
        self.nc, self.stack, self.scopes, self.names = nc, stack, [stack], {}
        self.live = []

    def name(self, name):
        self.names[name] = self.names.get(name, 0) + 1
        return name if self.names[name] == 1 else f"{name}_{self.names[name]}"

    def sb(self, name, shape, dt=F32):
        return self.scopes[-1].enter_context(self.nc.sbuf_tensor(self.name(name), shape, dt))

    def ps(self, name, shape, dt=F32):
        return self.scopes[-1].enter_context(self.nc.psum_tensor(self.name(name), shape, dt))

    def sem(self, name):
        self.live.append(self.nc.alloc_semaphore(name=name))
        return self.live[-1]

    def recycle(self):
        self.nc.clear_and_free_semaphores(self.live)
        self.nc.all_engine_barrier()
        self.live = []

    def sems(self, name, n):
        return [self.sem(f"{name}{k}") for k in range(n)]

    def dram(self, name, shape, dt=F32):
        return self.nc.dram_tensor(name, shape, dt).ap()

    def scope(self):
        return Scope(self)


class Scope:

    def __init__(self, core):
        self.core = core

    def __enter__(self):
        self.own = ExitStack()
        self.own.__enter__()
        self.core.scopes.append(self.own)
        return self

    def __exit__(self, *a):
        self.core.scopes.pop()
        return self.own.__exit__(*a)


def load_nodes(k, x):
    nc = k.nc
    loaded, made, linked = k.sem("x_loaded"), k.sem("consts_made"), k.sem("setup_link")
    iota_i = k.sb("iota_i", [P, P], I32)
    part_i = k.sb("part_i", [P, P], I32)
    part_f = k.sb("part_f", [P, P])
    columns = {heads: k.sb("columns", [96, 3, 32], I32) for heads in (H0, H1)}
    columns_f = k.sb("columns_f", [96, 3, 32])
    pick_f = k.sb("pick_f", [96, 32])
    full = (NJ - 1) * P
    with nc.Block() as block:

        @block.gpsimd
        def _(pool):
            pool.iota(iota_i[:, :], [[1, P]], base=0, channel_multiplier=0).then_inc(made, 1)
            pool.iota(part_i[:, :], [[0, P]], base=0, channel_multiplier=1).then_inc(made, 1)
            for heads, pick_i in columns.items():
                for n in range(3):
                    pool.iota(pick_i[:, n, :], [[3 * heads, 32 // heads], [1, heads]], base=n * heads,
                              channel_multiplier=0).then_inc(made, 1)

        @block.sync
        def _(sp):
            sp.dma_start(k.X[:, 0:NJ - 1, :], tile_rows(x[0:full, :])).then_inc(loaded, 16)
            sp.wait_ge(linked, 1)
            sp.dma_start(k.X[0:N - full, NJ - 1, :], x[full:N, :]).then_inc(loaded, 16)
            sp.wait_ge(loaded, 32)

        @block.vector
        def _(dve):
            link = Link(dve, linked)
            link(dve.memset(k.X[:, NJ - 1, :], 0.0))
            dve.memset(k.ones[:, :], 1.0)
            dve.wait_ge(made, 2 + 3 * len(columns))
            link(dve.tensor_copy(k.iota[:, :], iota_i[:, :]))
            link(dve.tensor_copy(part_f[:, :], part_i[:, :]))
            link(dve.tensor_tensor(k.ident[:, :], k.iota[:, :], part_f[:, :], ALU.is_equal))
            link(dve.tensor_tensor(k.before[:, :], k.iota[:, :], part_f[:, :], ALU.is_gt))
            link(dve.tensor_copy(k.ident16[:, :], k.ident[:, :]))
            link(dve.tensor_scalar(k.far[:, :, :], k.ident[:, :].unsqueeze(1).to_broadcast([P, 4, P]), -2.0 ** 93,
                                   None, ALU.mult))
            for heads, pick_i in columns.items():
                link(dve.tensor_copy(columns_f[:, :, :], pick_i[:, :, :]))
                link(dve.tensor_tensor(columns_f[:, :, :], columns_f[:, :, :],
                                       part_f[0:96, 0:32].unsqueeze(1).to_broadcast([96, 3, 32]), ALU.is_equal))
                link(dve.tensor_reduce(pick_f[:, :], columns_f[:, :, :].rearrange("r n c -> r c n"), AX.X, ALU.add))
                link(dve.tensor_copy(k.pick[heads][:, :], pick_f[:, :]))


class Ranks:

    def __init__(self, k, name, key, rows, cols, tiles, steps, slot, step_tile):
        self.k, self.key, self.rows, self.cols, self.tiles, self.steps = k, key, rows, cols, tiles, steps
        self.slot, self.step_tile = slot, step_tile
        self.loaded, self.counted, self.offset, self.linked, self.made = (
            k.sem(f"{name}_{s}") for s in ("key_loaded", "counted", "offset", "link", "steps_made"))
        self.key_i = k.sb("key_i", [rows, cols], I32)
        self.tile_f = k.sb("tile_f", [rows, cols], BF16)
        self.hit = k.sb("hit", [rows, cols])
        self.hit_i = k.sb("hit_i", [rows, cols], I16)
        self.run = k.sb("run", [rows, cols])
        self.place = k.sb("place", [rows, cols])
        self.count = k.sb("count", [rows, tiles])
        self.tot_f = k.sb("tot_f", [P, tiles])
        self.tot_i = k.sb("tot_i", [P, tiles], I32)
        self.first = k.sb("first", [P, tiles])
        self.base = k.sb("base", [rows, tiles])
        self.step_i = k.sb("step_i", [tiles, steps], I32)
        self.step_f = k.sb("step_f", [tiles, steps])
        self.own_first = k.sb("own_first", [P, 1])
        self.behind = k.sb("behind", [tiles, steps])
        self.ps_behind = k.ps("ps_behind", [P, 3 * 512])
        self.ps_before = k.ps("ps_before", [P, 512])
        self.ps_total = k.ps("ps_total", [P, 512])

    def sync(self, sp):
        sp.dma_start(self.key_i[:, :], self.key.rearrange("(p c) -> p c", p=self.rows)).then_inc(self.loaded, 16)

    def gpsimd(self, pool):
        pool.iota(self.step_i[:, :], [[1, self.steps]], base=0, channel_multiplier=0).then_inc(self.made, 1)

    def vector(self, dve):
        k, rows, tiles = self.k, self.rows, self.tiles
        key_i, tile_f, hit, run, place, slot = self.key_i, self.tile_f, self.hit, self.run, self.place, self.slot
        tot_f, tot_i, first = self.tot_f, self.tot_i, self.first
        link = Link(dve, self.linked)
        dve.wait_ge(self.made, 1)
        link(dve.tensor_copy(self.step_f[:, :], self.step_i[:, :]))
        link(dve.memset(place[:, :], 0.0))
        dve.wait_ge(self.loaded, 16)
        link(dve.tensor_scalar(key_i[:, :], key_i[:, :], 7, None, ALU.arith_shift_right))
        link(dve.tensor_copy(tile_f[:, :], key_i[:, :]))
        some = next(n for n in (7, 5) if tiles % n == 0)
        with dve.Fori(0, tiles // some) as i:
            link.loop(i, some)
            for u in range(some):
                b = i * some + u
                link(dve.tensor_scalar(hit[:, :], tile_f[:, :], k.iota[0:rows, bass.ds(b, 1)], None,
                                       ALU.is_equal, ALU.add, accum_out=self.count[:, bass.ds(b, 1)]))
        link.end(tiles // some)
        dve.sem_inc(self.counted, 1)
        dve.wait_ge(self.offset, 2)
        link(dve.tensor_scalar(tot_f[:, :], self.ps_total[:, 0:tiles], float(P - 1), None, ALU.add))
        link(dve.tensor_copy(tot_i[:, :], tot_f[:, :]))
        link(dve.tensor_scalar(tot_i[:, :], tot_i[:, :], 7, None, ALU.arith_shift_right))
        link(dve.tensor_copy(tot_f[:, :], tot_i[:, :]))
        link(dve.tensor_tensor_scan(first[:, :], tot_f[:, :], tot_f[:, :], 0.0, ALU.add, ALU.max))
        link(dve.tensor_tensor(first[:, :], first[:, :], tot_f[:, :], ALU.subtract))
        link(dve.scalar_tensor_tensor(self.base[:, :], first[0:rows, :], float(P), self.ps_before[0:rows, 0:tiles],
                                      ALU.mult, ALU.add))
        with dve.Fori(0, tiles // some) as i:
            link.loop(i, 3 * some)
            for u in range(some):
                b = i * some + u
                this = k.iota[0:rows, bass.ds(b, 1)]
                dve.tensor_scalar(self.hit_i[:, :], tile_f[:, :], this, None, ALU.is_equal)
                link(dve.tensor_scalar(hit[:, :], tile_f[:, :], this, None, ALU.is_equal))
                link(dve.tensor_tensor_scan(run[:, :], hit[:, :], hit[:, :], self.base[:, bass.ds(b, 1)],
                                            ALU.add, ALU.max))
                dve.sem_inc(k.held, 1)
                link(dve.copy_predicated(place[:, :], self.hit_i[:, :], run[:, :]))
        link.end(tiles // some)
        link(dve.tensor_tensor(first[:, :], first[:, :], k.ident[:, 0:tiles], ALU.mult))
        link(dve.tensor_reduce(self.own_first[:, :], first[:, :], AX.X, ALU.add))
        link(dve.tensor_scalar(self.behind[:, :], self.step_f[:, :], self.own_first[0:tiles, :], None, ALU.is_ge))
        dve.sem_inc(self.counted, 1)
        dve.wait_ge(self.offset, 2 + -(-self.steps // 512))
        link(dve.tensor_scalar(self.step_tile[0:1, :], self.ps_behind[0:1, 0:self.steps], -1.0, None, ALU.add))
        link(dve.tensor_scalar(hit[:, :], place[:, :], 1.0, NOWHERE, ALU.is_lt, ALU.mult))
        link(dve.scalar_tensor_tensor(place[:, :], place[:, :], -1.0, hit[:, :], ALU.add, ALU.add))
        link(dve.tensor_copy(key_i[:, :], place[:, :]))
        link(dve.tensor_scalar(slot[:, :], key_i[:, :], P - 1, None, ALU.bitwise_and))
        link(dve.tensor_scalar(key_i[:, :], key_i[:, :], 7, None, ALU.arith_shift_right))
        link(dve.tensor_copy(hit[:, :], slot[:, :]))
        link(dve.tensor_copy(run[:, :], key_i[:, :]))
        link(dve.scalar_tensor_tensor(place[:, :], hit[:, :], float(self.steps), run[:, :], ALU.mult, ALU.add))
        link(dve.tensor_copy(slot[:, :], place[:, :]))

    def tensor(self, pe):
        k, rows, tiles = self.k, self.rows, self.tiles
        pe.wait_ge(self.counted, 1)
        pe.matmul(self.ps_before[0:rows, 0:tiles], k.before[0:rows, 0:rows], self.count[:, :],
                  start=True, stop=True).then_inc(self.offset, 1)
        pe.matmul(self.ps_total[:, 0:tiles], k.ones[0:rows, 0:P], self.count[:, :],
                  start=True, stop=True).then_inc(self.offset, 1)
        pe.wait_ge(self.counted, 2)
        for lo in range(0, self.steps, 512):
            hi = min(lo + 512, self.steps)
            pe.matmul(self.ps_behind[0:1, lo:hi], k.ones[0:tiles, 0:1], self.behind[:, lo:hi],
                      start=True, stop=True).then_inc(self.offset, 1)


def rank_edges(k, *args):
    with k.scope():
        ranks = Ranks(k, *args)
        with k.nc.Block() as block:

            @block.sync
            def _(sp):
                ranks.sync(sp)

            @block.gpsimd
            def _(pool):
                ranks.gpsimd(pool)

            @block.vector
            def _(dve):
                ranks.vector(dve)

            @block.tensor
            def _(pe):
                ranks.tensor(pe)


def fill_rows(k, name, fills):
    filled, blank = k.sem(f"{name}_filled"), k.sem(f"{name}_blank")
    with k.scope():
        empty = [k.sb("empty", [P, out.shape[0] // P * out.shape[1]]) for out, _ in fills]
        with k.nc.Block() as block:

            @block.vector
            def _(dve):
                for t, (_, value) in zip(empty, fills):
                    dve.memset(t[:, :], value).then_inc(blank, 1)

            @block.sync
            def _(sp):
                for n, (t, (out, _)) in enumerate(zip(empty, fills)):
                    sp.wait_ge(blank, n + 1)
                    sp.dma_start(out.rearrange("(p s) w -> p (s w)", p=P), t[:, :]).then_inc(filled, 16)
                sp.wait_ge(filled, 16 * len(fills))


class Scatter:

    def __init__(self, k, name, rows, chunk, width, out):
        self.k, self.rows, self.chunk, self.width, self.out = k, rows, chunk, width, out
        self.copied = k.sem(f"{name}_copied")
        self.stored = k.sems(f"{name}_stored", 2)
        self.record = [k.sb("record", [rows, chunk, width]) for _ in (0, 1)]
        self.where = [k.sb("where", [rows, chunk], I32) for _ in (0, 1)]

    def turn(self, pool, i, h, fields, slot, before=None):
        chunk = self.chunk
        at = bass.ds(i * (2 * chunk) + h * chunk, chunk)
        n = len(fields) + 1
        hold(self.k, pool, self.stored[h], i * (chunk * 16))
        if before is not None:
            before()
        for lo, w, src in fields:
            pool.tensor_copy(self.record[h][:, :, lo:lo + w], src[:, at, :]).then_inc(self.copied, 1)
        pool.tensor_copy(self.where[h][:, :], slot[:, at]).then_inc(self.copied, 1)
        hold(self.k, pool, self.copied, i * (2 * n) + (h + 1) * n)
        for u in range(chunk):
            pool.indirect_dma_start(
                out=self.out, out_offset=bass.IndirectOffsetOnAxis(ap=self.where[h][:, u:u + 1], axis=0),
                in_=self.record[h][:, u, :], in_offset=None, bounds_check=self.out.shape[0] - 1,
                oob_is_err=False).then_inc(self.stored[h], 16)

    def finish(self, pool, bodies):
        for h in (0, 1):
            pool.wait_ge(self.stored[h], bodies * self.chunk * 16)

    def some(self, pool, fields, slot, first, bodies):
        def body(i, last):
            for h in (0, 1):
                self.turn(pool, i, h, fields, slot)

        if first == 0:
            turns(pool, bodies, body)
        else:
            with pool.Fori(first, first + bodies) as i:
                body(i, False)
        self.finish(pool, first + bodies)


class Gather:

    def __init__(self, k, name, steps, table, index, width):
        self.k, self.steps, self.table, self.index = k, steps, table, index
        self.copied = k.sem(f"{name}_index_copied")
        self.landed, self.used = k.sems(f"{name}_landed", 2), k.sems(f"{name}_used", 2)
        self.index_now = [k.sb("index_now", [P, HALF], I32) for _ in (0, 1)]
        self.rows = [k.sb("rows", [P, HALF, width]) for _ in (0, 1)]

    def gpsimd(self, pool):
        def body(i, last):
            for h in (0, 1):
                if not is_first(i):
                    pool.wait_ge(self.used[h], i * 2 - 1)
                hold(self.k, pool, self.copied, i * 2 + (h + 1))
                for u in range(HALF):
                    if u == HALF // 2:
                        hold(self.k, pool, self.used[h], i * 2)
                    pool.indirect_dma_start(
                        out=self.rows[h][:, u, :], out_offset=None, in_=self.table,
                        in_offset=bass.IndirectOffsetOnAxis(ap=self.index_now[h][:, u:u + 1], axis=0)
                    ).then_inc(self.landed[h], 16)

        turns(pool, self.steps // BODY, body)

    def copy_index(self, act, i, h):
        reached(act, self.landed[h], i * (HALF * 16))
        act.copy(self.index_now[h][:, :], self.index[:, bass.ds(i * BODY + h * HALF, HALF)]).then_inc(self.copied, 1)


def load_tiles(nc, step_tile, first, count, tiles, engine):
    return nc.values_load_multi_w_load_instructions(
        step_tile[0:1, bass.ds(first, count)], engines=[engine], min_val=0, max_val=tiles - 1,
        skip_runtime_bounds_check_because="a step's tile is a count of tiles, less one, of which the first counts")[1]


def split3(dve, link, src, parts, rest):
    link(dve.tensor_copy(parts[:, :, 0, :], src))
    link(dve.tensor_tensor(rest, src, parts[:, :, 0, :], ALU.subtract))
    link(dve.tensor_copy(parts[:, :, 1, :], rest))
    link(dve.tensor_tensor(parts[:, :, 2, :], rest, parts[:, :, 1, :], ALU.subtract))


def segment_max(k, name, steps, heads, width, table, index, local, step_tile, value, top):
    nc = k.nc
    groups = HALF * heads // 32
    each = HALF // groups
    banks = heads * P // 512
    TOPS = 4
    names = ("kept", "flipped", "turned", "other", "product", "reduced", "maxed", "link")
    kept, flipped, turned, other_ok, product, reduced, maxed, linked = (k.sem(f"{name}_{s}") for s in names)
    with k.scope():
        g = Gather(k, name, steps, table, index, width + 3 * heads // 2)
        parts = [k.sb("parts", [P, HALF, 3 * heads], BF16) for _ in (0, 1)]
        parts_t = [k.sb("parts_t", [96, groups, P], BF16) for _ in (0, 1)]
        other = [k.sb("other", [P, HALF, P], BF16) for _ in (0, 1)]
        most = k.sb("most", [P, BODY, heads])
        tops = k.sb("tops", [P, TOPS, top.shape[1], heads])
        ps = [k.ps("ps_max", [P, heads, P]) for _ in range(3)]
        ps_t = [k.ps("ps_parts", [96, groups, P], BF16) for _ in (0, 1)]

        with nc.Block() as block:

            @block.gpsimd
            def _(pool):
                g.gpsimd(pool)

            @block.scalar
            def _(act):
                def body(i, last):
                    if is_first(i):
                        for h in (0, 1):
                            g.copy_index(act, i, h)
                    for h in (0, 1):
                        at = i * BODY + h * HALF
                        act.wait_ge(g.landed[h], i * (HALF * 16) + HALF * 16)
                        act.copy(parts[h][:, :, :].bitcast(F32), g.rows[h][:, :, width:]).then_inc(kept, 1)
                        act.copy(value[:, bass.ds(at, HALF), :], g.rows[h][:, :, 0:width]).then_inc(kept, 1)
                        act.wait_ge(kept, (i * 2 + (h + 1)) * 2)
                        act.sem_inc(g.used[h], 2)
                        if not last:
                            g.copy_index(act, i + 1, h)
                        act.wait_ge(flipped, (i * 2 + (h + 1)) * groups)
                        act.copy(parts_t[h][:, :, :], ps_t[h][:, :, :]).then_inc(turned, 1)
                        if not is_first(i):
                            act.wait_ge(product, (i * BODY + ((h - 1) * HALF)) * banks)
                        for u in range(HALF):
                            act.activation(other[h][:, u, :], k.iota[:, :], ACT.Abs, scale=-1.0,
                                           bias=local[:, bass.ds(at + u, 1)]).then_inc(other_ok, 1)

                turns(act, steps // BODY, body, tail=True)

            @block.vector
            def _(dve):
                link = Link(dve, linked)
                link(dve.memset(tops[:, :, :, :], -3e38))

                def body(i, last):
                    tiles = []

                    def join(n):
                        into = tops[:, n % TOPS, bass.ds(tiles[n], 1), :].rearrange("p a h -> p (a h)")
                        dve.wait_ge(reduced, i * BODY + (n + 1))
                        if not (is_first(i) and n < TOPS):
                            dve.wait_ge(maxed, i * BODY + (n - TOPS + 1))
                        dve.tensor_tensor(into, into, most[:, n, :], ALU.max).then_inc(maxed, 1)

                    for n in range(BODY):
                        dve.wait_ge(product, (i * BODY + (n + 1)) * banks)
                        dve.tensor_reduce(most[:, n, :], ps[n % 3][:, :, :], AX.X, ALU.max).then_inc(reduced, 1)
                        if n % 4 == 0:
                            tiles += load_tiles(nc, step_tile, i * BODY + n, 4, top.shape[1], DVE)
                        if n > 0:
                            join(n - 1)
                    join(BODY - 1)

                turns(dve, steps // BODY, body)
                dve.wait_ge(maxed, steps)
                for n in range(TOPS):
                    link(dve.tensor_tensor(top[:, :, :], top[:, :, :], tops[:, n, :, :], ALU.max))

            @block.tensor
            def _(pe):
                def transpose(i, h):
                    pe.wait_ge(kept, (i * 2 + h) * 2 + 1)
                    if not (is_first(i) and h == 0):
                        pe.wait_ge(turned, i * 2 + h)
                    for c in range(groups):
                        pe.transpose(ps_t[h][:, c, :],
                                     parts[h][:, c * each:(c + 1) * each, :].rearrange("p u c -> p (u c)"),
                                     k.ident16[:, :]).then_inc(flipped, 1)

                def body(i, last):
                    if is_first(i):
                        transpose(i, 0)
                    for h in (0, 1):
                        if h == 0:
                            transpose(i, 1)
                        elif not last:
                            transpose(i + 1, 0)
                        pe.wait_ge(turned, i * 2 + (h + 1))
                        for u in range(HALF):
                            n = h * HALF + u
                            if n > 2:
                                pe.wait_ge(reduced, i * BODY + (n - 2))
                            elif not is_first(i):
                                pe.wait_ge(reduced, i * BODY - (BODY - 1 - n) % 3)
                            pe.wait_ge(other_ok, i * BODY + (n + 1))
                            for c in range(banks):
                                at = slice(c * 4, c * 4 + 4)
                                pe.matmul(ps[n % 3][:, at, :], other[h][:, u, :], k.far[:, :, :], start=True, stop=False)
                                for d in range(4):
                                    head = c * 4 + d
                                    row = (u % each) * heads + head
                                    ins = pe.matmul(ps[n % 3][:, head, :],
                                                    k.pick[heads][:, row:row + 1].to_broadcast([96, P]),
                                                    parts_t[h][:, u // each, :], start=False, stop=d == 3)
                                ins.then_inc(product, 1)

                turns(pe, steps // BODY, body, tail=True)


def segment_softmax(k, name, steps, heads, local, step_tile, node, value, wide, message, total, scatter=None):
    nc = k.nc
    tiles_n = total.shape[1]
    TOTALS = 4
    names = ("hot", "flipped", "turned", "spread", "shifted", "exped", "message", "summed", "added", "link", "ready",
             "kept")
    hot_ok, flipped, turned, spread, shifted, exped, message_ok, summed, added, linked, ready, kept = (
        k.sem(f"{name}_{s}") for s in names)
    with k.scope():
        hot = [k.sb(f"hot{h}", [P, HALF, P]) for h in (0, 1)]
        hot_t = [k.sb(f"hot_t{h}", [P, HALF, P], BF16) for h in (0, 1)]
        logit = k.sb("logit", [P, HALF, heads])
        msg = [k.sb(f"msg{h}", [P, HALF, wide]) for h in (0, 1)]
        node_parts = k.sb("node_parts", [P, tiles_n, 3, 2 * heads], BF16)
        node_rest = k.sb("node_rest", [P, tiles_n, 2 * heads])
        totals = k.sb("totals", [P, TOTALS, tiles_n, wide])
        ps_t = [k.ps(f"ps_t{h}", [P, HALF, P]) for h in (0, 1)]
        ps_n = [k.ps(f"ps_n{h}", [P, 512]) for h in (0, 1)]
        ps_s = [k.ps(f"ps_s{h}", [P, 512]) for h in (0, 1)]
        spread_parts = [x[:, 0:HALF * 6 * heads].rearrange("p (u n c) -> p u n c", u=HALF, n=3) for x in ps_n]
        at_node = k.sb("at_node", [P, HALF, 2 * heads])
        sums = [x[:, 0:HALF * wide].rearrange("p (u c) -> p u c", u=HALF) for x in ps_s]

        def half_tiles(i, h, engine):
            return load_tiles(nc, step_tile, i * BODY + h * HALF, HALF, tiles_n, engine)

        with nc.Block() as block:

            @block.vector
            def _(dve):
                link = Link(dve, linked)
                for h in (0, 1):
                    dve.memset(msg[h][:, :, :], 1.0)
                link(dve.memset(totals[:, :, :, :], 0.0))
                split3(dve, link, node[:, :, :], node_parts, node_rest[:, :, :])
                dve.sem_inc(ready, 1)

                def make_hot(i, h, q):
                    own = slice(q * HALF // 2, (q + 1) * HALF // 2)
                    at = bass.ds(i * BODY + (h * HALF + q * HALF // 2), HALF // 2)
                    dve.tensor_tensor(hot[h][:, own, :], k.iota[:, :].unsqueeze(1).to_broadcast([P, HALF // 2, P]),
                                      local[:, at].unsqueeze(2).to_broadcast([P, HALF // 2, P]),
                                      ALU.is_equal).then_inc(hot_ok, 1)

                def add(i, h, tiles, some):
                    for u in some:
                        n = h * HALF + u
                        into = totals[:, u % TOTALS, bass.ds(tiles[u], 1), :].rearrange("p a w -> p (a w)")
                        if not (is_first(i) and n < TOTALS):
                            dve.wait_ge(added, i * BODY + (n - TOTALS + 1))
                        dve.tensor_tensor(into, into, sums[h][:, u, :], ALU.add).then_inc(added, 1)

                def body(i, last):
                    if is_first(i):
                        for q in (0, 1):
                            make_hot(i, 0, q)
                    for h in (0, 1):
                        tiles = []

                        def load():
                            if not (is_first(i) and h == 0):
                                tiles.extend(load_tiles(nc, step_tile, i * BODY + (h * HALF - HALF + len(tiles)),
                                                        HALF // 2, tiles_n, DVE))

                        for q in (0, 1):
                            if not (is_first(i) and h == 0):
                                dve.wait_ge(summed, i * BODY + (h * HALF - (1 - q) * HALF // 2))
                            if h == 0:
                                make_hot(i, 1, q)
                            elif not last:
                                make_hot(i + 1, 0, q)
                        load()
                        at = bass.ds(i * BODY + h * HALF, HALF)
                        dve.wait_ge(spread, (i * 2 + (h + 1)) * HALF)
                        link(dve.tensor_reduce(at_node[:, :, :], spread_parts[h].rearrange("p u n c -> p u c n"),
                                               AX.X, ALU.add))
                        link(dve.tensor_tensor(logit[:, :, :], value[:, at, 0:heads],
                                               at_node[:, :, heads:2 * heads], ALU.add))
                        link(dve.scalar_tensor_tensor(logit[:, :, :], logit[:, :, :], 0.2, logit[:, :, :],
                                                      ALU.mult, ALU.max))
                        link(dve.tensor_tensor(logit[:, :, :], logit[:, :, :], at_node[:, :, 0:heads],
                                               ALU.subtract))
                        dve.tensor_scalar(logit[:, :, :], logit[:, :, :], 0.0, None, ALU.min).then_inc(shifted, 1)
                        for some in (range(0, 2), range(2, HALF)):
                            if h == 1:
                                add(i, 0, tiles, some)
                            elif not is_first(i):
                                add(i - 1, 1, tiles, some)
                            if some.start == 0:
                                dve.wait_ge(exped, i * 2 + (h + 1))
                                if message is not None:
                                    message(dve, msg[h], at).then_inc(message_ok, 1)
                                load()
                    if last:
                        tiles = half_tiles(i, 1, DVE)
                        dve.wait_ge(summed, i * BODY + BODY)
                        add(i, 1, tiles, range(HALF))

                turns(dve, steps // BODY, body, link, 2 * 4, tail=True)
                dve.wait_ge(added, steps)
                for n in range(TOTALS):
                    link(dve.tensor_tensor(total[:, :, :], total[:, :, :], totals[:, n, :, :], ALU.add))

            @block.tensor
            def _(pe):
                def transpose(i, h):
                    for u in range(HALF):
                        pe.wait_ge(hot_ok, (i * 2 + h) * 2 + (1 + u // (HALF // 2)))
                        pe.transpose(ps_t[h][:, u, :], hot[h][:, u, :], k.ident[:, :]).then_inc(flipped, 1)

                def body(i, last):
                    if is_first(i):
                        pe.wait_ge(ready, 1)
                        transpose(i, 0)
                    for h in (0, 1):
                        tiles = half_tiles(i, h, PE)
                        pe.wait_ge(turned, i * 2 + (h + 1))
                        for u in range(HALF):
                            pe.matmul(spread_parts[h][:, u, :, :], hot_t[h][:, u, :],
                                      node_parts[:, bass.ds(tiles[u], 1), :, :].rearrange("p a n c -> p (a n c)"),
                                      start=True, stop=True).then_inc(spread, 1)
                        if h == 0:
                            transpose(i, 1)
                        elif not last:
                            transpose(i + 1, 0)
                        pe.wait_ge(exped if message is None else message_ok, i * 2 + (h + 1))
                        for u in range(HALF):
                            pe.matmul(sums[h][:, u, :], hot[h][:, u, :], msg[h][:, u, :],
                                      start=True, stop=True).then_inc(summed, 1)

                turns(pe, steps // BODY, body, tail=True)

            @block.scalar
            def _(act):
                act.wait_ge(ready, 1)

                def turn_hot(i, h):
                    act.wait_ge(flipped, (i * 2 + (h + 1)) * HALF)
                    act.copy(hot_t[h][:, :, :], ps_t[h][:, :, :]).then_inc(turned, 1)

                def body(i, last):
                    if is_first(i):
                        turn_hot(i, 0)
                    for h in (0, 1):
                        act.wait_ge(shifted, i * 2 + (h + 1))
                        act.activation(msg[h][:, :, 0:heads], logit[:, :, :], ACT.Exp).then_inc(exped, 1)
                        if scatter is not None:
                            act.wait_ge(exped, i * 2 + (h + 1))
                            act.copy(value[:, bass.ds(i * BODY + h * HALF, HALF), 0:heads],
                                     msg[h][:, :, 0:heads]).then_inc(kept, 1)
                        if h == 0:
                            turn_hot(i, 1)
                        elif not last:
                            turn_hot(i + 1, 0)

                turns(act, steps // BODY, body, tail=True)

            if scatter is not None:

                @block.gpsimd
                def _(pool):
                    scatter(pool, kept)


def segment_sum(k, name, steps, table, index, local, step_tile, total, width=F, edge_weight=None, probs=None,
                count=None):
    nc = k.nc
    linked, hot_ok, message_ok, summed, added = (
        k.sem(f"{name}_{s}") for s in ("link", "hot", "message", "summed", "added"))
    with k.scope():
        g = Gather(k, name, steps, table, index, F)
        hot = [k.sb(f"hot{h}", [P, HALF, P]) for h in (0, 1)]
        msg = g.rows if probs is None else [k.sb(f"msg{h}", [P, HALF, width]) for h in (0, 1)]
        ps = [k.ps("ps_sum", [P, 512]) for _ in range(HALF)]
        msgs = 2 if count is not None else 1
        with nc.Block() as block:

            @block.gpsimd
            def _(pool):
                g.gpsimd(pool)

            @block.vector
            def _(dve):
                link = Link(dve, linked)

                def make(i, h, due=None):
                    at = bass.ds(i * BODY + h * HALF, HALF)
                    tiles = []

                    def load(count):
                        if due is not None:
                            tiles.extend(load_tiles(nc, step_tile, due + len(tiles), count, total.shape[1], DVE))
                    same = dve.tensor_tensor(
                        hot[h][:, :, :], k.iota[:, :].unsqueeze(1).to_broadcast([P, HALF, P]),
                        local[:, at].unsqueeze(2).to_broadcast([P, HALF, P]), ALU.is_equal)
                    if edge_weight is None:
                        same.then_inc(hot_ok, 1)
                    else:
                        link(same, meanwhile=lambda: load(HALF // 2))
                        dve.tensor_tensor(hot[h][:, :, :], hot[h][:, :, :],
                                          edge_weight[:, at].unsqueeze(2).to_broadcast([P, HALF, P]),
                                          ALU.mult).then_inc(hot_ok, 1)
                    if probs is not None:
                        dve.wait_ge(g.landed[h], i * (HALF * 16) + HALF * 16)
                        dve.tensor_tensor(
                            msg[h][:, :, 0:F].rearrange("p u (a c) -> p u a c", a=H0),
                            g.rows[h][:, :, :].rearrange("p u (a c) -> p u a c", a=H0),
                            probs[:, at, :].unsqueeze(3).to_broadcast([P, HALF, H0, C0]),
                            ALU.mult).then_inc(message_ok, 1)
                        if count is not None:
                            dve.tensor_copy(msg[h][:, :, F:F + 1], count[:, at].unsqueeze(2)).then_inc(message_ok, 1)
                    load(HALF - len(tiles))
                    return tiles

                def add(i, h, tiles):
                    for u in range(HALF):
                        dve.wait_ge(summed, i * BODY + (h * HALF + u + 1))
                        for c, (lo, hi) in enumerate(((0, F // 2), (F // 2, width))):
                            n = (h * HALF + u) * 2 + c
                            if not (is_first(i) and n < 2):
                                dve.wait_ge(added, i * (2 * BODY) + (n - 1))
                            into = total[:, bass.ds(tiles[u], 1), lo:hi].rearrange("p a w -> p (a w)")
                            dve.tensor_tensor(into, into, ps[u][:, lo:hi], ALU.add).then_inc(added, 1)

                def body(i, last):
                    if is_first(i):
                        make(i, 0)
                    else:
                        add(i - 1, 1, make(i, 0, i * BODY - HALF))
                    add(i, 0, make(i, 1, i * BODY))
                    if last:
                        add(i, 1, load_tiles(nc, step_tile, i * BODY + HALF, HALF, total.shape[1], DVE))

                turns(dve, steps // BODY, body, link, 0 if edge_weight is None else 2, tail=True)

            @block.tensor
            def _(pe):
                def body(i, last):
                    for h in (0, 1):
                        pe.wait_ge(hot_ok, i * 2 + (h + 1))
                        if probs is None:
                            pe.wait_ge(g.landed[h], i * (HALF * 16) + HALF * 16)
                        else:
                            pe.wait_ge(message_ok, (i * 2 + (h + 1)) * msgs)
                        for u in range(HALF):
                            if not (is_first(i) and h == 0):
                                pe.wait_ge(added, i * (2 * BODY) + 2 * (h * HALF + u + 1 - HALF))
                            pe.matmul(ps[u][:, 0:width], hot[h][:, u, :], msg[h][:, u, 0:width],
                                      start=True, stop=True).then_inc(summed, 1)

                turns(pe, steps // BODY, body)

            @block.scalar
            def _(act):
                def body(i, last):
                    for h in (0, 1):
                        if is_first(i):
                            g.copy_index(act, i, h)
                    for h in (0, 1):
                        if not last:
                            g.copy_index(act, i + 1, h)
                        if probs is None:
                            for q in (0, 1):
                                act.wait_ge(summed, i * BODY + (h * HALF + (q + 1) * HALF // 2))
                                act.sem_inc(g.used[h], 1)
                        else:
                            act.wait_ge(message_ok, (i * 2 + (h + 1)) * msgs)
                            act.sem_inc(g.used[h], 2)

                turns(act, steps // BODY, body, tail=True)


def norm_scales(k, name, scale, shift):
    nc = k.nc
    stats_ok, rooted, linked = (k.sem(f"{name}_{s}") for s in ("variance", "root", "link"))
    with k.scope():
        stats = k.sb("stats", [P, NJ, 6])
        mean_var = k.sb("mean_var", [P, NJ, 2])
        with nc.Block() as block:

            @block.vector
            def _(dve):
                link = Link(dve, linked)
                for j in range(NJ):
                    ins = dve.bn_stats(stats[:, j, :], k.X[:, j, :])
                link(ins)
                for j in range(NJ):
                    ins = dve.bn_aggr(mean_var[:, j, :], stats[:, j, :])
                link(ins)
                dve.tensor_scalar(scale[:, :], mean_var[:, :, 1], LN_EPS, None, ALU.add).then_inc(stats_ok, 1)
                dve.wait_ge(rooted, 1)
                link(dve.reciprocal(scale[:, :], scale[:, :]))
                link(dve.scalar_tensor_tensor(shift[:, :], mean_var[:, :, 0], -1.0, scale[:, :], ALU.mult, ALU.mult))

            @block.scalar
            def _(act):
                act.wait_ge(stats_ok, 1)
                act.activation(scale[:, :], scale[:, :], ACT.Sqrt).then_inc(rooted, 1)


class Normed:

    def __init__(self, k, name, src, bt, scale, shift, ps):
        self.k, self.src, self.bt, self.scale, self.shift, self.ps = k, src, bt, scale, shift, ps
        self.flat = k.sb("flat", [P, bt, F])
        self.xt = k.sb("xt", [P, 2, bt * P])
        self.normed, self.flipped, self.copied = (k.sem(f"{name}_{s}") for s in ("normed", "flipped", "xt_copied"))

    def vector(self, dve, b):
        for u in range(self.bt):
            at = bass.ds(b * self.bt + u, 1)
            dve.tensor_scalar(self.flat[:, u, :], self.src[:, at, :].rearrange("p a f -> p (a f)"),
                              self.scale[:, at], self.shift[:, at], ALU.mult, ALU.add).then_inc(self.normed, 1)

    def tensor(self, pe, b):
        for u in range(self.bt):
            pe.wait_ge(self.normed, b * self.bt + (u + 1))
            for c in (0, 1):
                at = (u % 2) * F + c * P
                pe.transpose(self.ps[u // 2][:, at:at + P], self.flat[:, u, c * P:(c + 1) * P],
                             self.k.ident[:, :]).then_inc(self.flipped, 1)
        pe.wait_ge(self.copied, b * self.bt + self.bt)

    def scalar(self, act, b, free=None):
        for u in range(self.bt):
            act.wait_ge(self.flipped, b * (2 * self.bt) + 2 * min(u | 1, self.bt - 1) + 2)
            if u == 0 and free is not None:
                free()
            act.copy(self.xt[:, :, u * P:(u + 1) * P],
                     self.ps[u // 2][:, (u % 2) * F:(u % 2) * F + F].rearrange("p (c n) -> p c n", c=2)
                     ).then_inc(self.copied, 1)


def project(k, name, src, blocks, bt, scale, shift, weight, cols, table=None, keep=None, att=None, side=None,
            beside=None):
    nc = k.nc
    loaded, product, out_ok, saved, linked = (
        k.sem(f"{name}_{s}") for s in ("w_loaded", "product", "out", "saved", "link"))
    with k.scope():
        w = k.sb("w", [P, 2, cols])
        rows = k.sb("rows", [P, bt, cols])
        scaled = k.sb("scaled", [P, F])
        ps_x = [k.ps(f"ps_x{u}", [P, 512]) for u in range(4)]
        ps_w = [k.ps(f"ps_w{u}", [P, 512]) for u in range(4)]
        norm = Normed(k, name, src, bt, scale, shift, ps_x)
        with nc.Block() as block:

            @block.sync
            def _(sp):
                sp.dma_start(w[:, :, :], weight.rearrange("(a p) c -> p a c", p=P)).then_inc(loaded, 16)
                if table is not None:
                    out = table.rearrange("(b j p) f -> b p j f", p=P, j=bt)
                    with sp.Fori(0, blocks) as b:
                        hold(k, sp, out_ok, b * bt + bt)
                        sp.dma_start(out[bass.ds(b, 1), :, :, :].rearrange("a p j f -> p (a j) f"),
                                     rows[:, :, :]).then_inc(saved, 16)
                    sp.wait_ge(saved, blocks * 16)

            @block.vector
            def _(dve):
                link = Link(dve, linked)

                def body(b, last):
                    reached(dve, norm.flipped, b * (2 * bt))
                    norm.vector(dve, b)
                    if att is not None:
                        for u in range(bt):
                            dve.wait_ge(out_ok, b * bt + (u + 1))
                            link(dve.tensor_tensor(scaled[:, :], rows[:, u, :],
                                                   att[:, :, :].rearrange("p h c -> p (h c)"), ALU.mult))
                            link(dve.tensor_reduce(side[:, bass.ds(b * bt + u, 1), :].rearrange("p a h -> p (a h)"),
                                                   scaled[:, :].rearrange("p (h c) -> p h c", h=H0), AX.X, ALU.add))

                turns(dve, blocks, body, link, 0 if att is None else 2 * bt)

            @block.tensor
            def _(pe):
                pe.wait_ge(loaded, 16)

                def body(b, last):
                    norm.tensor(pe, b)
                    reached(pe, out_ok, b * bt)
                    for u in range(bt):
                        for c in (0, 1):
                            at = (u % 2) * F
                            ins = pe.matmul(ps_w[u // 2][:, at:at + cols], norm.xt[:, c, u * P:(u + 1) * P],
                                            w[:, c, :], start=c == 0, stop=c == 1)
                        ins.then_inc(product, 1)

                turns(pe, blocks, body)

            @block.scalar
            def _(act):

                def body(b, last):
                    norm.scalar(act, b)
                    if table is not None:
                        reached(act, saved, b * 16)
                    if att is not None:
                        reached(act, linked, b * (2 * bt))
                    for u in range(bt):
                        act.wait_ge(product, b * bt + (min(u | 1, bt - 1) + 1))
                        into = rows[:, u, :] if keep is None else (
                            keep[:, bass.ds(b * bt + u, 1), :].rearrange("p a c -> p (a c)"))
                        act.copy(into, ps_w[u // 2][:, (u % 2) * F:(u % 2) * F + cols]).then_inc(out_ok, 1)

                turns(act, blocks, body)

            if beside is not None:

                @block.gpsimd
                def _(pool):
                    beside(pool)


def mixture(k, name, scale, shift, gate, experts, hidden, func, layers, w_out, b_out, beside=None):
    nc = k.nc
    ct = hidden // P
    groups = 2 * ct * len(layers)
    wide = BT * P // 2
    names = ("w_loaded", "group", "evacuated", "y", "y_taken", "link")
    loaded, group_ok, evacuated, y_ok, y_taken, linked = (k.sem(f"{name}_{s}") for s in names)
    with k.scope():
        ws = [k.sb(f"w{n}", [P, experts, 2, hidden]) for n in range(len(layers))]
        wo = k.sb("wo", [P, experts, ct, F])
        bo = k.sb("bo", [P, experts, F])
        hid = [k.sb(f"hid{n}", [P, ct, BT * P]) for n in range(len(layers))]
        part = k.sb("part", [P, F])
        ps_h = [k.ps(f"ps_h{u}", [P, 512]) for u in range(4)]
        ps_y = [k.ps(f"ps_y{u}", [P, 512]) for u in range(4)]
        norm = Normed(k, name, k.X, BT, scale, shift, ps_h)
        with nc.Block() as block:

            @block.sync
            def _(sp):
                for w, (dram, _, _) in zip(ws, layers):
                    for e in range(experts):
                        sp.dma_start(w[:, e, :, :], dram[e, :, :].rearrange("(a p) h -> p a h", p=P)).then_inc(loaded, 16)
                for e in range(experts):
                    sp.dma_start(wo[:, e, :, :], w_out[e, :, :].rearrange("(a p) f -> p a f", p=P)).then_inc(loaded, 16)
                sp.dma_start(bo[:, :, :], b_out.partition_broadcast(P)).then_inc(loaded, 16)

            loads = (len(layers) * experts + experts + 1) * 16

            @block.tensor
            def _(pe):
                pe.wait_ge(loaded, loads)
                with pe.Fori(0, NB) as b:
                    pe.wait_ge(evacuated, b * (experts * groups) + 4)
                    norm.tensor(pe, b)
                    for e in range(experts):
                        for n, w in enumerate(ws):
                            src, kt = (norm.xt, 2) if n == 0 else (hid[n - 1], ct)
                            for half in (0, 1):
                                for c in range(ct):
                                    g = e * groups + n * 2 * ct + half * ct + c
                                    if n and c == 0:
                                        pe.wait_ge(evacuated, b * (experts * groups) + (g - 2 * ct + ct + 4))
                                    pe.wait_ge(evacuated, b * (experts * groups) + (g + 1))
                                    for a in range(kt):
                                        ins = pe.matmul(ps_h[g % 4][:, 0:wide], w[:, e, a, c * P:(c + 1) * P],
                                                        src[:, a, half * wide:(half + 1) * wide],
                                                        start=a == 0, stop=a == kt - 1)
                                    ins.then_inc(group_ok, 1)
                        pe.wait_ge(evacuated, b * (experts * groups) + ((e + 1) * groups + 4))
                        for u in range(BT):
                            m = e * BT + u
                            pe.wait_ge(y_taken, b * (experts * BT) + (m + 1))
                            for a in range(ct):
                                ins = pe.matmul(ps_y[m % 4][:, 0:F], hid[-1][:, a, u * P:(u + 1) * P],
                                                wo[:, e, a, :], start=a == 0, stop=a == ct - 1)
                            ins.then_inc(y_ok, 1)

            @block.scalar
            def _(act):
                act.sem_inc(evacuated, 4)
                with act.Fori(0, NB) as b:
                    norm.scalar(act, b)
                    for e in range(experts):
                        for n, (_, s, t) in enumerate(layers):
                            for half in (0, 1):
                                for c in range(ct):
                                    g = e * groups + n * 2 * ct + half * ct + c
                                    act.wait_ge(group_ok, b * (experts * groups) + (g + 1))
                                    act.activation(
                                        hid[n][:, c, half * wide:(half + 1) * wide], ps_h[g % 4][:, 0:wide], func,
                                        bias=t[:, e, c:c + 1],
                                        scale=1.0 if s is None else s[:, e, c:c + 1]).then_inc(evacuated, 1)

            @block.vector
            def _(dve):
                link = Link(dve, linked)
                dve.sem_inc(y_taken, 4)
                dve.wait_ge(loaded, loads)

                def body(b, last):
                    if is_first(b):
                        norm.vector(dve, b)
                    for e in range(experts):
                        if e == experts - 1 and not last:
                            dve.wait_ge(norm.flipped, b * (2 * BT) + 2 * BT)
                            norm.vector(dve, b + 1)
                        for u in range(BT):
                            m = e * BT + u
                            at = bass.ds(b * BT + u, 1)
                            x = k.X[:, at, :].rearrange("p a f -> p (a f)")
                            dve.wait_ge(y_ok, b * (experts * BT) + (m + 1))
                            dve.tensor_tensor(part[:, :], ps_y[m % 4][:, 0:F], bo[:, e, :], ALU.add).then_inc(y_taken, 1)
                            dve.wait_ge(y_taken, b * (experts * BT) + (m + 1 + 4))
                            link(dve.scalar_tensor_tensor(
                                x, part[:, :], gate[:, at, e:e + 1].rearrange("p a e -> p (a e)"), x,
                                ALU.mult, ALU.add))

                turns(dve, NB, body, link, experts * BT, tail=True)

            if beside is not None:

                @block.gpsimd
                def _(pool):
                    beside(pool)


def vector_only(k, name, body):
    linked = k.sem(f"{name}_link")
    with k.nc.Block() as block:

        @block.vector
        def _(dve):
            body(dve, Link(dve, linked))


def load_all(k, name, pairs):
    done = k.sem(f"{name}_done")
    with k.nc.Block() as block:

        @block.sync
        def _(sp):
            for to, src in pairs:
                sp.dma_start(to, src).then_inc(done, 16)
            sp.wait_ge(done, 16 * len(pairs))


def flat2(ap):
    return ap.rearrange("p a b -> p (a b)")


def graph_network(nc, x, src, dst, edge_weight, attr, w_gnn, att, wr, br, w1, b1, g1, be1, m1, v1, w2, b2, g2, be2,
                  m2, v2, wo, bo, weight, bias, w_gat, att_src, att_dst, b_gat, ln_gamma, ln_beta, u1, c1, u2, c2,
                  edge_index, out):
    stack = ExitStack()
    with stack:
        k = Core(nc, stack)
        k.held = stack.enter_context(nc.semaphore("held"))
        k.X = k.sb("X", [P, NJ, F])
        k.iota = k.sb("iota", [P, P])
        k.ident = k.sb("ident", [P, P])
        k.ones = k.sb("ones", [P, P])
        k.before = k.sb("before", [P, P])
        k.ident16 = k.sb("ident16", [P, P], BF16)
        k.far = k.sb("far", [P, 4, P], BF16)
        k.pick = {heads: k.sb(f"pick{heads}", [96, 32], BF16) for heads in (H0, H1)}
        scale = k.sb("scale", [P, NJ])
        shift = k.sb("shift", [P, NJ])
        tile_src = k.sb("tile_src", [1, S_SRC], I32)
        tile_dst = k.sb("tile_dst", [1, S_DST], I32)
        tile_gat = k.sb("tile_gat", [1, S_GAT], I32)

        REC_SRC, REC_DST, REC_GAT = 5, H0 + 3, 2
        by_src = k.dram("by_src", (P * S_SRC, REC_SRC))
        by_dst = k.dram("by_dst", (P * S_DST, REC_DST))
        by_gat = k.dram("by_gat", (P * S_GAT, REC_GAT))
        hyper_a = k.dram("hyper_a", (MJ * P, H0 + 3 * H0 // 2))
        node_h = k.dram("node_h", (NJ * P, F))
        hyper_out = k.dram("hyper_out", (MJ * P, F))
        gat_table = k.dram("gat_table", (NJ * P, H1 * C1 + H1 + 3 * H1 // 2))

        with k.scope():
            load_nodes(k, x)

        GC = EG // P
        plan_slot = k.dram("plan_slot", (P, GC), I32)
        plan_fields = k.dram("plan_fields", (P, GC, REC_GAT))
        node_a = k.sb("node_a", [P, NJ, H0])
        fill_rows(k, "blank", [(by_src, -1.0), (by_gat, -1.0), (by_dst, 0.0)])

        EP, EC = 125, E // 125
        with k.scope():
            slot_src = k.sb("slot_src", [EP, EC], I32)
            slot_dst = k.sb("slot_dst", [EP, EC], I32)
            slot_gat = k.sb("slot_gat", [P, GC], I32)
            rank_edges(k, "rank_src", src, EP, EC, NJ, S_SRC, slot_src, tile_src)
            rank_edges(k, "rank_dst", dst, EP, EC, MJ, S_DST, slot_dst, tile_dst)
            low_bits = k.sb("low_bits", [EP, EC], I32)
            fields = k.sb("fields", [EP, EC, REC_SRC])
            weights = k.sb("weights", [EP, EC])
            src_i = k.sb("src_i", [EP, EC], I32)
            dst_i = k.sb("dst_i", [EP, EC], I32)
            load_all(k, "edge_loads", [(t[:, :], d.rearrange("(p c) -> p c", p=EP))
                                       for t, d in ((src_i, src), (dst_i, dst), (weights, edge_weight))])

            def edge_fields(dve, link):
                link(dve.tensor_scalar(low_bits[:, :], src_i[:, :], P - 1, None, ALU.bitwise_and))
                for n, t in enumerate((low_bits, src_i, dst_i, weights, slot_dst)):
                    ins = dve.tensor_copy(fields[:, :, n], t[:, :])
                link(ins)

            vector_only(k, "edge_fields", edge_fields)
            to_src = Scatter(k, "to_src", EP, 25, REC_SRC, by_src)

            def store_edges(pool, first, bodies):
                to_src.some(pool, [(0, REC_SRC, fields)], slot_src, first, bodies)

            with k.scope():
                ranks = Ranks(k, "rank_gat", edge_index[1, :], P, GC, NJ, S_GAT, slot_gat, tile_gat)
                with nc.Block() as block:

                    @block.sync
                    def _(sp):
                        ranks.sync(sp)

                    @block.gpsimd
                    def _(pool):
                        ranks.gpsimd(pool)
                        store_edges(pool, 0, 9)

                    @block.vector
                    def _(dve):
                        ranks.vector(dve)

                    @block.tensor
                    def _(pe):
                        ranks.tensor(pe)

            norm_scales(k, "norm0", scale, shift)
            with k.scope():
                atts = k.sb("atts", [P, H0, 2 * C0])
                half_att = [k.sb(f"att{n}", [P, H0, C0]) for n in (0, 1)]
                hyper = k.sb("hyper", [P, MJ, F])
                hyper_side = k.sb("hyper_side", [P, MJ, H0])
                plain = k.sb("plain", [P, 2, MJ])
                full = (MJ - 1) * P

                def clear(dve, link):
                    link(dve.memset(hyper[:, :, :], 0.0))
                    link(dve.memset(plain[:, 0, :], 1.0))
                    link(dve.memset(plain[:, 1, :], 0.0))

                vector_only(k, "hyper_clear", clear)
                load_all(k, "hyper_loads", [
                    (atts[:, :, :], att[0, :, :].partition_broadcast(P)),
                    (hyper[:, 0:MJ - 1, :], tile_rows(attr[0:full, :])),
                    (hyper[0:M - full, MJ - 1, :], attr[full:M, :])])

                def split_att(dve, link):
                    for n in (0, 1):
                        link(dve.tensor_copy(half_att[n][:, :, :], atts[:, :, n * C0:(n + 1) * C0]))

                vector_only(k, "split_att", split_att)
                project(k, "node0", k.X, NB, BT, scale, shift, w_gnn, F, table=node_h, att=half_att[0],
                        side=node_a, beside=lambda pool: store_edges(pool, 9, 7))
                hyper_h = k.dram("hyper_h", (MJ * P, F))
                project(k, "hyper0", hyper, 2, MJ // 2, plain[:, 0, :], plain[:, 1, :], w_gnn, F,
                        table=hyper_h, att=half_att[1], side=hyper_side,
                        beside=lambda pool: store_edges(pool, 16, EC // 50 - 16))
                hyper_row = k.sb("hyper_row", [P, MJ, hyper_a.shape[1]])
                hyper_rest = k.sb("hyper_rest", [P, MJ, H0])

                def hyper_rows(dve, link):
                    link(dve.tensor_copy(hyper_row[:, :, 0:H0], hyper_side[:, :, :]))
                    parts = hyper_row[:, :, H0:].bitcast(BF16).rearrange("p j (n h) -> p j n h", n=3)
                    split3(dve, link, hyper_side[:, :, :], parts, hyper_rest[:, :, :])

                vector_only(k, "hyper_rows", hyper_rows)
                load_all(k, "hyper_a", [(tile_rows(hyper_a), hyper_row[:, :, :])])

            g_src = k.sb("g_src", [P, GC], I32)
            g_dst = k.sb("g_dst", [P, GC], I32)
            g_fields = k.sb("g_fields", [P, GC, REC_GAT])
            load_all(k, "gat_loads", [(g_src[:, :], edge_index[0, :].rearrange("(p c) -> p c", p=P)),
                                      (g_dst[:, :], edge_index[1, :].rearrange("(p c) -> p c", p=P))])

            def gat_fields(dve, link):
                link(dve.tensor_scalar(g_dst[:, :], g_dst[:, :], P - 1, None, ALU.bitwise_and))
                dve.tensor_copy(g_fields[:, :, 0], g_dst[:, :])
                link(dve.tensor_copy(g_fields[:, :, 1], g_src[:, :]))

            vector_only(k, "gat_fields", gat_fields)
            load_all(k, "plan_store", [(plan_slot, slot_gat[:, :]), (plan_fields, g_fields[:, :, :])])
        k.recycle()

        with k.scope():
            local = k.sb("local", [P, S_SRC])
            to_dst = k.sb("to_dst", [P, S_SRC], I32)
            ew = k.sb("ew", [P, S_SRC])
            degree_part = k.sb("degree_part", [P, NJ, H0])
            with k.scope():
                prob = k.sb("prob", [P, S_SRC, H0])
                to_hyper = k.sb("to_hyper", [P, S_SRC], I32)
                with k.scope():
                    src_f = k.sb("src_f", [P, S_SRC])
                    hyper_local = k.sb("hyper_local", [P, S_SRC])
                    hyper_slot = k.sb("hyper_slot", [P, S_SRC], I32)
                    present = k.sb("present", [P, S_SRC])
                    with k.scope():
                        rec = k.sb("rec", [P, S_SRC, REC_SRC])
                        low_i = k.sb("low_i", [P, S_SRC], I32)
                        dst_f = k.sb("dst_f", [P, S_SRC])
                        load_all(k, "by_src_load", [(rec[:, :, :], by_src.rearrange("(p s) w -> p s w", p=P))])

                        def unpack(dve, link):
                            link(dve.tensor_copy(local[:, :], rec[:, :, 0]))
                            link(dve.tensor_scalar(src_f[:, :], rec[:, :, 1], 0.0, None, ALU.max))
                            link(dve.tensor_scalar(dst_f[:, :], rec[:, :, 2], 0.0, None, ALU.max))
                            link(dve.tensor_copy(to_dst[:, :], dst_f[:, :]))
                            link(dve.tensor_scalar(low_i[:, :], to_dst[:, :], P - 1, None, ALU.bitwise_and))
                            link(dve.tensor_copy(hyper_local[:, :], low_i[:, :]))
                            link(dve.tensor_scalar(dst_f[:, :], dst_f[:, :], float(M - 1), None, ALU.min))
                            link(dve.tensor_copy(to_hyper[:, :], dst_f[:, :]))
                            link(dve.tensor_copy(ew[:, :], rec[:, :, 3]))
                            link(dve.tensor_scalar(dst_f[:, :], rec[:, :, 4], 0.0, NOWHERE, ALU.is_lt, ALU.mult))
                            link(dve.scalar_tensor_tensor(dst_f[:, :], rec[:, :, 4], 0.0, dst_f[:, :], ALU.max, ALU.add))
                            link(dve.tensor_copy(hyper_slot[:, :], dst_f[:, :]))
                            link(dve.memset(present[:, :], 1.0))

                        vector_only(k, "unpack", unpack)

                    with k.scope():
                        top = k.sb("top", [P, NJ, H0])
                        node = k.sb("node", [P, NJ, 2 * H0])
                        total = k.sb("total", [P, NJ, H0 + 1])
                        inv = k.sb("inv", [P, NJ, H0])
                        vector_only(k, "top0_clear", lambda dve, link: (
                            link(dve.memset(top[:, :, :], -3e38)), link(dve.memset(total[:, :, :], 0.0))))
                        segment_max(k, "max0", S_SRC, H0, H0, hyper_a, to_hyper, local, tile_src, prob, top)

                        def node_side0(dve, link):
                            link(dve.tensor_tensor(top[:, :, :], top[:, :, :], node_a[:, :, :], ALU.add))
                            link(dve.scalar_tensor_tensor(node[:, :, 0:H0], top[:, :, :], 0.2, top[:, :, :],
                                                          ALU.mult, ALU.max))
                            link(dve.tensor_copy(node[:, :, H0:2 * H0], node_a[:, :, :]))

                        vector_only(k, "node_side0", node_side0)
                        with k.scope():
                            to_dst_order = Scatter(k, "to_dst_order", P, HALF, REC_DST, by_dst)

                            def scatter(pool, kept):
                                def body(i, last):
                                    for h in (0, 1):
                                        to_dst_order.turn(
                                            pool, i, h,
                                            [(0, H0, prob), (H0, 1, src_f[:, :].unsqueeze(2)),
                                             (H0 + 1, 1, hyper_local[:, :].unsqueeze(2)),
                                             (H0 + 2, 1, present[:, :].unsqueeze(2))], hyper_slot,
                                            before=lambda: pool.wait_ge(kept, i * 2 + (h + 1)))

                                turns(pool, S_SRC // BODY, body)
                                to_dst_order.finish(pool, S_SRC // BODY)

                            segment_softmax(k, "soft0", S_SRC, H0, local, tile_src, node, prob, H0 + 1, None, total,
                                            scatter)

                        def inverses0(dve, link):
                            link(dve.tensor_scalar(inv[:, :, :], total[:, :, 0:H0], 1e-16, None, ALU.add))
                            link(dve.reciprocal(inv[:, :, :], inv[:, :, :]))
                            link(dve.tensor_scalar(total[:, :, H0], total[:, :, H0], 1.0, None, ALU.max))
                            link(dve.reciprocal(total[:, :, H0], total[:, :, H0]))
                            link(dve.tensor_tensor(degree_part[:, :, :], inv[:, :, :],
                                                   total[:, :, H0:H0 + 1].to_broadcast([P, NJ, H0]), ALU.mult))

                        vector_only(k, "inverses0", inverses0)
                        scale_rows(k, "scale_h", node_h, inv)

                with k.scope():
                    rec_d = k.sb("rec_d", [P, S_DST, REC_DST])
                    from_src = k.sb("from_src", [P, S_DST], I32)
                    local_d = k.sb("local_d", [P, S_DST])
                    sums = k.sb("sums", [P, MJ, F + 1])
                    load_all(k, "by_dst_load", [(rec_d[:, :, :], by_dst.rearrange("(p s) w -> p s w", p=P))])

                    def unpack_d(dve, link):
                        link(dve.tensor_copy(from_src[:, :], rec_d[:, :, H0]))
                        link(dve.tensor_copy(local_d[:, :], rec_d[:, :, H0 + 1]))
                        link(dve.memset(sums[:, :, :], 0.0))

                    vector_only(k, "unpack_d", unpack_d)
                    segment_sum(k, "hyper_sum", S_DST, node_h, from_src, local_d, tile_dst, sums, width=F + 1,
                                probs=rec_d[:, :, 0:H0], count=rec_d[:, :, H0 + 2])

                    def mean_d(dve, link):
                        link(dve.tensor_scalar(sums[:, :, F], sums[:, :, F], 1.0, None, ALU.max))
                        link(dve.reciprocal(sums[:, :, F], sums[:, :, F]))
                        link(dve.tensor_tensor(sums[:, :, 0:F], sums[:, :, 0:F],
                                               sums[:, :, F:F + 1].to_broadcast([P, MJ, F]), ALU.mult))

                    vector_only(k, "mean_d", mean_d)
                    load_all(k, "hyper_out", [(tile_rows(hyper_out), sums[:, :, 0:F])])

                with k.scope():
                    acc = k.sb("acc", [P, NJ, F])
                    vector_only(k, "acc0_clear", lambda dve, link: link(dve.memset(acc[:, :, :], 0.0)))
                    segment_sum(k, "node_sum", S_SRC, hyper_out, to_hyper, local, tile_src, acc, probs=prob[:, :, :])

                    def add0(dve, link):
                        for j in range(NJ):
                            x_heads = acc[:, j, :].rearrange("p (h c) -> p h c", h=H0)
                            ins = dve.tensor_tensor(x_heads, x_heads,
                                                    degree_part[:, j, :].unsqueeze(2).to_broadcast([P, H0, C0]), ALU.mult)
                        link(ins)
                        link(dve.tensor_tensor(flat2(k.X[:, :, :]), flat2(k.X[:, :, :]), flat2(acc[:, :, :]), ALU.add))

                    vector_only(k, "add0", add0)


            k.recycle()
            norm_scales(k, "norm1", scale, shift)
            with k.scope():
                gate = k.sb("gate", [P, NJ, EX0])
                project(k, "logits0", k.X, NB, BT, scale, shift, wr, EX0, keep=gate)
                softmax_gate(k, gate, br)
                bn = [batch_norm(k, f"bn{n}", *a) for n, a in enumerate(((b1, g1, be1, m1, v1), (b2, g2, be2, m2, v2)))]
                slot_gat = k.sb("slot_gat", [P, GC], I32)
                g_fields = k.sb("g_fields", [P, GC, REC_GAT])
                load_all(k, "plan_load", [(slot_gat[:, :], plan_slot), (g_fields[:, :, :], plan_fields)])
                to_gat = Scatter(k, "to_gat", P, 16, REC_GAT, by_gat)
                mixture(k, "ffn0", scale, shift, gate, EX0, HID0, ACT.Relu, [(w1, *bn[0]), (w2, *bn[1])], wo, bo,
                        beside=lambda pool: to_gat.some(pool, [(0, REC_GAT, g_fields)], slot_gat, 0, GC // 32))

            norm_scales(k, "norm2", scale, shift)
            project(k, "node1", k.X, NB, BT, scale, shift, weight, F, table=node_h)
            with k.scope():
                acc = k.sb("acc1", [P, NJ, F])
                bias_b = k.sb("bias_b", [P, F])
                vector_only(k, "acc1_clear", lambda dve, link: link(dve.memset(acc[:, :, :], 0.0)))
                load_all(k, "bias_load", [(bias_b[:, :], bias.partition_broadcast(P))])
                segment_sum(k, "edge_sum", S_SRC, node_h, to_dst, local, tile_src, acc, edge_weight=ew)

                def add1(dve, link):
                    link(dve.tensor_tensor(flat2(k.X[:, :, :]), flat2(k.X[:, :, :]), flat2(acc[:, :, :]), ALU.add))
                    link(dve.tensor_tensor(k.X[:, :, :], k.X[:, :, :],
                                           bias_b[:, :].unsqueeze(1).to_broadcast([P, NJ, F]), ALU.add))

                vector_only(k, "add1", add1)

        k.recycle()
        norm_scales(k, "norm3", scale, shift)
        gate1 = k.sb("gate1", [P, NJ, EX1])
        HC = H1 * C1
        with k.scope():
            g_local = k.sb("g_local", [P, S_GAT])
            g_from = k.sb("g_from", [P, S_GAT], I32)
            with k.scope():
                rec_g = k.sb("rec_g", [P, S_GAT, REC_GAT])
                from_f = k.sb("from_f", [P, S_GAT])
                load_all(k, "by_gat_load", [(rec_g[:, :, :], by_gat.rearrange("(p s) w -> p s w", p=P))])

                def unpack_g(dve, link):
                    link(dve.tensor_copy(g_local[:, :], rec_g[:, :, 0]))
                    link(dve.tensor_scalar(from_f[:, :], rec_g[:, :, 1], 0.0, float(N - 1), ALU.max, ALU.min))
                    link(dve.tensor_copy(g_from[:, :], from_f[:, :]))

                vector_only(k, "unpack_g", unpack_g)
            h_node = k.sb("h_node", [P, NJ, HC])
            project(k, "gat_h", k.X, NB, BT, scale, shift, w_gat, HC, keep=h_node)
            attention_gates(k, h_node, gate1, gat_table, g_local, g_from, tile_gat, att_src, att_dst, b_gat,
                            ln_gamma, ln_beta)

        with k.scope():
            c1_t = k.sb("c1_t", [P, EX1, HID1 // P])
            by_channel(k, "c1_load", [c1], flat2(c1_t[:, :, :]))
            mixture(k, "ffn1", scale, shift, gate1, EX1, HID1, ACT.Gelu, [(u1, None, c1_t)], u2, c2)
        store_nodes(k, out)


def store_nodes(k, out):
    full = (NJ - 1) * P
    load_all(k, "store", [(tile_rows(out[0:full, :]), k.X[:, 0:NJ - 1, :]),
                          (out[full:N, :], k.X[0:N - full, NJ - 1, :])])


def scale_rows(k, name, table, by):
    nc = k.nc
    loaded, scaled, stored = (k.sem(f"{name}_{s}") for s in ("loaded", "scaled", "stored"))
    with k.scope():
        rows = k.sb("rows", [P, BT, F])
        blocks = table.rearrange("(b j p) f -> b p j f", p=P, j=BT)
        with nc.Block() as block:

            @block.sync
            def _(sp):
                with sp.Fori(0, NB) as b:
                    now = blocks[bass.ds(b, 1), :, :, :].rearrange("a p j f -> p (a j) f")
                    sp.dma_start(rows[:, :, :], now).then_inc(loaded, 16)
                    hold(k, sp, scaled, b * BT + BT)
                    sp.dma_start(now, rows[:, :, :]).then_inc(stored, 16)
                    hold(k, sp, stored, b * 16 + 16)

            @block.vector
            def _(dve):
                with dve.Fori(0, NB) as b:
                    dve.wait_ge(loaded, b * 16 + 16)
                    for u in range(BT):
                        heads = rows[:, u, :].rearrange("p (h c) -> p h c", h=H0)
                        weight = by[:, bass.ds(b * BT + u, 1), :].rearrange("p a h -> p (a h)")
                        dve.tensor_tensor(heads, heads, weight.unsqueeze(2).to_broadcast([P, H0, C0]),
                                          ALU.mult).then_inc(scaled, 1)


def softmax_gate(k, gate, br):
    shifted, exped, linked = k.sem("gate_shifted"), k.sem("gate_exp"), k.sem("gate_link")
    with k.scope():
        br_b = k.sb("br_b", [P, EX0])
        most = k.sb("most", [P, NJ])
        load_all(k, "br_load", [(br_b[:, :], br.partition_broadcast(P))])
        with k.nc.Block() as block:

            @block.vector
            def _(dve):
                link = Link(dve, linked)
                link(dve.tensor_tensor(gate[:, :, :], gate[:, :, :], br_b[:, :].unsqueeze(1).to_broadcast([P, NJ, EX0]),
                                       ALU.add))
                link(dve.tensor_reduce(most[:, :], gate[:, :, :], AX.X, ALU.max))
                dve.tensor_tensor(gate[:, :, :], gate[:, :, :], most[:, :].unsqueeze(2).to_broadcast([P, NJ, EX0]),
                                  ALU.subtract).then_inc(shifted, 1)
                dve.wait_ge(exped, 1)
                link(dve.tensor_reduce(most[:, :], gate[:, :, :], AX.X, ALU.add))
                link(dve.reciprocal(most[:, :], most[:, :]))
                link(dve.tensor_tensor(gate[:, :, :], gate[:, :, :], most[:, :].unsqueeze(2).to_broadcast([P, NJ, EX0]),
                                       ALU.mult))

            @block.scalar
            def _(act):
                act.wait_ge(shifted, 1)
                act.activation(gate[:, :, :], gate[:, :, :], ACT.Exp).then_inc(exped, 1)


def by_channel(k, name, arrays, out):
    nc = k.nc
    loaded, flipped, copied = (k.sem(f"{name}_{s}") for s in ("loaded", "flipped", "copied"))
    experts, channels = arrays[0].shape
    each = experts * channels // P
    rows = each * len(arrays)
    with k.scope():
        lines = k.sb("lines", [rows, P])
        ps = k.ps("ps_lines", [P, 512])
        with nc.Block() as block:

            @block.sync
            def _(sp):
                for n, a in enumerate(arrays):
                    sp.dma_start(lines[n * each:(n + 1) * each, :], a.rearrange("e (c p) -> (e c) p", p=P)).then_inc(loaded, 16)

            @block.tensor
            def _(pe):
                pe.wait_ge(loaded, 16 * len(arrays))
                pe.transpose(ps[:, 0:rows], lines[:, :], k.ident[0:rows, 0:rows]).then_inc(flipped, 1)

            @block.scalar
            def _(act):
                act.wait_ge(flipped, 1)
                act.copy(out, ps[:, 0:rows]).then_inc(copied, 1)


def batch_norm(k, name, b, g, be, m, v):
    ct = HID0 // P
    every = k.sb(f"{name}_params", [P, 5, EX0, ct])
    t = {n: every[:, i, :, :] for i, n in enumerate(("b", "g", "be", "m", "v"))}
    ready, rooted, linked = k.sem(f"{name}_ready"), k.sem(f"{name}_root"), k.sem(f"{name}_link")
    by_channel(k, f"{name}_load", [b, g, be, m, v], every[:, :, :, :].rearrange("p n e c -> p (n e c)"))
    with k.nc.Block() as block:

        @block.vector
        def _(dve):
            link = Link(dve, linked)
            dve.tensor_scalar(t["v"][:, :, :], t["v"][:, :, :], BN_EPS, None, ALU.add).then_inc(ready, 1)
            dve.wait_ge(rooted, 1)
            link(dve.reciprocal(t["v"][:, :, :], t["v"][:, :, :]))
            link(dve.tensor_tensor(t["g"][:, :, :], t["g"][:, :, :], t["v"][:, :, :], ALU.mult))
            link(dve.tensor_tensor(t["b"][:, :, :], t["b"][:, :, :], t["m"][:, :, :], ALU.subtract))
            link(dve.tensor_tensor(t["b"][:, :, :], t["b"][:, :, :], t["g"][:, :, :], ALU.mult))
            link(dve.tensor_tensor(t["b"][:, :, :], t["b"][:, :, :], t["be"][:, :, :], ALU.add))

        @block.scalar
        def _(act):
            act.wait_ge(ready, 1)
            act.activation(t["v"][:, :, :], t["v"][:, :, :], ACT.Sqrt).then_inc(rooted, 1)

    return t["g"], t["b"]


def attention_gates(k, h_node, gate, gat_table, g_local, g_from, tile_gat, att_src, att_dst, b_gat, ln_gamma, ln_beta):
    nc = k.nc
    HC = H1 * C1
    ROW = H1 + HC
    with k.scope():
        value = k.sb("value", [P, S_GAT, ROW])
        prod = k.sb("prod", [P, NJ, HC])
        a_dst = k.sb("a_dst", [P, NJ, H1])
        top = k.sb("top", [P, NJ, H1])
        own = k.sb("own", [P, NJ, H1])
        node = k.sb("node", [P, NJ, 2 * H1])
        total = k.sb("total", [P, NJ, ROW])
        small = {n: k.sb(n, [P, HC]) for n in ("s_src", "s_dst", "s_bias", "s_gamma", "s_beta")}
        load_all(k, "gat_params", [
            (small["s_src"][:, :], att_src.rearrange("h c -> (h c)").partition_broadcast(P)),
            (small["s_dst"][:, :], att_dst.rearrange("h c -> (h c)").partition_broadcast(P)),
            (small["s_bias"][:, :], b_gat.partition_broadcast(P)),
            (small["s_gamma"][:, :], ln_gamma.partition_broadcast(P)),
            (small["s_beta"][:, :], ln_beta.partition_broadcast(P))])

        def wide(t):
            return t[:, :].unsqueeze(1).to_broadcast([P, NJ, HC])

        def heads(t):
            return t.rearrange("p j (h c) -> p (j h) c", h=H1)

        def per_head(t):
            return t.rearrange("p j h -> p (j h)").unsqueeze(2).to_broadcast([P, NJ * H1, C1])

        with k.scope():
            row = k.sb("row", [P, NJ, gat_table.shape[1]])

            def sides(dve, link):
                link(dve.tensor_tensor(prod[:, :, :], h_node[:, :, :], wide(small["s_dst"]), ALU.mult))
                link(dve.tensor_reduce(flat2(a_dst[:, :, :]), heads(prod[:, :, :]), AX.X, ALU.add))
                link(dve.tensor_tensor(prod[:, :, :], h_node[:, :, :], wide(small["s_src"]), ALU.mult))
                link(dve.tensor_reduce(flat2(own[:, :, :]), heads(prod[:, :, :]), AX.X, ALU.add))
                link(dve.tensor_copy(row[:, :, 0:H1], own[:, :, :]))
                link(dve.tensor_copy(row[:, :, H1:ROW], h_node[:, :, :]))
                parts = row[:, :, ROW:].bitcast(BF16).rearrange("p j (n h) -> p j n h", n=3)
                split3(dve, link, own[:, :, :], parts, top[:, :, :])

            vector_only(k, "gat_sides", sides)
            load_all(k, "gat_rows", [(tile_rows(gat_table), row[:, :, :])])

        vector_only(k, "gat_first_top", lambda dve, link: link(dve.tensor_copy(top[:, :, :], own[:, :, :])))
        segment_max(k, "max1", S_GAT, H1, ROW, gat_table, g_from, g_local, tile_gat, value, top)

        shifted, exped, linked = k.sem("own_shifted"), k.sem("own_exp"), k.sem("own_link")
        with nc.Block() as block:

            @block.vector
            def _(dve):
                link = Link(dve, linked)
                link(dve.tensor_tensor(top[:, :, :], top[:, :, :], a_dst[:, :, :], ALU.add))
                link(dve.scalar_tensor_tensor(node[:, :, 0:H1], top[:, :, :], 0.2, top[:, :, :], ALU.mult, ALU.max))
                link(dve.tensor_copy(node[:, :, H1:2 * H1], a_dst[:, :, :]))
                link(dve.tensor_tensor(own[:, :, :], own[:, :, :], a_dst[:, :, :], ALU.add))
                link(dve.scalar_tensor_tensor(own[:, :, :], own[:, :, :], 0.2, own[:, :, :], ALU.mult, ALU.max))
                link(dve.tensor_tensor(own[:, :, :], own[:, :, :], node[:, :, 0:H1], ALU.subtract))
                dve.tensor_scalar(own[:, :, :], own[:, :, :], 0.0, None, ALU.min).then_inc(shifted, 1)
                dve.wait_ge(exped, 1)
                link(dve.tensor_copy(total[:, :, 0:H1], own[:, :, :]))
                link(dve.tensor_tensor(heads(prod[:, :, :]), heads(h_node[:, :, :]), per_head(own[:, :, :]), ALU.mult))
                link(dve.tensor_copy(total[:, :, H1:ROW], prod[:, :, :]))

            @block.scalar
            def _(act):
                act.wait_ge(shifted, 1)
                act.activation(own[:, :, :], own[:, :, :], ACT.Exp).then_inc(exped, 1)

        def message(dve, msg, at):
            return dve.tensor_tensor(
                msg[:, :, H1:ROW].rearrange("p u (h c) -> p u h c", h=H1),
                value[:, at, H1:ROW].rearrange("p u (h c) -> p u h c", h=H1),
                msg[:, :, 0:H1].unsqueeze(3).to_broadcast([P, HALF, H1, C1]), ALU.mult)

        segment_softmax(k, "soft1", S_GAT, H1, g_local, tile_gat, node, value, ROW, message, total)

        mean = k.sb("mean", [P, NJ])
        var = k.sb("var", [P, NJ])
        agg = k.sb("agg", [P, NJ, HC])
        scores = k.sb("scores", [P, NJ, EX1])
        picked = [k.sb(f"picked{n}", [P, NJ, EX1]) for n in (0, 1)]
        best = [k.sb(f"best{n}", [P, NJ]) for n in (0, 1)]
        taken = k.sb("taken", [P, NJ])
        free = k.sb("free", [P, NJ])
        ready, rooted, shifted2, exped2, linked2 = (k.sem(f"gates_{s}") for s in
                                                    ("var", "root", "shifted", "exp", "link"))
        with nc.Block() as block:

            @block.vector
            def _(dve):
                link = Link(dve, linked2)

                def each(t):
                    return t[:, :].unsqueeze(2).to_broadcast([P, NJ, HC])

                link(dve.tensor_scalar(own[:, :, :], total[:, :, 0:H1], 1e-16, None, ALU.add))
                link(dve.reciprocal(own[:, :, :], own[:, :, :]))
                link(dve.tensor_copy(agg[:, :, :], total[:, :, H1:ROW]))
                link(dve.tensor_tensor(heads(agg[:, :, :]), heads(agg[:, :, :]), per_head(own[:, :, :]), ALU.mult))
                link(dve.tensor_tensor(agg[:, :, :], agg[:, :, :], wide(small["s_bias"]), ALU.add))
                link(dve.tensor_reduce(mean[:, :], agg[:, :, :], AX.X, ALU.add))
                link(dve.tensor_scalar(mean[:, :], mean[:, :], 1.0 / HC, None, ALU.mult))
                link(dve.tensor_tensor(agg[:, :, :], agg[:, :, :], each(mean), ALU.subtract))
                link(dve.tensor_tensor(prod[:, :, :], agg[:, :, :], agg[:, :, :], ALU.mult))
                link(dve.tensor_reduce(var[:, :], prod[:, :, :], AX.X, ALU.add))
                dve.tensor_scalar(var[:, :], var[:, :], 1.0 / HC, LN_EPS, ALU.mult, ALU.add).then_inc(ready, 1)
                dve.wait_ge(rooted, 1)
                link(dve.reciprocal(var[:, :], var[:, :]))
                link(dve.tensor_tensor(agg[:, :, :], agg[:, :, :], each(var), ALU.mult))
                link(dve.tensor_tensor(agg[:, :, :], agg[:, :, :], wide(small["s_gamma"]), ALU.mult))
                link(dve.tensor_tensor(agg[:, :, :], agg[:, :, :], wide(small["s_beta"]), ALU.add))
                link(dve.tensor_reduce(scores[:, :, :], agg[:, :, :].rearrange("p j (h c) -> p j c h", h=H1),
                                       AX.X, ALU.add))
                link(dve.tensor_scalar(scores[:, :, :], scores[:, :, :], 1.0 / H1, None, ALU.mult))
                for n in (0, 1):
                    link(dve.tensor_reduce(best[n][:, :], scores[:, :, :], AX.X, ALU.max))
                    link(dve.memset(taken[:, :], 0.0))
                    for e in range(EX1):
                        link(dve.tensor_tensor(picked[n][:, :, e], scores[:, :, e], best[n][:, :], ALU.is_equal))
                        link(dve.tensor_scalar(free[:, :], taken[:, :], -1.0, 1.0, ALU.mult, ALU.add))
                        link(dve.tensor_tensor(picked[n][:, :, e], picked[n][:, :, e], free[:, :], ALU.mult))
                        link(dve.tensor_tensor(taken[:, :], taken[:, :], picked[n][:, :, e], ALU.add))
                    if n == 0:
                        link(dve.scalar_tensor_tensor(scores[:, :, :], picked[0][:, :, :], -3e38, scores[:, :, :],
                                                      ALU.mult, ALU.add))
                dve.tensor_tensor(best[1][:, :], best[1][:, :], best[0][:, :], ALU.subtract).then_inc(shifted2, 1)
                dve.wait_ge(exped2, 1)
                link(dve.tensor_scalar(best[0][:, :], best[1][:, :], 1.0, None, ALU.add))
                link(dve.reciprocal(best[0][:, :], best[0][:, :]))
                link(dve.tensor_tensor(best[1][:, :], best[1][:, :], best[0][:, :], ALU.mult))
                for n in (0, 1):
                    link(dve.tensor_tensor(picked[n][:, :, :], picked[n][:, :, :],
                                           best[n][:, :].unsqueeze(2).to_broadcast([P, NJ, EX1]), ALU.mult))
                link(dve.tensor_tensor(gate[:, :, :], picked[0][:, :, :], picked[1][:, :, :], ALU.add))

            @block.scalar
            def _(act):
                act.wait_ge(ready, 1)
                act.activation(var[:, :], var[:, :], ACT.Sqrt).then_inc(rooted, 1)
                act.wait_ge(shifted2, 1)
                act.activation(best[1][:, :], best[1][:, :], ACT.Exp).then_inc(exped2, 1)


_INS = ["x", "src", "dst", "edge_weight", "L0_gnn_hyperedge_attr", "L0_gnn_W", "L0_gnn_att", "L0_ffn_Wr", "L0_ffn_br",
        "L0_ffn_W1", "L0_ffn_b1", "L0_ffn_g1", "L0_ffn_be1", "L0_ffn_m1", "L0_ffn_v1", "L0_ffn_W2", "L0_ffn_b2",
        "L0_ffn_g2", "L0_ffn_be2", "L0_ffn_m2", "L0_ffn_v2", "L0_ffn_Wo", "L0_ffn_bo", "L1_gnn_weight", "L1_gnn_bias",
        "L1_ffn_W_gat", "L1_ffn_att_src", "L1_ffn_att_dst", "L1_ffn_b_gat", "L1_ffn_ln_gamma", "L1_ffn_ln_beta",
        "L1_ffn_W1", "L1_ffn_b1", "L1_ffn_W2", "L1_ffn_b2", "L1_ffn_edge_index"]


def kernel(**inputs):
    import concourse.bacc as bacc
    import numpy as np
    from concourse.bass_utils import run_bass_kernel_spmd

    nc = bacc.Bacc("TRN2", target_bir_lowering=False, num_devices=1)
    arrays, args = {}, []
    for name in _INS:
        a = np.ascontiguousarray(inputs[name])
        arrays[f"in_{name}"] = a
        args.append(nc.dram_tensor(f"in_{name}", a.shape, mybir.dt.from_np(a.dtype), kind="ExternalInput").ap())
    args.append(nc.dram_tensor("out_0", (N, F), F32, kind="ExternalOutput").ap())
    graph_network(nc, *args)
    r = run_bass_kernel_spmd(nc, [arrays], core_ids=[0])
    return r.results[0]["out_0"]
```
